# Optimizing a Trainium2 kernel written in Bass

```python
import numpy as np
import jax
import jax.numpy as jnp

def _softmax(x, axis=-1):
    return jax.nn.softmax(x, axis=axis)

def _gelu(x):
    return jax.nn.gelu(x, approximate=True)

def _silu(x):
    return jax.nn.silu(x)

def _sigmoid(x):
    return jax.nn.sigmoid(x)

def _layernorm(x, axis=-1, eps=1e-05):
    m = jnp.mean(x, axis=axis, keepdims=True)
    v = jnp.var(x, axis=axis, keepdims=True)
    return (x - m) / jnp.sqrt(v + eps)

def _scatter_add(tgt, idx, src, axis=0):
    return tgt.at[idx].add(src)

def _segment_sum(src, seg, n):
    return jax.ops.segment_sum(src, seg, n)
kernel_name = 'mk_gnn_resnorm_d4_gnn_r8_015627'

def setup_inputs(seed: int=0):
    np.random.seed(seed)
    _w = jnp.asarray

    def _rec_inputs():
        import jax
        import jax.numpy as jnp
        _gk = jax.random.key(seed)
        x = -0.0003713 + 1 * jax.random.normal(jax.random.fold_in(_gk, 1), (6250, 256), jnp.float32)
        src = jax.random.randint(jax.random.fold_in(_gk, 2), (100000,), 0, 6250, jnp.int32)
        dst = jax.random.randint(jax.random.fold_in(_gk, 3), (100000,), 0, 6250, jnp.int32)
        _o = jnp.argsort(dst, stable=True)
        src = src[_o]
        dst = dst[_o]
        edge_attr_256 = 9.41057e-06 + 1 * jax.random.normal(jax.random.fold_in(_gk, 12), (100000, 256), jnp.float32)
        edge_attr_64 = 1.36993e-05 + 0.999972 * jax.random.normal(jax.random.fold_in(_gk, 13), (100000, 64), jnp.float32)
        edge_weight = jax.random.uniform(jax.random.fold_in(_gk, 15), (100000,), jnp.float32, 0.0, 1)
        return (x, src, dst, edge_attr_256, edge_attr_64, edge_weight)
    x, src, dst, edge_attr_256, edge_attr_64, edge_weight = _rec_inputs()

    def _L0_gnn_setup():
        import jax, jax.numpy as jnp
        import numpy as np
        N = 6250
        E = 100000
        F_IN = 256
        HEADS = 4
        C = 64
        NEG_SLOPE = 0.2

        def _gat_forward(x, edge_index, W, att_src, att_dst, bias, prelu_a):
            n = x.shape[0]
            loops = jnp.arange(n, dtype=edge_index.dtype)
            src = jnp.concatenate([edge_index[0], loops])
            dst = jnp.concatenate([edge_index[1], loops])
            h = (x @ W).reshape(n, HEADS, C)
            a_src = jnp.einsum('nhc,hc->nh', h, att_src)
            a_dst = jnp.einsum('nhc,hc->nh', h, att_dst)
            e = a_src[src] + a_dst[dst]
            e = jnp.where(e >= 0, e, NEG_SLOPE * e)
            m = jax.ops.segment_max(e, dst, num_segments=n)
            alpha = jnp.exp(e - m[dst])
            denom = jax.ops.segment_sum(alpha, dst, num_segments=n)
            alpha = alpha / (denom[dst] + 1e-16)
            msg = alpha[:, :, None] * h[src]
            out = jax.ops.segment_sum(msg, dst, num_segments=n)
            out = out.reshape(n, HEADS * C) + bias
            return jnp.where(out >= 0, out, prelu_a * out)
        key = jax.random.key(seed)
        ks = jax.random.split(key, 7)
        x = jax.random.normal(ks[0], (N, F_IN), dtype=jnp.float32)
        edge_index = jax.random.randint(ks[1], (2, E), 0, N, dtype=jnp.int64)
        W = jax.random.normal(ks[2], (F_IN, HEADS * C), dtype=jnp.float32) / np.sqrt(F_IN)
        att_src = jax.random.normal(ks[3], (HEADS, C), dtype=jnp.float32) / np.sqrt(C)
        att_dst = jax.random.normal(ks[4], (HEADS, C), dtype=jnp.float32) / np.sqrt(C)
        bias = jnp.zeros((HEADS * C,), dtype=jnp.float32)
        prelu_a = jnp.full((1,), 0.25, dtype=jnp.float32)
        return {'x': x, 'edge_index': edge_index, 'W': W, 'att_src': att_src, 'att_dst': att_dst, 'bias': bias, 'prelu_a': prelu_a}
    _L0_gnn_all = _L0_gnn_setup()
    _L0_gnn_in = {k: v for k, v in _L0_gnn_all.items() if k in ('W', 'att_src', 'att_dst', 'bias', 'prelu_a')}
    del _L0_gnn_all

    def _L1_gnn_setup():
        import jax, jax.numpy as jnp
        import numpy as np
        HIDDEN = 256

        def _layernorm(h, gamma, beta, eps=1e-05):
            mu = jnp.mean(h, axis=-1, keepdims=True)
            var = jnp.mean(jnp.square(h - mu), axis=-1, keepdims=True)
            return (h - mu) * jax.lax.rsqrt(var + eps) * gamma + beta
        key = jax.random.key(seed)
        ks = jax.random.split(key, 8)
        N, E, C = (6250, 100000, HIDDEN)
        x = jax.random.normal(ks[0], (N, C), dtype=jnp.float32)
        edge_index = jax.random.randint(ks[1], (2, E), 0, N, dtype=jnp.int64)
        edge_attr = jax.random.normal(ks[2], (E, C), dtype=jnp.float32)
        s = 1.0 / np.sqrt(C)
        W1 = jax.random.uniform(ks[3], (C, C), jnp.float32, -s, s)
        b1 = jax.random.uniform(ks[4], (C,), jnp.float32, -s, s)
        W2 = jax.random.uniform(ks[5], (C, C), jnp.float32, -s, s)
        b2 = jax.random.uniform(ks[6], (C,), jnp.float32, -s, s)
        gamma = jnp.ones((C,), jnp.float32)
        beta = jnp.zeros((C,), jnp.float32)
        return {'x': x, 'edge_index': edge_index, 'edge_attr': edge_attr, 'W1': W1, 'b1': b1, 'W2': W2, 'b2': b2, 'gamma': gamma, 'beta': beta}
    _L1_gnn_all = _L1_gnn_setup()
    _L1_gnn_in = {k: v for k, v in _L1_gnn_all.items() if k in ('W1', 'b1', 'W2', 'b2', 'gamma', 'beta')}
    del _L1_gnn_all

    def _L2_gnn_setup():
        import jax, jax.numpy as jnp
        import numpy as np
        N_NODES = 12500
        N_EDGES = 400000
        D_IN = 256
        D_OUT = 256
        key = jax.random.key(seed)
        k1, k2, k3, k4, k5, k6 = jax.random.split(key, 6)
        x = jax.random.normal(k1, (N_NODES, D_IN), dtype=jnp.float32)
        edge_val = jax.random.uniform(k2, (N_EDGES,), dtype=jnp.float32)
        stdv = 1.0 / np.sqrt(D_OUT)
        W = jax.random.uniform(k3, (D_IN, D_OUT), dtype=jnp.float32, minval=-stdv, maxval=stdv)
        b = jax.random.uniform(k4, (D_OUT,), dtype=jnp.float32, minval=-stdv, maxval=stdv)
        edge_row = jax.random.randint(k5, (N_EDGES,), 0, N_NODES, dtype=jnp.int32)
        edge_col = jax.random.randint(k6, (N_EDGES,), 0, N_NODES, dtype=jnp.int32)
        return {'x': x, 'edge_val': edge_val, 'W': W, 'b': b, 'edge_row': edge_row, 'edge_col': edge_col}
    _L2_gnn_all = _L2_gnn_setup()
    _L2_gnn_in = {k: v for k, v in _L2_gnn_all.items() if k in ('W', 'b')}
    del _L2_gnn_all

    def _L3_gnn_setup():
        import jax, jax.numpy as jnp
        import numpy as np
        N = 2500
        E = 40000
        D = 256
        H = 8
        DH = D // H
        ED = 64
        FF = 4 * D
        EPS = 1e-05

        def _layernorm(x, g, b):
            m = jnp.mean(x, axis=-1, keepdims=True)
            v = jnp.var(x, axis=-1, keepdims=True)
            return (x - m) * jax.lax.rsqrt(v + EPS) * g + b

        def _edge_attention(xn, edge_index, ef, ew, Wq, bq, Wk, bk, Wv, bv, We, be, Wo, bo):
            n = xn.shape[0]
            scale = DH ** (-0.5)
            q = (xn @ Wq + bq).reshape(n, H, DH)
            k = (xn @ Wk + bk).reshape(n, H, DH)
            v = (xn @ Wv + bv).reshape(n, H, DH)
            src, dst = (edge_index[0], edge_index[1])
            ep = ef @ We + be
            scores = jnp.einsum('ehd,ehd->eh', q[dst], k[src] + ep[:, None, :]) * scale
            scores = scores * ew[:, None]
            m = jax.ops.segment_max(scores, dst, num_segments=n)
            m = jnp.where(jnp.isfinite(m), m, 0.0)
            ex = jnp.exp(scores - m[dst])
            s = jax.ops.segment_sum(ex, dst, num_segments=n)
            attn = ex / s[dst]
            out = jax.ops.segment_sum(attn[:, :, None] * v[src], dst, num_segments=n)
            out = out.reshape(n, D) @ Wo + bo
            return out
        key = jax.random.key(seed)
        ks = jax.random.split(key, 32)

        def lin_w(k, i, o):
            return (jax.random.normal(k, (i, o), jnp.float32) / np.sqrt(i)).astype(jnp.float32)
        return {'x': jax.random.normal(ks[0], (N, D), jnp.float32), 'edge_features': jax.random.normal(ks[1], (E, ED), jnp.float32), 'edge_weights': jax.random.uniform(ks[2], (E,), jnp.float32), 'edge_index': jax.random.randint(ks[3], (2, E), 0, N, dtype=jnp.int32), 'Wq': lin_w(ks[4], D, D), 'bq': jnp.zeros((D,), jnp.float32), 'Wk': lin_w(ks[5], D, D), 'bk': jnp.zeros((D,), jnp.float32), 'Wv': lin_w(ks[6], D, D), 'bv': jnp.zeros((D,), jnp.float32), 'We': lin_w(ks[7], ED, DH), 'be': jnp.zeros((DH,), jnp.float32), 'Wo': lin_w(ks[8], D, D), 'bo': jnp.zeros((D,), jnp.float32), 'ln1_g': jnp.ones((D,), jnp.float32), 'ln1_b': jnp.zeros((D,), jnp.float32), 'ln2_g': jnp.ones((D,), jnp.float32), 'ln2_b': jnp.zeros((D,), jnp.float32), 'W1': lin_w(ks[9], D, FF), 'b1': jnp.zeros((FF,), jnp.float32), 'W2': lin_w(ks[10], FF, D), 'b2': jnp.zeros((D,), jnp.float32), 'alpha': jnp.ones((1,), jnp.float32), 'beta': jnp.ones((1,), jnp.float32)}
    _L3_gnn_all = _L3_gnn_setup()
    _L3_gnn_in = {k: v for k, v in _L3_gnn_all.items() if k in ('Wq', 'bq', 'Wk', 'bk', 'Wv', 'bv', 'We', 'be', 'Wo', 'bo', 'ln1_g', 'ln1_b', 'ln2_g', 'ln2_b', 'W1', 'b1', 'W2', 'b2', 'alpha', 'beta')}
    del _L3_gnn_all
    return {'x': x, 'src': src, 'dst': dst, 'edge_attr_256': edge_attr_256, 'edge_attr_64': edge_attr_64, 'edge_weight': edge_weight, 'L0_gnn_W': _L0_gnn_in['W'], 'L0_gnn_att_src': _L0_gnn_in['att_src'], 'L0_gnn_att_dst': _L0_gnn_in['att_dst'], 'L0_gnn_bias': _L0_gnn_in['bias'], 'L0_gnn_prelu_a': _L0_gnn_in['prelu_a'], 'L1_gnn_W1': _L1_gnn_in['W1'], 'L1_gnn_b1': _L1_gnn_in['b1'], 'L1_gnn_W2': _L1_gnn_in['W2'], 'L1_gnn_b2': _L1_gnn_in['b2'], 'L1_gnn_gamma': _L1_gnn_in['gamma'], 'L1_gnn_beta': _L1_gnn_in['beta'], 'L2_gnn_W': _L2_gnn_in['W'], 'L2_gnn_b': _L2_gnn_in['b'], 'L3_gnn_Wq': _L3_gnn_in['Wq'], 'L3_gnn_bq': _L3_gnn_in['bq'], 'L3_gnn_Wk': _L3_gnn_in['Wk'], 'L3_gnn_bk': _L3_gnn_in['bk'], 'L3_gnn_Wv': _L3_gnn_in['Wv'], 'L3_gnn_bv': _L3_gnn_in['bv'], 'L3_gnn_We': _L3_gnn_in['We'], 'L3_gnn_be': _L3_gnn_in['be'], 'L3_gnn_Wo': _L3_gnn_in['Wo'], 'L3_gnn_bo': _L3_gnn_in['bo'], 'L3_gnn_ln1_g': _L3_gnn_in['ln1_g'], 'L3_gnn_ln1_b': _L3_gnn_in['ln1_b'], 'L3_gnn_ln2_g': _L3_gnn_in['ln2_g'], 'L3_gnn_ln2_b': _L3_gnn_in['ln2_b'], 'L3_gnn_W1': _L3_gnn_in['W1'], 'L3_gnn_b1': _L3_gnn_in['b1'], 'L3_gnn_W2': _L3_gnn_in['W2'], 'L3_gnn_b2': _L3_gnn_in['b2'], 'L3_gnn_alpha': _L3_gnn_in['alpha'], 'L3_gnn_beta': _L3_gnn_in['beta']}

def reference(x, src, dst, edge_attr_256, edge_attr_64, edge_weight, L0_gnn_W, L0_gnn_att_src, L0_gnn_att_dst, L0_gnn_bias, L0_gnn_prelu_a, L1_gnn_W1, L1_gnn_b1, L1_gnn_W2, L1_gnn_b2, L1_gnn_gamma, L1_gnn_beta, L2_gnn_W, L2_gnn_b, L3_gnn_Wq, L3_gnn_bq, L3_gnn_Wk, L3_gnn_bk, L3_gnn_Wv, L3_gnn_bv, L3_gnn_We, L3_gnn_be, L3_gnn_Wo, L3_gnn_bo, L3_gnn_ln1_g, L3_gnn_ln1_b, L3_gnn_ln2_g, L3_gnn_ln2_b, L3_gnn_W1, L3_gnn_b1, L3_gnn_W2, L3_gnn_b2, L3_gnn_alpha, L3_gnn_beta):
    import jax
    import jax.numpy as jnp

    def _L0_gnn_ref(x, edge_index, W, att_src, att_dst, bias, prelu_a):
        import jax, jax.numpy as jnp
        import numpy as np
        N = 6250
        E = 100000
        F_IN = 256
        HEADS = 4
        C = 64
        NEG_SLOPE = 0.2

        def _gat_forward(x, edge_index, W, att_src, att_dst, bias, prelu_a):
            n = x.shape[0]
            loops = jnp.arange(n, dtype=edge_index.dtype)
            src = jnp.concatenate([edge_index[0], loops])
            dst = jnp.concatenate([edge_index[1], loops])
            h = (x @ W).reshape(n, HEADS, C)
            a_src = jnp.einsum('nhc,hc->nh', h, att_src)
            a_dst = jnp.einsum('nhc,hc->nh', h, att_dst)
            e = a_src[src] + a_dst[dst]
            e = jnp.where(e >= 0, e, NEG_SLOPE * e)
            m = jax.ops.segment_max(e, dst, num_segments=n)
            alpha = jnp.exp(e - m[dst])
            denom = jax.ops.segment_sum(alpha, dst, num_segments=n)
            alpha = alpha / (denom[dst] + 1e-16)
            msg = alpha[:, :, None] * h[src]
            out = jax.ops.segment_sum(msg, dst, num_segments=n)
            out = out.reshape(n, HEADS * C) + bias
            return jnp.where(out >= 0, out, prelu_a * out)
        return _gat_forward(x, edge_index, W, att_src, att_dst, bias, prelu_a)

    def _L1_gnn_ref(x, edge_index, edge_attr, W1, b1, W2, b2, gamma, beta):
        import jax, jax.numpy as jnp
        import numpy as np
        HIDDEN = 256

        def _layernorm(h, gamma, beta, eps=1e-05):
            mu = jnp.mean(h, axis=-1, keepdims=True)
            var = jnp.mean(jnp.square(h - mu), axis=-1, keepdims=True)
            return (h - mu) * jax.lax.rsqrt(var + eps) * gamma + beta
        N = x.shape[0]
        src, dst = (edge_index[0], edge_index[1])
        msg = jax.nn.relu(x[src] + edge_attr)
        aggr = jax.ops.segment_sum(msg, dst, num_segments=N)
        z = x + aggr
        h = jax.nn.relu(z @ W1 + b1) @ W2 + b2
        return _layernorm(x + jax.nn.relu(h), gamma, beta)

    def _L2_gnn_ref(x, edge_val, W, b, edge_row, edge_col):
        import jax, jax.numpy as jnp
        import numpy as np
        N_NODES = 12500
        N_EDGES = 400000
        D_IN = 256
        D_OUT = 256
        support = jnp.matmul(x, W)
        gathered = support[edge_col] * edge_val[:, None]
        out = jax.ops.segment_sum(gathered, edge_row, num_segments=x.shape[0])
        return out + b

    def _L3_gnn_ref(x, edge_features, edge_weights, edge_index, Wq, bq, Wk, bk, Wv, bv, We, be, Wo, bo, ln1_g, ln1_b, ln2_g, ln2_b, W1, b1, W2, b2, alpha, beta):
        import jax, jax.numpy as jnp
        import numpy as np
        N = 2500
        E = 40000
        D = 256
        H = 8
        DH = D // H
        ED = 64
        FF = 4 * D
        EPS = 1e-05

        def _layernorm(x, g, b):
            m = jnp.mean(x, axis=-1, keepdims=True)
            v = jnp.var(x, axis=-1, keepdims=True)
            return (x - m) * jax.lax.rsqrt(v + EPS) * g + b

        def _edge_attention(xn, edge_index, ef, ew, Wq, bq, Wk, bk, Wv, bv, We, be, Wo, bo):
            n = xn.shape[0]
            scale = DH ** (-0.5)
            q = (xn @ Wq + bq).reshape(n, H, DH)
            k = (xn @ Wk + bk).reshape(n, H, DH)
            v = (xn @ Wv + bv).reshape(n, H, DH)
            src, dst = (edge_index[0], edge_index[1])
            ep = ef @ We + be
            scores = jnp.einsum('ehd,ehd->eh', q[dst], k[src] + ep[:, None, :]) * scale
            scores = scores * ew[:, None]
            m = jax.ops.segment_max(scores, dst, num_segments=n)
            m = jnp.where(jnp.isfinite(m), m, 0.0)
            ex = jnp.exp(scores - m[dst])
            s = jax.ops.segment_sum(ex, dst, num_segments=n)
            attn = ex / s[dst]
            out = jax.ops.segment_sum(attn[:, :, None] * v[src], dst, num_segments=n)
            out = out.reshape(n, D) @ Wo + bo
            return out
        xn = _layernorm(x, ln1_g, ln1_b)
        attn_out = _edge_attention(xn, edge_index, edge_features, edge_weights, Wq, bq, Wk, bk, Wv, bv, We, be, Wo, bo)
        x = x + alpha * attn_out
        xn = _layernorm(x, ln2_g, ln2_b)
        ff = jax.nn.gelu(xn @ W1 + b1, approximate=False) @ W2 + b2
        x = x + beta * ff
        return x
    edge_index = jnp.stack([src, dst])
    x = _layernorm(x + _L0_gnn_ref(x, edge_index, L0_gnn_W, L0_gnn_att_src, L0_gnn_att_dst, L0_gnn_bias, L0_gnn_prelu_a), axis=-1)
    x = _layernorm(x + _L1_gnn_ref(x, edge_index, edge_attr_256, L1_gnn_W1, L1_gnn_b1, L1_gnn_W2, L1_gnn_b2, L1_gnn_gamma, L1_gnn_beta), axis=-1)
    x = _layernorm(x + _L2_gnn_ref(x, edge_weight, L2_gnn_W, L2_gnn_b, src, dst), axis=-1)
    x = _layernorm(x + _L3_gnn_ref(x, edge_attr_64, edge_weight, edge_index, L3_gnn_Wq, L3_gnn_bq, L3_gnn_Wk, L3_gnn_bk, L3_gnn_Wv, L3_gnn_bv, L3_gnn_We, L3_gnn_be, L3_gnn_Wo, L3_gnn_bo, L3_gnn_ln1_g, L3_gnn_ln1_b, L3_gnn_ln2_g, L3_gnn_ln2_b, L3_gnn_W1, L3_gnn_b1, L3_gnn_W2, L3_gnn_b2, L3_gnn_alpha, L3_gnn_beta), axis=-1)
    return x

_drawn_inputs = setup_inputs


def setup_inputs(seed=0):
    import zlib

    import numpy as np

    out = dict(_drawn_inputs(seed))
    spreads = {'L0_gnn_bias': (0.0, 0.1),
     'L1_gnn_gamma': (1.0, 0.2),
     'L1_gnn_beta': (0.0, 0.1),
     'L3_gnn_bq': (0.0, 0.8),
     'L3_gnn_bk': (0.0, 2.0),
     'L3_gnn_bv': (0.0, 0.1),
     'L3_gnn_be': (0.0, 2.0),
     'L3_gnn_bo': (0.0, 0.1),
     'L3_gnn_ln1_g': (1.0, 0.2),
     'L3_gnn_ln1_b': (0.0, 0.1),
     'L3_gnn_ln2_g': (1.0, 0.2),
     'L3_gnn_ln2_b': (0.0, 0.274),
     'L3_gnn_b1': (0.0, 0.1),
     'L3_gnn_b2': (0.0, 0.1)}
    factors = {'L1_gnn_b1': 8.0, 'L1_gnn_b2': 4.04, 'L2_gnn_b': 4.312}
    for name, (base, spread) in spreads.items():
        noise = np.random.default_rng([zlib.crc32(name.encode()), seed]).standard_normal(out[name].shape)
        drawn = base * np.exp(spread * noise) if base else spread * noise
        out[name] = jnp.asarray(drawn.astype(out[name].dtype))
    for name, factor in factors.items():
        out[name] = (out[name] * factor).astype(out[name].dtype)
    return out
```

```python
import numpy as np
from contextlib import ExitStack, contextmanager

import concourse.bass as bass
from concourse import mybir

F32 = mybir.dt.float32
I32 = mybir.dt.int32
ALU = mybir.AluOpType
ACT = mybir.ActivationFunctionType
AX = mybir.AxisListType

P = 128
N = 6250
E = 100000
D = 256
NODE_TILES = -(-N // P)
EDGE_TILES = -(-E // P)
NT = 50
NP = NT * P
SPARE_ROW = NODE_TILES * P
GROUP = 4
RING = 4
STEPS = -(-(EDGE_TILES + NODE_TILES - 1) // (GROUP * RING)) * GROUP * RING
PASSES = STEPS // (GROUP * RING)
SEL_TILES = 7
IDX_ROWS = SEL_TILES * P
EA_TILES = STEPS - (NODE_TILES - 1)
DST_PAD = 64 * P
SLOTS = STEPS * P
HALF = STEPS // 2
BIG = 1.0e30
LN_EPS = 1e-5


@contextmanager
def semaphores(nc):
    held = []

    def sem(name):
        held.append(nc.alloc_semaphore(name=name))
        return held[-1]

    yield sem
    nc.all_engine_barrier()
    nc.clear_and_free_semaphores(held)
    nc.all_engine_barrier()


class Chain:

    def __init__(self, eng, sem, base=0):
        self.eng, self.sem, self.base, self.n = eng, sem, base, 0

    def tick(self, ins):
        ins.then_inc(self.sem, 1)
        self.n += 1
        return ins

    def wait(self):
        self.eng.wait_ge(self.sem, self.base + self.n)

    def then(self, ins):
        self.tick(ins)
        self.wait()


def passes(eng, count):
    yield 0
    with eng.Fori(1, count) as it:
        yield it


def wait_if_any(eng, sem, count):
    if not isinstance(count, int) or count > 0:
        eng.wait_ge(sem, count)


def one_ahead(eng, nc, table, top, ahead, now):
    def one_pass(it, last):
        steps = None
        if table is not None:
            steps = load_indices(nc, eng, table, it * (RING * GROUP), RING * GROUP, top)
        for q in range(RING):
            if q < RING - 1:
                ahead(it, q + 1)
            elif not last:
                ahead(it + 1, 0)
            now(it, q, steps)

    ahead(0, 0)
    one_pass(0, False)
    with eng.Fori(1, PASSES - 1) as it:
        one_pass(it, False)
    one_pass(PASSES - 1, True)


def load_indices(nc, eng, row, at, count, top):
    _, values = nc.values_load_multi_w_load_instructions(
        row[0:1, bass.ds(at, count)], engines=[eng.engine], min_val=0, max_val=top,
        skip_runtime_bounds_check_because="step tables are built in range by prepare()")
    return values


class Shared:
    pass


def allocate(nc, ctx):
    k = Shared()

    def sb(name, shape, dt=F32):
        return ctx.enter_context(nc.sbuf_tensor(name, shape, dt))

    def dram(name, shape):
        return nc.dram_tensor(name, shape, F32, kind="Internal").ap()

    k.lane = sb("lane", [P, 1])
    k.iota = sb("iota", [P, P])
    k.ident = sb("ident", [P, P])
    k.src_idx = sb("src_idx", [P, STEPS], I32)
    k.src = sb("src_f", [P, STEPS])
    k.dloc = sb("dloc", [P, STEPS])
    k.keep = sb("keep", [P, STEPS])
    k.weight = sb("weight", [P, STEPS])
    k.step_j = sb("step_j", [1, STEPS], I32)
    k.step_i = sb("step_i", [1, STEPS], I32)
    k.psum = ctx.enter_context(nc.psum_tensor("psum", [P, 8, 512], F32))

    k.rows_src = dram("rows_src", (STEPS, P))
    k.rows_key = dram("rows_key", (STEPS + 2, P))
    k.rows_dloc = dram("rows_dloc", (STEPS, P))
    k.rows_weight = dram("rows_weight", (STEPS, P))
    k.hrow = dram("hrow", (NP, 260))
    k.spill = dram("spill", (STEPS, P, D))
    k.scores = dram("scores", (STEPS * 8, P))
    k.alphas = dram("alphas", (3, STEPS * 8, P))
    k.x1 = dram("x1", (NP, D))
    k.x2 = dram("x2", (NP, D))
    k.x3 = dram("x3", (NP, D))
    k.kv = dram("kv", (NP, 2 * D))
    k.gcn = [dram(f"gcn{a}", (NP, D)) for a in range(GROUP)]
    return k


def prepare(nc, k, src, dst, weight):
    with ExitStack() as ctx:
        def sb(name, shape, dt=F32):
            return ctx.enter_context(nc.sbuf_tensor(name, shape, dt))

        sem = ctx.enter_context(semaphores(nc))

        raw = sb("p_raw", [P, 2, SEL_TILES, P], I32)
        tiles = sb("p_tiles", [P, SEL_TILES, 3, P])
        step_i32 = sb("p_step_i32", [P, STEPS], I32)
        lane_i32 = sb("p_lane_i32", [P, 1], I32)
        step = sb("p_step", [P, STEPS])
        ones = sb("p_ones", [P, P])
        bound = sb("p_bound", [P, NODE_TILES])
        below = sb("p_below", [P, SEL_TILES, NODE_TILES])
        last = sb("p_last", [NODE_TILES, 1])
        left = sb("p_left", [NODE_TILES, STEPS])
        jrow = sb("p_jrow", [P, STEPS])
        irow = sb("p_irow", [P, STEPS])
        jcol = sb("p_jcol", [P, SEL_TILES])
        lanes = sb("p_lanes", [P, SEL_TILES])
        select = sb("p_select", [P, SEL_TILES, STEPS])
        rowbuf = sb("p_rowbuf", [P, SEL_TILES, 4, P])
        halo = sb("p_halo", [1, 2, P])
        ps = k.psum

        iotas, loaded, dve_done = sem("p_iotas"), sem("p_loaded"), sem("p_dve")
        below_ready, count_ready = sem("p_below_ready"), sem("p_count_ready")
        left_ready, j_ready = sem("p_left_ready"), sem("p_j_ready")
        select_ready, slots_ready = sem("p_select_ready"), sem("p_slots_ready")
        rows_ready, rows_out, stored = sem("p_rows_ready"), sem("p_rows_out"), sem("p_stored")
        block = ctx.enter_context(nc.Block())
        NOPEN = NODE_TILES - 1
        LAST_ROWS = STEPS - (SEL_TILES - 1) * P

        @block.sync
        def _(sp):
            sp.dma_start(raw[:, 0], src.rearrange("(c p) l -> p c l", p=P)).then_inc(loaded, 16)
            sp.dma_start(raw[:, 1], dst.rearrange("(c p) l -> p c l", p=P)).then_inc(loaded, 16)
            sp.dma_start(tiles[:, :, 2, :], weight.rearrange("(c p) l -> p c l", p=P)).then_inc(loaded, 16)
            n = 0
            for c in range(SEL_TILES):
                rows = P if c < SEL_TILES - 1 else LAST_ROWS
                sp.wait_ge(rows_out, c + 1)
                for a, to in enumerate((k.rows_src, k.rows_key, k.rows_weight, k.rows_dloc)):
                    at = c * P + (1 if a == 1 else 0)
                    sp.dma_start(to[at:at + rows, :], rowbuf[0:rows, c, a, :]).then_inc(stored, 16)
                    n += 16
            sp.dma_start(k.rows_key[0:1, :], halo[0:1, 0, :]).then_inc(stored, 16)
            sp.dma_start(k.rows_key[STEPS + 1:STEPS + 2, :], halo[0:1, 1, :]).then_inc(stored, 16)
            sp.wait_ge(stored, n + 32)

        @block.gpsimd
        def _(pool):
            pool.iota(step_i32[:], pattern=[[1, STEPS]], base=0, channel_multiplier=0).then_inc(iotas, 1)
            pool.iota(lane_i32[:], pattern=[[0, 1]], base=0, channel_multiplier=1).then_inc(iotas, 1)

        @block.vector
        def _(dve):
            ch = Chain(dve, dve_done)
            ch.tick(dve.memset(ones[:], 1.0))
            ch.tick(dve.memset(halo[0:1, 0, :], -1.0))
            ch.tick(dve.memset(halo[0:1, 1, :], -2.0))
            ch.tick(dve.memset(k.keep[:, 0:1], 0.0))
            dve.wait_ge(iotas, 2)
            ch.tick(dve.tensor_copy(step[:], step_i32[:]))
            ch.then(dve.tensor_copy(k.lane[:], lane_i32[:]))
            ch.tick(dve.tensor_copy(k.iota[:], step[:, 0:P]))
            ch.tick(dve.tensor_scalar(bound[:], step[:, 0:NODE_TILES], float(P), float(P), ALU.mult, ALU.add))
            for c in range(SEL_TILES):
                ch.tick(dve.tensor_scalar(lanes[:, c:c + 1], k.lane[:], float(P * c), None, ALU.add))
            dve.wait_ge(loaded, 48)
            for a in range(2):
                ch.tick(dve.tensor_copy(tiles[:, :, a, :], raw[:, a]))
            ch.wait()
            ch.tick(dve.tensor_scalar(k.ident[:], k.iota[:], k.lane[:, 0:1], None, ALU.is_equal))
            for c in range(SEL_TILES):
                ins = dve.tensor_scalar(below[:, c, :], bound[:], tiles[:, c, 1, P - 1:P], None, ALU.is_gt)
            ins.then_inc(below_ready, 1)
            dve.wait_ge(count_ready, 1)
            ch.then(dve.tensor_tensor(last[:], ps[0:NODE_TILES, 0, 0:1], k.lane[0:NODE_TILES, :], ALU.add))
            dve.tensor_scalar(left[:], step[0:NODE_TILES, :], last[:, 0:1], None, ALU.is_gt).then_inc(left_ready, 1)
            dve.wait_ge(j_ready, 1)
            ch.tick(dve.tensor_copy(jrow[:, 0:HALF], ps[:, 1, 0:HALF]))
            ch.tick(dve.tensor_copy(jrow[:, HALF:STEPS], ps[:, 2, 0:HALF]))
            ch.tick(dve.tensor_scalar(jcol[:, 0:SEL_TILES - 1], ps[:, 3, 0:SEL_TILES - 1], float(P), None, ALU.mult))
            ch.tick(dve.tensor_scalar(jcol[0:LAST_ROWS, SEL_TILES - 1:SEL_TILES],
                                        ps[0:LAST_ROWS, 3, SEL_TILES - 1:SEL_TILES], float(P), None, ALU.mult))
            ch.wait()
            ch.tick(dve.tensor_copy(k.step_j[:], jrow[0:1, :]))
            ch.tick(dve.tensor_tensor(k.keep[:, 1:STEPS], jrow[:, 1:STEPS], jrow[:, 0:STEPS - 1], ALU.is_equal))
            ch.then(dve.tensor_tensor(irow[:], step[:], jrow[:], ALU.subtract))
            ch.tick(dve.tensor_copy(k.step_i[:], irow[0:1, :]))
            for c in range(SEL_TILES):
                ins = dve.tensor_scalar(select[:, c, :], irow[:], lanes[:, c:c + 1], None, ALU.is_equal)
            ins.then_inc(select_ready, 1)
            dve.wait_ge(slots_ready, 1)
            for h in range(2):
                at = slice(h * HALF, (h + 1) * HALF)
                ch.tick(dve.tensor_copy(k.src_idx[:, at], ps[:, h, 0:HALF]))
                ch.tick(dve.tensor_copy(k.src[:, at], ps[:, h, 0:HALF]))
                ch.tick(dve.scalar_tensor_tensor(out=k.dloc[:, at], in0=jrow[:, at], scalar=-float(P),
                                                   in1=ps[:, 2 + h, 0:HALF], op0=ALU.mult, op1=ALU.add))
                ch.tick(dve.tensor_copy(k.weight[:, at], ps[:, 4 + h, 0:HALF]))
            for c in range(SEL_TILES):
                rows = P if c < SEL_TILES - 1 else LAST_ROWS
                dve.wait_ge(rows_ready, c + 1)
                bank = ps[0:rows, 6 + c % 2, 0:3 * P]
                dve.tensor_copy(rowbuf[0:rows, c, 0:3, :], bank.rearrange("p (a l) -> p a l", a=3))
                dve.tensor_scalar(rowbuf[0:rows, c, 3, :], bank[:, P:2 * P], jcol[0:rows, c:c + 1], None,
                                  ALU.subtract).then_inc(rows_out, 1)

        @block.tensor
        def _(pe):
            pe.wait_ge(below_ready, 1)
            for c in range(SEL_TILES):
                ins = pe.matmul(ps[0:NODE_TILES, 0, 0:1], below[:, c, :], ones[:, 0:1],
                                start=(c == 0), stop=(c == SEL_TILES - 1))
            ins.then_inc(count_ready, 1)
            pe.wait_ge(left_ready, 1)
            for h in range(2):
                pe.matmul(ps[:, 1 + h, 0:HALF], ones[0:NOPEN, :], left[0:NOPEN, h * HALF:(h + 1) * HALF],
                          start=True, stop=True)
            for c in range(SEL_TILES):
                rows = P if c < SEL_TILES - 1 else LAST_ROWS
                ins = pe.matmul(ps[0:rows, 3, c:c + 1], left[0:NOPEN, c * P:c * P + rows], ones[0:NOPEN, 0:1],
                                start=True, stop=True)
            ins.then_inc(j_ready, 1)
            pe.wait_ge(select_ready, 1)
            for a in range(3):
                for h in range(2):
                    for c in range(SEL_TILES):
                        ins = pe.matmul(ps[:, 2 * a + h, 0:HALF], tiles[:, c, a, :],
                                        select[:, c, h * HALF:(h + 1) * HALF],
                                        start=(c == 0), stop=(c == SEL_TILES - 1))
            ins.then_inc(slots_ready, 1)
            for b in range(SEL_TILES):
                rows = P if b < SEL_TILES - 1 else LAST_ROWS
                if b >= 2:
                    pe.wait_ge(rows_out, b - 1)
                for c in range(SEL_TILES):
                    ins = pe.matmul(ps[0:rows, 6 + b % 2, 0:3 * P], select[:, c, b * P:b * P + rows],
                                    tiles[:, c, :, :].rearrange("p a l -> p (a l)"),
                                    start=(c == 0), stop=(c == SEL_TILES - 1))
                ins.then_inc(rows_ready, 1)


PAIRS = 5
BANKS = 2
NODE_PASSES = NT // (2 * PAIRS)


def bank_free(n, b):
    return n + 1 + (b == 0)


def pair(table, m):
    return table.rearrange("(t p) d -> p t d", p=P)[:, bass.ds(2 * m, 2), :]


def transpose_pair(pe, psum_bank, rows, ident, halves=2):
    for t in range(2):
        for h in range(halves):
            at = (t * halves + h) * P
            ins = pe.transpose(psum_bank[:, at:at + P], rows[:, t, h * P:(h + 1) * P], ident)
    return ins


def gat_nodes(nc, k, x, w, att_src, att_dst):
    with ExitStack() as ctx:
        def sb(name, shape, dt=F32):
            return ctx.enter_context(nc.sbuf_tensor(name, shape, dt))

        sem = ctx.enter_context(semaphores(nc))

        WC = D + 8
        wext = sb("n0_wext", [P, 2, WC])
        att = sb("n0_att", [P, 2, D])
        prod = sb("n0_prod", [P, 2, D])
        xin = [sb(f"n0_x{b}", [P, 2, D]) for b in range(PAIRS)]
        xt = [sb(f"n0_xt{b}", [P, 2, 2, P]) for b in range(PAIRS)]
        hout = [sb(f"n0_h{b}", [P, 2, WC]) for b in range(PAIRS)]
        w_landed, w_chain, w_ready = sem("n0_w_landed"), sem("n0_w_chain"), sem("n0_w_ready")
        x_landed = [sem(f"n0_x_landed{b}") for b in range(PAIRS)]
        turned, xt_ready = sem("n0_turned"), sem("n0_xt_ready")
        h_done, h_ready = sem("n0_h_done"), sem("n0_h_ready")
        stored = [sem(f"n0_stored{b}") for b in range(PAIRS)]
        block = ctx.enter_context(nc.Block())
        CREDIT = PAIRS

        @block.sync
        def _(sp):
            sp.dma_start(wext[:, :, 0:D], w.rearrange("(h p) n -> p h n", p=P)).then_inc(w_landed, 16)
            sp.dma_start(att[:, 0, :], att_src.partition_broadcast(P)).then_inc(w_landed, 16)
            sp.dma_start(att[:, 1, :], att_dst.partition_broadcast(P)).then_inc(w_landed, 16)
            for it in passes(sp, NODE_PASSES):
                for b in range(PAIRS):
                    m = it * PAIRS + b
                    sp.wait_ge(turned, m + 1)
                    sp.dma_start(xin[b][:], pair(x, m)).then_inc(x_landed[b], 16)

        @block.gpsimd
        def _(pool):
            for it in passes(pool, NODE_PASSES):
                for b in range(PAIRS):
                    m = it * PAIRS + b
                    pool.wait_ge(h_ready, m + 1 + BANKS)
                    pool.dma_start(pair(k.hrow, m), hout[b][:, :, 0:260]).then_inc(stored[b], 16)
            for b in range(PAIRS):
                pool.wait_ge(stored[b], 16 * NODE_PASSES)

        @block.tensor
        def _(pe):
            pe.sem_inc(turned, CREDIT)
            pe.sem_inc(h_done, CREDIT)
            pe.wait_ge(w_ready, 1)
            for it in passes(pe, NODE_PASSES):
                for b in range(PAIRS):
                    m = it * PAIRS + b
                    pe.wait_ge(x_landed[b], (it + 1) * 16)
                    pe.wait_ge(xt_ready, bank_free(m, b))
                    transpose_pair(pe, k.psum[:, b % BANKS], xin[b], k.ident[:]).then_inc(turned, 1)
                for b in range(PAIRS):
                    m = it * PAIRS + b
                    pe.wait_ge(xt_ready, m + 1 + BANKS)
                    pe.wait_ge(h_ready, bank_free(m, b))
                    for t in range(2):
                        for h in range(2):
                            ins = pe.matmul(k.psum[:, 2 + 2 * (b % BANKS) + t, 0:WC], xt[b][:, t, h, :], wext[:, h, :],
                                            start=(h == 0), stop=(h == 1))
                    ins.then_inc(h_done, 1)

        @block.scalar
        def _(act):
            act.sem_inc(xt_ready, BANKS)
            for it in passes(act, NODE_PASSES):
                for b in range(PAIRS):
                    m = it * PAIRS + b
                    act.wait_ge(turned, m + 1 + CREDIT)
                    act.wait_ge(h_done, m + 1)
                    act.copy(xt[b][:].rearrange("p t h n -> p (t h n)"), k.psum[:, b % BANKS, :]).then_inc(xt_ready, 1)

        @block.vector
        def _(dve):
            dve.sem_inc(h_ready, BANKS)
            ch = Chain(dve, w_chain)
            dve.wait_ge(w_landed, 48)
            for a in range(2):
                for h in range(2):
                    ch.then(dve.tensor_tensor(prod[:, h, :], wext[:, h, 0:D], att[:, a, :], ALU.mult))
                    ch.then(dve.tensor_reduce(wext[:, h, D + 4 * a:D + 4 * a + 4],
                                              prod[:, h, :].rearrange("p (h c) -> p h c", h=4), AX.X, ALU.add))
            dve.sem_inc(w_ready, 1)
            for it in passes(dve, NODE_PASSES):
                for b in range(PAIRS):
                    m = it * PAIRS + b
                    dve.wait_ge(h_done, m + 1 + CREDIT)
                    wait_if_any(dve, stored[b], it * 16)
                    hp = k.psum[:, 2 + 2 * (b % BANKS):4 + 2 * (b % BANKS), :]
                    dve.tensor_copy(k.att[:, bass.ds(2 * m, 2), :], hp[:, :, D:WC])
                    dve.tensor_copy(hout[b][:], hp[:, :, 0:WC]).then_inc(h_ready, 1)


def gat_scores(nc, k):
    H = 4
    with ExitStack() as ctx:
        def sb(name, shape, dt=F32):
            return ctx.enter_context(nc.sbuf_tensor(name, shape, dt))

        sem = ctx.enter_context(semaphores(nc))

        idx = [sb(f"s0_idx{q}", [P, GROUP], I32) for q in range(RING)]
        rows = [sb(f"s0_rows{q}", [P, GROUP, 260]) for q in range(RING)]
        drow = [sb(f"s0_drow{q}", [P, GROUP * P]) for q in range(RING)]
        spread = [sb(f"s0_spread{b}", [P, GROUP * P]) for b in range(2)]
        idx_ready, passed = sem("s0_idx_ready"), sem("s0_passed")
        gathered = [sem(f"s0_gathered{q}") for q in range(RING)]
        drow_landed = [sem(f"s0_drow_landed{q}") for q in range(RING)]
        spilled = [sem(f"s0_spilled{q}") for q in range(RING)]
        spread_ready, looked_up, added = sem("s0_spread_ready"), sem("s0_looked_up"), sem("s0_added")
        block = ctx.enter_context(nc.Block())
        dloc_rows = k.rows_dloc.rearrange("(o s) l -> o (s l)", o=1)
        spill_rows = k.spill.rearrange("s p d -> p s d")

        @block.scalar
        def _(act):
            for it in passes(act, PASSES):
                for q in range(RING):
                    g = it * RING + q
                    wait_if_any(act, gathered[q], it * (16 * GROUP))
                    act.copy(idx[q][:], k.src_idx[:, bass.ds(g * GROUP, GROUP)]).then_inc(idx_ready, 1)
                    act.wait_ge(spread_ready, g + 1)
                    act.dma_start(drow[q][:], dloc_rows[:, bass.ds(g * (GROUP * P), GROUP * P)]
                                  .partition_broadcast(P)).then_inc(drow_landed[q], 16)

        @block.gpsimd
        def _(pool):
            for it in passes(pool, PASSES):
                for q in range(RING):
                    g = it * RING + q
                    pool.wait_ge(idx_ready, g + 1)
                    pool.wait_ge(added, g + 1)
                    wait_if_any(pool, spilled[q], it * 16)
                    pool.sem_inc(passed, 1)
                    for s in range(GROUP):
                        pool.indirect_dma_start(rows[q][:, s, :], None, k.hrow,
                                                bass.IndirectOffsetOnAxis(ap=idx[q][:, s:s + 1], axis=0)
                                                ).then_inc(gathered[q], 16)

        @block.sync
        def _(sp):
            for it in passes(sp, PASSES):
                for q in range(RING):
                    g = it * RING + q
                    sp.wait_ge(gathered[q], (it + 1) * (16 * GROUP))
                    sp.dma_start(spill_rows[:, bass.ds(g * GROUP, GROUP), :], rows[q][:, :, 0:D]
                                 ).then_inc(spilled[q], 16)
            for q in range(RING):
                sp.wait_ge(spilled[q], 16 * PASSES)

        @block.vector
        def _(dve):
            dve.sem_inc(spread_ready, RING)
            dve.sem_inc(added, RING)

            def spread_group(it, q):
                g = it * RING + q
                dve.wait_ge(drow_landed[q], (it + 1) * 16)
                dve.wait_ge(looked_up, g + 1)
                dve.tensor_scalar(spread[q % 2][:], drow[q][:], k.lane[:, 0:1], None, ALU.is_equal
                                  ).then_inc(spread_ready, 1)

            def add_group(it, q, _):
                g = it * RING + q
                dve.wait_ge(looked_up, g + 1 + 2)
                dve.wait_ge(gathered[q], (it + 1) * (16 * GROUP))
                dve.tensor_tensor(k.logits[:, bass.ds(g * GROUP, GROUP), 0:H], rows[q][:, :, D:D + H],
                                  k.psum[:, q % 2, 0:GROUP * H].rearrange("p (s h) -> p s h", s=GROUP), ALU.add
                                  ).then_inc(added, 1)

            one_ahead(dve, nc, None, None, spread_group, add_group)

        @block.tensor
        def _(pe):
            pe.sem_inc(looked_up, 2)
            for it in passes(pe, PASSES):
                j = load_indices(nc, pe, k.step_j, it * (RING * GROUP), RING * GROUP, NODE_TILES - 1)
                for q in range(RING):
                    g = it * RING + q
                    b = q % 2
                    pe.wait_ge(spread_ready, g + 1 + RING)
                    pe.wait_ge(added, g + 1 + RING - 2)
                    for s in range(GROUP):
                        ins = pe.matmul(k.psum[:, b, s * H:(s + 1) * H], spread[b][:, s * P:(s + 1) * P],
                                        k.att[:, bass.ds(j[q * GROUP + s], 1), 4:8]
                                        .rearrange("p o h -> p (o h)"), start=True, stop=True)
                    ins.then_inc(looked_up, 1)


def turn_logits(nc, k, H):
    BLK = P // H
    NBLK = STEPS // BLK
    with ExitStack() as ctx:
        def sb(name, shape, dt=F32):
            return ctx.enter_context(nc.sbuf_tensor(name, shape, dt))

        sem = ctx.enter_context(semaphores(nc))

        turn = [sb(f"m{H}_turn{b}", [P, P]) for b in range(2)]
        turned, turn_ready = sem(f"m{H}_turned"), sem(f"m{H}_turn_ready")
        turn_out = [sem(f"m{H}_turn_out{b}") for b in range(2)]
        with nc.Block() as block:
            @block.tensor
            def _(pe):
                for n in range(NBLK):
                    if n >= 2:
                        pe.wait_ge(turn_ready, n - 1)
                    pe.transpose(k.psum[:, n % 2, 0:P],
                                 k.logits[:, n * BLK:(n + 1) * BLK, 0:H].rearrange("p s h -> p (s h)"),
                                 k.ident[:]).then_inc(turned, 1)

            @block.vector
            def _(dve):
                for n in range(NBLK):
                    dve.wait_ge(turned, n + 1)
                    if n >= 2:
                        dve.wait_ge(turn_out[n % 2], 16 * (n // 2))
                    dve.tensor_copy(turn[n % 2][:], k.psum[:, n % 2, 0:P]).then_inc(turn_ready, 1)

            @block.sync
            def _(sp):
                for n in range(NBLK):
                    sp.wait_ge(turn_ready, n + 1)
                    sp.dma_start(k.scores[n * P:(n + 1) * P, :], turn[n % 2][:]).then_inc(turn_out[n % 2], 16)
                for b in range(2):
                    sp.wait_ge(turn_out[b], 16 * len(range(b, NBLK, 2)))


def softmax(nc, k, H, scale, leaky):
    CHUNKS = P // H
    CH = STEPS // CHUNKS
    L = CH * P
    BLK = P // H
    NBLK = STEPS // BLK
    OUTS = 3 if leaky else 1
    with ExitStack() as ctx:
        def sb(name, shape, dt=F32):
            return ctx.enter_context(nc.sbuf_tensor(name, shape, dt))

        sem = ctx.enter_context(semaphores(nc))

        logit = sb(f"m{H}_logit", [P, L])
        key = sb(f"m{H}_key", [P, L + 2])
        stop = sb(f"m{H}_stop", [P, L])
        best = sb(f"m{H}_best", [P, L])
        ends = sb(f"m{H}_ends", [P, 2])
        row = sb(f"m{H}_row", [1, 2, P])
        cut = sb(f"m{H}_cut", [1, P])
        carried = sb(f"m{H}_carried", [1, P])
        carry = sb(f"m{H}_carry", [P, 1])
        landed, key_landed, w_landed, tmp_landed = (sem(f"m{H}_{n}") for n in ("landed", "key", "w", "tmp"))
        chain, ask, got, tmp_free, w_used = (sem(f"m{H}_{n}") for n in ("chain", "ask", "got", "tmp_free", "w_used"))
        masked, flags_ready, best_ready, expo, exp_done = (
            sem(f"m{H}_{n}") for n in ("masked", "flags_ready", "best_ready", "expo", "exp_done"))
        out_done = sem(f"m{H}_out_done")
        score_rows = k.scores[0:STEPS * H, :].rearrange("(c s h) l -> h c s l", c=CHUNKS, h=H)
        alpha_rows = [k.alphas[a, 0:STEPS * H, :].rearrange("(c s h) l -> h c s l", c=CHUNKS, h=H)
                      for a in range(OUTS)]
        split = lambda t: t.rearrange("p (s l) -> p s l", l=P)
        with nc.Block() as block:
            @block.sync
            def _(sp):
                for h in range(H):
                    at = slice(h * CHUNKS, (h + 1) * CHUNKS)
                    sp.dma_start(split(logit[at, :]), score_rows[h]).then_inc(landed, 16)
                    sp.dma_start(split(best[at, :]),
                                 k.rows_dloc.rearrange("(c s) l -> c s l", c=CHUNKS)).then_inc(tmp_landed, 16)
                    sp.dma_start(key[at, :], bass.AP(k.rows_key.tensor, P - 1, [[L, CHUNKS], [1, L + 2]])
                                 ).then_inc(key_landed, 16)
                if scale is not None:
                    for h in range(H):
                        at = slice(h * CHUNKS, (h + 1) * CHUNKS)
                        sp.dma_start(split(stop[at, :]),
                                     k.rows_weight.rearrange("(c s) l -> c s l", c=CHUNKS)).then_inc(w_landed, 16)
                for a in range(OUTS):
                    sp.wait_ge(exp_done if a == 0 else best_ready if a == 1 else flags_ready, 1)
                    source = (best, logit, stop)[a]
                    for h in range(H):
                        at = slice(h * CHUNKS, (h + 1) * CHUNKS)
                        sp.dma_start(alpha_rows[a][h], split(source[at, :])).then_inc(out_done, 16)
                sp.wait_ge(out_done, 16 * H * OUTS)

            @block.vector
            def _(dve):
                ch = Chain(dve, chain)
                dve.wait_ge(landed, 16 * H)
                if leaky:
                    ch.then(dve.scalar_tensor_tensor(out=logit[:], in0=logit[:], scalar=0.2, in1=logit[:],
                                                     op0=ALU.mult, op1=ALU.max))
                if scale is not None:
                    dve.wait_ge(w_landed, 16 * H)
                    ch.then(dve.scalar_tensor_tensor(out=logit[:], in0=logit[:], scalar=scale, in1=stop[:],
                                                     op0=ALU.mult, op1=ALU.mult))
                dve.wait_ge(tmp_landed, 16 * H)
                ch.then(dve.tensor_scalar(stop[:], best[:], 0.0, -BIG, ALU.is_lt, ALU.mult))
                ch.then(dve.tensor_tensor(logit[:], logit[:], stop[:], ALU.add))
                ch.then(dve.tensor_scalar(stop[:], best[:], float(P - 1), -BIG, ALU.is_gt, ALU.mult))
                ch.then(dve.tensor_tensor(logit[:], logit[:], stop[:], ALU.add))
                dve.wait_ge(key_landed, 16 * H)

                def spread_max(sign, value):
                    fwd = sign > 0
                    near = key[:, 0:L] if fwd else key[:, 2:L + 2]
                    ch.then(dve.tensor_tensor(stop[:], key[:, 1:L + 1], near, ALU.not_equal))
                    ch.then(dve.tensor_scalar(stop[:], stop[:], -BIG, None, ALU.mult))
                    view = (lambda t: t[:, 0:L]) if fwd else (lambda t: t[:, L - 1::-1])
                    ch.then(dve.tensor_tensor_scan(view(best), view(stop), view(value), -BIG, ALU.add, ALU.max))
                    ch.tick(dve.tensor_copy(ends[:, 0:1], best[:, L - 1:L] if fwd else best[:, 0:1]))
                    ch.tick(dve.tensor_reduce(ends[:, 1:2], stop[:], AX.X, ALU.min))
                    ch.wait()
                    dve.sem_inc(ask, 1)
                    n = 1 if fwd else 3
                    dve.wait_ge(got, n)
                    ch.then(dve.tensor_copy(row[:], k.psum[0:1, 0, 0:2 * P].rearrange("p (a c) -> p a c", a=2)))
                    first = slice(0, P, CHUNKS) if fwd else slice(CHUNKS - 1, P, CHUNKS)
                    ch.then(dve.memset(cut[:], 0.0))
                    ch.then(dve.memset(cut[0:1, first], -BIG))
                    ch.then(dve.memset(carried[:], -BIG))
                    ch.then(dve.tensor_tensor(row[:, 1, :], row[:, 1, :], cut[:], ALU.add))
                    rv = (lambda t: t) if fwd else (lambda t: t[0:1, ::-1])
                    out = row[0:1, 0, :]
                    ch.then(dve.tensor_tensor_scan(rv(cut[0:1, :]), rv(row[0:1, 1, :]), rv(out), -BIG, ALU.add, ALU.max))
                    if fwd:
                        ch.then(dve.tensor_copy(carried[:, 1:P], cut[:, 0:P - 1]))
                    else:
                        ch.then(dve.tensor_copy(carried[:, 0:P - 1], cut[:, 1:P]))
                    ch.then(dve.memset(carried[0:1, first], -BIG))
                    dve.sem_inc(ask, 1)
                    dve.wait_ge(got, n + 1)
                    ch.then(dve.tensor_copy(carry[:], k.psum[:, 1, 0:1]))
                    ch.then(dve.tensor_tensor_scan(view(best), view(stop), view(value), carry[:, 0:1], ALU.add, ALU.max))

                spread_max(1, logit)
                spread_max(-1, best)
                if leaky:
                    ch.then(dve.tensor_scalar(stop[:], stop[:], -1.0 / BIG, None, ALU.mult))
                    ch.then(dve.tensor_scalar(stop[:], stop[:], 0.5, None, ALU.is_gt))
                    ch.then(dve.tensor_tensor(key[:, 0:L], logit[:], best[:], ALU.subtract))
                    ch.then(dve.tensor_tensor(logit[:], stop[:], best[:], ALU.mult))
                    dve.sem_inc(best_ready, 1)
                    dve.sem_inc(flags_ready, 1)
                else:
                    ch.then(dve.tensor_tensor(key[:, 0:L], logit[:], best[:], ALU.subtract))
                dve.sem_inc(expo, 1)

            @block.tensor
            def _(pe):
                for n in (1, 3):
                    pe.wait_ge(ask, n)
                    for a in range(2):
                        ins = pe.transpose(k.psum[0:1, 0, a * P:(a + 1) * P], ends[:, a:a + 1], k.ident[:])
                    ins.then_inc(got, 1)
                    pe.wait_ge(ask, n + 1)
                    pe.transpose(k.psum[:, 1, 0:1], carried[0:1, :], k.ident[0:1, 0:1]).then_inc(got, 1)

            @block.scalar
            def _(act):
                act.wait_ge(expo, 1)
                act.activation(best[:], key[:, 0:L], ACT.Exp).then_inc(exp_done, 1)

        back = [sb(f"m{H}_back{b}", [P, P]) for b in range(2)]
        back_in = [sem(f"m{H}_back_in{b}") for b in range(2)]
        back_turned, back_out = sem(f"m{H}_back_turned"), sem(f"m{H}_back_out")
        TOTAL = OUTS * NBLK
        with nc.Block() as block:
            @block.sync
            def _(sp):
                for n in range(TOTAL):
                    a, c = divmod(n, NBLK)
                    if n >= 2:
                        sp.wait_ge(back_turned, n - 1)
                    sp.dma_start(back[n % 2][:], k.alphas[a, c * P:(c + 1) * P, :]).then_inc(back_in[n % 2], 16)

            @block.tensor
            def _(pe):
                for n in range(TOTAL):
                    pe.wait_ge(back_in[n % 2], 16 * (n // 2 + 1))
                    if n >= 2:
                        pe.wait_ge(back_out, n - 1)
                    pe.transpose(k.psum[:, n % 2, 0:P], back[n % 2][:], k.ident[:]).then_inc(back_turned, 1)

            @block.vector
            def _(dve):
                for n in range(TOTAL):
                    a, c = divmod(n, NBLK)
                    dve.wait_ge(back_turned, n + 1)
                    dve.tensor_copy(k.aux[:, c * BLK:(c + 1) * BLK, a * H:(a + 1) * H],
                                    k.psum[:, n % 2, 0:P].rearrange("p (s h) -> p s h", h=H)).then_inc(back_out, 1)


def one_hot(dve, k, out, g):
    return dve.tensor_tensor(out[:], k.iota[:].unsqueeze(1).to_broadcast([P, GROUP, P]),
                             k.dloc[:, bass.ds(g * GROUP, GROUP)].unsqueeze(2).to_broadcast([P, GROUP, P]),
                             ALU.is_equal)


def attend(nc, k, H, outs):
    AUX = outs * H
    W = D + AUX
    with ExitStack() as ctx:
        def sb(name, shape, dt=F32):
            return ctx.enter_context(nc.sbuf_tensor(name, shape, dt))

        sem = ctx.enter_context(semaphores(nc))

        rows = [sb(f"t{H}_rows{q}", [P, GROUP, D]) for q in range(RING)]
        msg = [sb(f"t{H}_msg{b}", [P, GROUP, W]) for b in range(2)]
        onehot = [sb(f"t{H}_onehot{b}", [P, GROUP, P]) for b in range(2)]
        run = sb(f"t{H}_run", [P, 2 * GROUP, W])
        landed = [sem(f"t{H}_landed{q}") for q in range(RING)]
        weighed, aux_copied = sem(f"t{H}_weighed"), sem(f"t{H}_aux_copied")
        onehot_ready, summed = sem(f"t{H}_onehot_ready"), sem(f"t{H}_summed")
        chained, kept = sem(f"t{H}_chained"), sem(f"t{H}_kept")
        block = ctx.enter_context(nc.Block())
        spill_rows = k.spill.rearrange("s p d -> p s d")
        R = 2 * GROUP

        @block.sync
        def _(sp):
            for it in passes(sp, PASSES):
                for q in range(RING):
                    g = it * RING + q
                    sp.wait_ge(weighed, g + 1)
                    sp.dma_start(rows[q][:], spill_rows[:, bass.ds(g * GROUP, GROUP), :]).then_inc(landed[q], 16)

        @block.gpsimd
        def _(pool):
            pool.sem_inc(weighed, RING)
            for it in passes(pool, PASSES):
                for q in range(RING):
                    g = it * RING + q
                    b = q % 2
                    pool.wait_ge(landed[q], (it + 1) * 16)
                    pool.wait_ge(summed, g * GROUP + GROUP)
                    for s in range(GROUP):
                        split = lambda t: t.rearrange("p (h c) -> p h c", h=H)
                        a = k.aux[:, bass.ds(g * GROUP + s, 1), 0:H].rearrange("p o h -> p (o h)")
                        ins = pool.tensor_tensor(split(msg[b][:, s, 0:D]), split(rows[q][:, s, :]),
                                                 a.unsqueeze(2).to_broadcast([P, H, D // H]), ALU.mult)
                    ins.then_inc(weighed, 1)

        @block.scalar
        def _(act):
            act.sem_inc(aux_copied, 2)
            act.sem_inc(kept, R)

            def copy_aux(it, q):
                g = it * RING + q
                act.wait_ge(summed, g * GROUP + GROUP)
                act.copy(msg[q % 2][:, :, D:W], k.aux[:, bass.ds(g * GROUP, GROUP), 0:AUX]).then_inc(aux_copied, 1)

            def keep_group(it, q, j):
                for s in range(GROUP):
                    st = (it * RING + q) * GROUP + s
                    act.wait_ge(chained, st + 1 + R)
                    act.wait_ge(kept, st + R)
                    act.copy(k.acc[:, bass.ds(j[q * GROUP + s], 1), 0:W].rearrange("p o w -> p (o w)"),
                             run[:, (q % 2) * GROUP + s, :]).then_inc(kept, 1)

            one_ahead(act, nc, k.step_j, NODE_TILES - 1, copy_aux, keep_group)

        @block.vector
        def _(dve):
            dve.memset(run[:, R - 1, :], 0.0)
            dve.sem_inc(chained, R)
            dve.sem_inc(onehot_ready, 2)

            def mark_group(it, q):
                g = it * RING + q
                dve.wait_ge(summed, g * GROUP + GROUP)
                one_hot(dve, k, onehot[q % 2], g).then_inc(onehot_ready, 1)

            def chain_group(it, q, _):
                for s in range(GROUP):
                    st = (it * RING + q) * GROUP + s
                    at = (q % 2) * GROUP + s
                    dve.wait_ge(summed, st + 1 + R)
                    dve.wait_ge(kept, st + 1)
                    dve.wait_ge(chained, st + R)
                    dve.scalar_tensor_tensor(out=run[:, at, :], in0=run[:, (at - 1) % R, :],
                                             scalar=k.keep[:, bass.ds(st, 1)], in1=k.psum[:, at, 0:W],
                                             op0=ALU.mult, op1=ALU.add).then_inc(chained, 1)

            one_ahead(dve, nc, None, None, mark_group, chain_group)

        @block.tensor
        def _(pe):
            pe.sem_inc(summed, R)
            for it in passes(pe, PASSES):
                for q in range(RING):
                    g = it * RING + q
                    b = q % 2
                    pe.wait_ge(weighed, g + 1 + RING)
                    pe.wait_ge(aux_copied, g + 1 + 2)
                    pe.wait_ge(onehot_ready, g + 1 + 2)
                    for s in range(GROUP):
                        pe.wait_ge(chained, g * GROUP + s + 1)
                        pe.matmul(k.psum[:, b * GROUP + s, 0:W], onehot[b][:, s, :], msg[b][:, s, :],
                                  start=True, stop=True).then_inc(summed, 1)


def flat(t):
    return t.rearrange("p t d -> p (t d)")


def over_tiles(row):
    return row.unsqueeze(1).to_broadcast([P, 2, D])


def norm_stats(dve, ch, value, stats, mean_var, var_ready):
    for t in range(2):
        ch.tick(dve.bn_stats(stats[:, t, :], value[:, t, :]))
    ch.wait()
    dve.sem_inc(ch.sem, 1)
    ch.n += 1
    for t in range(2):
        ins = dve.bn_aggr(mean_var[:, t, :], stats[:, t, :])
    ins.then_inc(var_ready, 1)


def norm_apply(dve, ch, out, value, mean_var, std):
    ch.then(dve.reciprocal(std[:], std[:]))
    for t in range(2):
        ch.tick(dve.tensor_scalar(out[:, t, :], value[:, t, :], mean_var[:, t, 0:1], std[:, t:t + 1],
                                    ALU.subtract, ALU.mult))
    ch.wait()


def gat_finish(nc, k, x, bias, slope):
    H = 4
    with ExitStack() as ctx:
        def sb(name, shape, dt=F32):
            return ctx.enter_context(nc.sbuf_tensor(name, shape, dt))

        sem = ctx.enter_context(semaphores(nc))

        own = sb("n1_own", [P, NT, H])
        top = sb("n1_top", [P, NT, H])
        scaled = sb("n1_scaled", [P, NT, H])
        den = sb("n1_den", [P, NT, H])
        bias_row, slope_col, eps = sb("n1_bias", [P, D]), sb("n1_slope", [P, 1]), sb("n1_eps", [P, 1])
        B = range(PAIRS)
        xin = [sb(f"n1_x{b}", [P, 2, D]) for b in B]
        hin = [sb(f"n1_h{b}", [P, 2, D]) for b in B]
        y = [sb(f"n1_y{b}", [P, 2, D]) for b in B]
        neg = [sb(f"n1_neg{b}", [P, 2, D]) for b in B]
        out = [sb(f"n1_out{b}", [P, 2, D]) for b in B]
        stats = [sb(f"n1_stats{b}", [P, 2, 6]) for b in B]
        mean_var = [sb(f"n1_mv{b}", [P, 2, 2]) for b in B]
        std = [sb(f"n1_std{b}", [P, 2]) for b in B]
        consts, diff_ready, exps_ready, coef_ready, chain = (
            sem(f"n1_{n}") for n in ("consts", "diff_ready", "exps_ready", "coef_ready", "chain"))
        loads = [sem(f"n1_loads{b}") for b in B]
        own_ready, var_ready, std_ready, out_ready = (
            sem(f"n1_{n}") for n in ("own_ready", "var_ready", "std_ready", "out_ready"))
        stored = [sem(f"n1_stored{b}") for b in B]
        loop_chain = sem("n1_loop_chain")
        block = ctx.enter_context(nc.Block())
        CREDIT = PAIRS
        heads = lambda t: t.rearrange("p t (h c) -> p t h c", h=H)

        def per_head(table, m):
            return table[:, bass.ds(2 * m, 2), :].unsqueeze(3).to_broadcast([P, 2, H, D // H])

        @block.sync
        def _(sp):
            sp.dma_start(bias_row[:], bias.partition_broadcast(P)).then_inc(consts, 16)
            sp.dma_start(slope_col[:], slope.partition_broadcast(P)).then_inc(consts, 16)
            for it in passes(sp, NODE_PASSES):
                for b in B:
                    m = it * PAIRS + b
                    sp.wait_ge(out_ready, m + 1)
                    sp.dma_start(xin[b][:], pair(x, m)).then_inc(loads[b], 16)
                    sp.dma_start(hin[b][:], pair(k.hrow, m)[:, :, 0:D]).then_inc(loads[b], 16)

        @block.gpsimd
        def _(pool):
            pool.wait_ge(coef_ready, 1)
            for it in passes(pool, NODE_PASSES):
                for b in B:
                    m = it * PAIRS + b
                    pool.wait_ge(loads[b], (it + 1) * 32)
                    for t in range(2):
                        w = own[:, bass.ds(2 * m + t, 1), :].rearrange("p o h -> p (o h)")
                        ins = pool.tensor_tensor(hin[b][:, t].rearrange("p (h c) -> p h c", h=H),
                                                 hin[b][:, t].rearrange("p (h c) -> p h c", h=H),
                                                 w.unsqueeze(2).to_broadcast([P, H, D // H]), ALU.mult)
                    ins.then_inc(own_ready, 1)
                for b in B:
                    m = it * PAIRS + b
                    pool.wait_ge(out_ready, m + 1 + CREDIT)
                    pool.dma_start(pair(k.x1, m), out[b][:]).then_inc(stored[b], 16)
            for b in B:
                pool.wait_ge(stored[b], 16 * NODE_PASSES)

        @block.scalar
        def _(act):
            act.wait_ge(diff_ready, 1)
            act.activation(scaled[:], scaled[:], ACT.Exp)
            act.activation(own[:], own[:], ACT.Exp).then_inc(exps_ready, 1)
            for it in passes(act, NODE_PASSES):
                for b in B:
                    act.wait_ge(var_ready, it * PAIRS + b + 1)
                    act.activation(std[b][:], mean_var[b][:, :, 1], ACT.Sqrt, bias=eps[:, 0:1]).then_inc(std_ready, 1)

        @block.vector
        def _(dve):
            dve.sem_inc(out_ready, CREDIT)
            ch = Chain(dve, chain)
            ch.tick(dve.memset(eps[:], LN_EPS))
            ch.then(dve.memset(k.acc[:, NODE_TILES:NT, :], 0.0))
            maxima, weights, flag = (k.acc[:, :, D + a * H:D + (a + 1) * H] for a in (1, 0, 2))
            ch.then(dve.tensor_tensor(own[:], k.att[:, :, 0:H], k.att[:, :, H:2 * H], ALU.add))
            ch.then(dve.scalar_tensor_tensor(out=own[:], in0=own[:], scalar=0.2, in1=own[:],
                                             op0=ALU.mult, op1=ALU.max))
            ch.then(dve.tensor_scalar(den[:], flag, -1.0, BIG, ALU.add, ALU.mult))
            ch.then(dve.tensor_tensor(scaled[:], maxima, den[:], ALU.add))
            ch.then(dve.tensor_tensor(top[:], scaled[:], own[:], ALU.max))
            ch.then(dve.tensor_tensor(scaled[:], scaled[:], top[:], ALU.subtract))
            dve.tensor_tensor(own[:], own[:], top[:], ALU.subtract).then_inc(diff_ready, 1)
            dve.wait_ge(exps_ready, 1)
            ch.then(dve.tensor_tensor(den[:], scaled[:], weights, ALU.mult))
            ch.then(dve.tensor_tensor(den[:], den[:], own[:], ALU.add))
            ch.then(dve.tensor_scalar(den[:], den[:], 1e-16, None, ALU.add))
            ch.then(dve.reciprocal(den[:], den[:]))
            ch.tick(dve.tensor_tensor(scaled[:], scaled[:], den[:], ALU.mult))
            ch.then(dve.tensor_tensor(own[:], own[:], den[:], ALU.mult))
            dve.sem_inc(coef_ready, 1)
            dve.wait_ge(consts, 32)
            OPS = 12 * PAIRS
            for it in passes(dve, NODE_PASSES):
                ch = Chain(dve, loop_chain, it * OPS)
                for b in B:
                    m = it * PAIRS + b
                    for t in range(2):
                        a = scaled[:, bass.ds(2 * m + t, 1), :].rearrange("p o h -> p (o h)")
                        ch.tick(dve.tensor_tensor(
                            y[b][:, t].rearrange("p (h c) -> p h c", h=H),
                            k.acc[:, bass.ds(2 * m + t, 1), 0:D].rearrange("p o (h c) -> p (o h) c", h=H),
                            a.unsqueeze(2).to_broadcast([P, H, D // H]), ALU.mult))
                    dve.wait_ge(own_ready, m + 1)
                    ch.wait()
                    ch.then(dve.tensor_tensor(y[b][:], y[b][:], hin[b][:], ALU.add))
                    ch.then(dve.tensor_tensor(y[b][:], y[b][:], over_tiles(bias_row[:]), ALU.add))
                    ch.then(dve.tensor_scalar(neg[b][:], y[b][:], 0.0, None, ALU.min))
                    ch.then(dve.scalar_tensor_tensor(out=y[b][:], in0=y[b][:], scalar=0.0, in1=xin[b][:],
                                                     op0=ALU.max, op1=ALU.add))
                    ch.then(dve.scalar_tensor_tensor(out=y[b][:], in0=neg[b][:], scalar=slope_col[:, 0:1],
                                                     in1=y[b][:], op0=ALU.mult, op1=ALU.add))
                    norm_stats(dve, ch, y[b], stats[b], mean_var[b], var_ready)
                for b in B:
                    m = it * PAIRS + b
                    dve.wait_ge(std_ready, m + 1)
                    wait_if_any(dve, stored[b], it * 16)
                    ch.then(dve.reciprocal(std[b][:], std[b][:]))
                    for t in range(2):
                        ins = dve.tensor_scalar(out[b][:, t, :], y[b][:, t, :], mean_var[b][:, t, 0:1],
                                                std[b][:, t:t + 1], ALU.subtract, ALU.mult)
                        if t == 0:
                            ch.tick(ins)
                    ins.then_inc(out_ready, 1)
                assert ch.n == OPS


def gin_edges(nc, k, edge_attr):
    with ExitStack() as ctx:
        def sb(name, shape, dt=F32):
            return ctx.enter_context(nc.sbuf_tensor(name, shape, dt))

        sem = ctx.enter_context(semaphores(nc))

        R = 2 * GROUP
        idx = [sb(f"g_idx{q}", [P, GROUP], I32) for q in range(RING)]
        rows = [sb(f"g_rows{q}", [P, GROUP, D]) for q in range(RING)]
        attr = [sb(f"g_attr{q}", [P, GROUP, D]) for q in range(RING)]
        msg = [sb(f"g_msg{b}", [P, GROUP, D]) for b in range(2)]
        onehot = [sb(f"g_onehot{b}", [P, GROUP, P]) for b in range(2)]
        run = sb("g_run", [P, R, D])
        gathered = [sem(f"g_gathered{q}") for q in range(RING)]
        attr_landed = [sem(f"g_attr_landed{q}") for q in range(RING)]
        idx_landed = [sem(f"g_idx_landed{q}") for q in range(RING)]
        passed, added, msg_ready = (sem(f"g_{n}") for n in ("passed", "added", "msg_ready"))
        onehot_ready, summed, chained, kept = (
            sem(f"g_{n}") for n in ("onehot_ready", "summed", "chained", "kept"))
        block = ctx.enter_context(nc.Block())

        @block.sync
        def _(sp):
            for it in passes(sp, PASSES):
                i = load_indices(nc, sp, k.step_i, it * (RING * GROUP), RING * GROUP, EA_TILES - 1)
                for q in range(RING):
                    g = it * RING + q
                    wait_if_any(sp, gathered[q], it * (16 * GROUP))
                    sp.dma_start(idx[q][:], k.src_idx[:, bass.ds(g * GROUP, GROUP)]).then_inc(idx_landed[q], 16)
                    sp.wait_ge(msg_ready, g + 1)
                    for s in range(GROUP):
                        sp.dma_start(attr[q][:, s, :], edge_attr[bass.ds(i[q * GROUP + s] * P, P), :]
                                     ).then_inc(attr_landed[q], 16)

        @block.gpsimd
        def _(pool):
            for it in passes(pool, PASSES):
                for q in range(RING):
                    pool.wait_ge(idx_landed[q], (it + 1) * 16)
                    pool.wait_ge(added, it * RING + q + 1)
                    pool.sem_inc(passed, 1)
                    for s in range(GROUP):
                        pool.indirect_dma_start(rows[q][:, s, :], None, k.x1,
                                                bass.IndirectOffsetOnAxis(ap=idx[q][:, s:s + 1], axis=0)
                                                ).then_inc(gathered[q], 16)

        @block.scalar
        def _(act):
            act.sem_inc(msg_ready, RING)
            act.sem_inc(kept, R)

            def relu_group(it, q):
                g = it * RING + q
                act.wait_ge(added, g + 1 + RING)
                act.wait_ge(summed, g * GROUP + GROUP)
                act.activation(flat(msg[q % 2][:]), flat(attr[q][:]), ACT.Relu).then_inc(msg_ready, 1)

            def keep_group(it, q, j):
                for s in range(GROUP):
                    st = (it * RING + q) * GROUP + s
                    act.wait_ge(chained, st + 1 + R)
                    act.wait_ge(kept, st + R)
                    act.copy(k.acc[:, bass.ds(j[q * GROUP + s], 1), 0:D].rearrange("p o w -> p (o w)"),
                             run[:, (q % 2) * GROUP + s, :]).then_inc(kept, 1)

            one_ahead(act, nc, k.step_j, NODE_TILES - 1, relu_group, keep_group)

        @block.vector
        def _(dve):
            dve.memset(run[:, R - 1, :], 0.0)
            dve.sem_inc(added, RING)
            dve.sem_inc(chained, R)
            dve.sem_inc(onehot_ready, 2)

            def add_group(it, q):
                g = it * RING + q
                dve.wait_ge(summed, g * GROUP + GROUP)
                one_hot(dve, k, onehot[q % 2], g).then_inc(onehot_ready, 1)
                dve.wait_ge(gathered[q], (it + 1) * (16 * GROUP))
                dve.wait_ge(attr_landed[q], (it + 1) * (16 * GROUP))
                dve.tensor_tensor(flat(attr[q][:]), flat(attr[q][:]), flat(rows[q][:]), ALU.add).then_inc(added, 1)

            def chain_group(it, q, _):
                for s in range(GROUP):
                    st = (it * RING + q) * GROUP + s
                    at = (q % 2) * GROUP + s
                    dve.wait_ge(summed, st + 1 + R)
                    dve.wait_ge(kept, st + 1)
                    dve.wait_ge(chained, st + R)
                    dve.scalar_tensor_tensor(out=run[:, at, :], in0=run[:, (at - 1) % R, :],
                                             scalar=k.keep[:, bass.ds(st, 1)], in1=k.psum[:, at, 0:D],
                                             op0=ALU.mult, op1=ALU.add).then_inc(chained, 1)

            one_ahead(dve, nc, None, None, add_group, chain_group)

        @block.tensor
        def _(pe):
            pe.sem_inc(summed, R)
            for it in passes(pe, PASSES):
                for q in range(RING):
                    g = it * RING + q
                    b = q % 2
                    pe.wait_ge(msg_ready, g + 1 + RING)
                    pe.wait_ge(onehot_ready, g + 1 + 2)
                    for s in range(GROUP):
                        pe.wait_ge(chained, g * GROUP + s + 1)
                        pe.matmul(k.psum[:, b * GROUP + s, 0:D], onehot[b][:, s, :], msg[b][:, s, :],
                                  start=True, stop=True).then_inc(summed, 1)


def turn_pair(pe, bank, rows, ident):
    for h in range(2):
        for t in range(2):
            at = (h * 2 + t) * P
            ins = pe.transpose(bank[:, at:at + P], rows[:, t, h * P:(h + 1) * P], ident)
    return ins


def gin_nodes(nc, k, w1, b1, w2, b2, gamma, beta, w_next):
    with ExitStack() as ctx:
        def sb(name, shape, dt=F32):
            return ctx.enter_context(nc.sbuf_tensor(name, shape, dt))

        sem = ctx.enter_context(semaphores(nc))

        B = range(PAIRS)
        ws = [sb(f"n2_w{n}", [P, 2, D]) for n in range(3)]
        b1_col, rows3 = sb("n2_b1", [P, 2]), sb("n2_rows", [P, 3, D])
        eps, zero = sb("n2_eps", [P, 1]), sb("n2_zero", [P, 5, D])
        xin = [sb(f"n2_x{b}", [P, 2, D]) for b in B]
        z = [sb(f"n2_z{b}", [P, 2, D]) for b in B]
        y = [sb(f"n2_y{b}", [P, 2, D]) for b in B]
        out = [sb(f"n2_out{b}", [P, 2, D]) for b in B]
        turned_sb = [sb(f"n2_turned{b}", [P, 2, 2 * P]) for b in B]
        hidden = [sb(f"n2_hidden{b}", [P, 2, 2 * P]) for b in B]
        stats = [sb(f"n2_stats{b}", [P, 2, 6]) for b in B]
        mean_var = [sb(f"n2_mv{b}", [P, 2, 2]) for b in B]
        std = [sb(f"n2_std{b}", [P, 2]) for b in B]
        consts = sem("n2_consts")
        landed = [sem(f"n2_landed{b}") for b in B]
        stored = [sem(f"n2_stored{b}") for b in B]
        zeroed, zero_out = sem("n2_zeroed"), sem("n2_zero_out")
        (z_ready, turned, copied, mixed, hidden_ready, h_done, var_ready, std_ready, out_ready, next_done,
         support_ready, chain) = (sem(f"n2_{n}") for n in (
             "z_ready", "turned", "copied", "mixed", "hidden_ready", "h_done", "var_ready", "std_ready",
             "out_ready", "next_done", "support_ready", "chain"))
        h_taken = sem("n2_h_taken")
        block = ctx.enter_context(nc.Block())

        @block.sync
        def _(sp):
            for n, w in enumerate((w1, w2, w_next)):
                sp.dma_start(ws[n][:], w.rearrange("(h p) n -> p h n", p=P)).then_inc(consts, 16)
            sp.dma_start(b1_col[:], b1).then_inc(consts, 16)
            for n, r in enumerate((b2, gamma, beta)):
                sp.dma_start(rows3[:, n, :], r.partition_broadcast(P)).then_inc(consts, 16)
            for it in passes(sp, NODE_PASSES):
                for b in B:
                    m = it * PAIRS + b
                    sp.wait_ge(out_ready, m + 1)
                    sp.dma_start(xin[b][:], pair(k.x1, m)).then_inc(landed[b], 16)

        @block.gpsimd
        def _(pool):
            pool.memset(zero[:], 0.0).then_inc(zeroed, 1)
            pool.wait_ge(zeroed, 1)
            for table in k.gcn:
                for t in range(0, NT, 5):
                    pool.dma_start(table.rearrange("(t p) d -> p t d", p=P)[:, t:t + 5, :], zero[:]
                                   ).then_inc(zero_out, 16)
            for it in passes(pool, NODE_PASSES):
                for b in B:
                    m = it * PAIRS + b
                    pool.wait_ge(out_ready, m + 1 + PAIRS)
                    pool.dma_start(pair(k.x2, m), out[b][:]).then_inc(stored[b], 16)
            for b in B:
                pool.wait_ge(stored[b], 16 * NODE_PASSES)
            pool.wait_ge(zero_out, 16 * len(k.gcn) * (NT // 5))

        @block.scalar
        def _(act):
            act.sem_inc(copied, BANKS)
            act.sem_inc(hidden_ready, BANKS)
            act.sem_inc(support_ready, BANKS)
            act.wait_ge(consts, 16 * 7)
            for it in passes(act, NODE_PASSES):
                def copy_turned(n):
                    for b in B:
                        act.wait_ge(turned, (it * 2 + n) * PAIRS + b + 1)
                        act.copy(flat(turned_sb[b][:]), k.psum[:, b % BANKS, :]).then_inc(copied, 1)

                def root(n):
                    for b in B:
                        act.wait_ge(var_ready, (it * 2 + n) * PAIRS + b + 1)
                        act.activation(std[b][:], mean_var[b][:, :, 1], ACT.Sqrt, bias=eps[:, 0:1]
                                       ).then_inc(std_ready, 1)

                copy_turned(0)
                for b in B:
                    act.wait_ge(mixed, it * PAIRS + b + 1)
                    for f in range(2):
                        ins = act.activation(hidden[b][:, f, :], k.psum[:, 2 + b % BANKS, f * 2 * P:(f + 1) * 2 * P],
                                             ACT.Relu, bias=b1_col[:, f:f + 1])
                    ins.then_inc(hidden_ready, 1)
                root(0)
                root(1)
                copy_turned(1)
                for b in B:
                    m = it * PAIRS + b
                    act.wait_ge(next_done, m + 1)
                    act.copy(k.support[:, bass.ds(2 * m, 2), :],
                             k.psum[:, 6 + b % BANKS, :].rearrange("p (t d) -> p t d", t=2)
                             ).then_inc(support_ready, 1)

        @block.tensor
        def _(pe):
            pe.wait_ge(consts, 16 * 7)
            for it in passes(pe, NODE_PASSES):
                def rows_by(n, b, left, at):
                    for t in range(2):
                        for h in range(2):
                            ins = pe.matmul(k.psum[:, at, t * D:(t + 1) * D], left[b][:, h, t * P:(t + 1) * P],
                                            ws[n][:, h, :], start=(h == 0), stop=(h == 1))
                    return ins

                for b in B:
                    m = it * PAIRS + b
                    pe.wait_ge(z_ready, m + 1)
                    pe.wait_ge(copied, bank_free(it * 2 * PAIRS + b, b))
                    turn_pair(pe, k.psum[:, b % BANKS], z[b], k.ident[:]).then_inc(turned, 1)
                for b in B:
                    pe.wait_ge(copied, it * 2 * PAIRS + b + 1 + BANKS)
                    pe.wait_ge(hidden_ready, bank_free(it * PAIRS + b, b))
                    for f in range(2):
                        for h in range(2):
                            ins = pe.matmul(k.psum[:, 2 + b % BANKS, f * 2 * P:(f + 1) * 2 * P],
                                            ws[0][:, h, f * P:(f + 1) * P], turned_sb[b][:, h, :],
                                            start=(h == 0), stop=(h == 1))
                    ins.then_inc(mixed, 1)
                for b in B:
                    m = it * PAIRS + b
                    pe.wait_ge(hidden_ready, m + 1 + BANKS)
                    pe.wait_ge(h_taken, bank_free(m, b))
                    rows_by(1, b, hidden, 4 + b % BANKS).then_inc(h_done, 1)
                for b in B:
                    pe.wait_ge(out_ready, it * PAIRS + b + 1 + PAIRS)
                    pe.wait_ge(copied, bank_free((it * 2 + 1) * PAIRS + b, b))
                    turn_pair(pe, k.psum[:, b % BANKS], out[b], k.ident[:]).then_inc(turned, 1)
                for b in B:
                    pe.wait_ge(copied, (it * 2 + 1) * PAIRS + b + 1 + BANKS)
                    pe.wait_ge(support_ready, bank_free(it * PAIRS + b, b))
                    rows_by(2, b, turned_sb, 6 + b % BANKS).then_inc(next_done, 1)

        @block.vector
        def _(dve):
            dve.sem_inc(out_ready, PAIRS)
            dve.sem_inc(h_taken, BANKS)
            dve.memset(k.acc[:, NODE_TILES:NT, :], 0.0)
            OPS = 17 * PAIRS
            Chain(dve, chain).then(dve.memset(eps[:], LN_EPS))
            dve.wait_ge(consts, 16 * 7)
            for it in passes(dve, NODE_PASSES):
                ch = Chain(dve, chain, it * OPS + 1)
                for b in B:
                    m = it * PAIRS + b
                    dve.wait_ge(landed[b], (it + 1) * 16)
                    dve.tensor_tensor(z[b][:], xin[b][:], k.acc[:, bass.ds(2 * m, 2), 0:D], ALU.add).then_inc(z_ready, 1)
                for b in B:
                    m = it * PAIRS + b
                    dve.wait_ge(h_done, m + 1)
                    h = k.psum[:, 4 + b % BANKS, :].rearrange("p (t d) -> p t d", t=2)
                    ch.then(dve.tensor_tensor(y[b][:], h, over_tiles(rows3[:, 0, :]), ALU.add))
                    dve.sem_inc(h_taken, 1)
                    ch.then(dve.scalar_tensor_tensor(out=y[b][:], in0=y[b][:], scalar=0.0, in1=xin[b][:],
                                                     op0=ALU.max, op1=ALU.add))
                    norm_stats(dve, ch, y[b], stats[b], mean_var[b], var_ready)
                for b in B:
                    dve.wait_ge(std_ready, it * 2 * PAIRS + b + 1)
                    norm_apply(dve, ch, y[b], y[b], mean_var[b], std[b])
                    ch.then(dve.tensor_tensor(y[b][:], y[b][:], over_tiles(rows3[:, 1, :]), ALU.mult))
                    ch.then(dve.tensor_tensor(y[b][:], y[b][:], over_tiles(rows3[:, 2, :]), ALU.add))
                    ch.then(dve.tensor_tensor(y[b][:], y[b][:], xin[b][:], ALU.add))
                    norm_stats(dve, ch, y[b], stats[b], mean_var[b], var_ready)
                for b in B:
                    dve.wait_ge(std_ready, (it * 2 + 1) * PAIRS + b + 1)
                    wait_if_any(dve, stored[b], it * 16)
                    norm_apply(dve, ch, out[b], y[b], mean_var[b], std[b])
                    dve.sem_inc(out_ready, 1)
                assert ch.n == OPS, ch.n


def gcn_edges(nc, k):
    with ExitStack() as ctx:
        def sb(name, shape, dt=F32):
            return ctx.enter_context(nc.sbuf_tensor(name, shape, dt))

        sem = ctx.enter_context(semaphores(nc))

        away = sb("c_away", [P, STEPS])
        earlier = sb("c_earlier", [P, P])
        srow = [sb(f"c_srow{q}", [P, GROUP, P]) for q in range(RING)]
        onehot = [sb(f"c_onehot{b}", [P, GROUP, P]) for b in range(2)]
        same = [sb(f"c_same{b}", [P, GROUP, P]) for b in range(2)]
        dump = [sb(f"c_dump{b}", [P, GROUP, P]) for b in range(2)]
        before = [sb(f"c_before{b}", [P, GROUP]) for b in range(2)]
        shift = [sb(f"c_shift{b}", [P, GROUP]) for b in range(2)]
        target = [sb(f"c_target{q}", [P, GROUP], I32) for q in range(RING)]
        mix = [sb(f"c_mix{b}", [P, GROUP * P]) for b in range(2)]
        update = [sb(f"c_update{q}", [P, GROUP, D]) for q in range(RING)]
        srow_landed = [sem(f"c_srow_landed{q}") for q in range(RING)]
        scattered = [sem(f"c_scattered{a}") for a in range(GROUP)]
        setup, chain, passed = sem("c_setup"), sem("c_chain"), sem("c_passed")
        built, target_ready, mixed, mix_ready, spread, update_ready = (
            sem(f"c_{n}") for n in ("built", "target_ready", "mixed", "mix_ready", "spread", "update_ready"))
        block = ctx.enter_context(nc.Block())
        src_rows = k.rows_src.rearrange("(o s) l -> o (s l)", o=1)

        @block.sync
        def _(sp):
            for it in passes(sp, PASSES):
                for q in range(RING):
                    g = it * RING + q
                    sp.wait_ge(built, g + 1)
                    sp.dma_start(srow[q][:].rearrange("p s l -> p (s l)"),
                                 src_rows[:, bass.ds(g * (GROUP * P), GROUP * P)].partition_broadcast(P)
                                 ).then_inc(srow_landed[q], 16)

        @block.vector
        def _(dve):
            OPS = RING * 6
            FIRST = 3
            ch = Chain(dve, chain)
            ch.tick(dve.tensor_scalar(away[:], k.src[:], -1.0, float(SPARE_ROW), ALU.mult, ALU.add))
            ch.then(dve.tensor_scalar(earlier[:], k.iota[:], k.lane[:, 0:1], None, ALU.is_lt))
            ch.then(dve.tensor_scalar(away[:], away[:], k.lane[:, 0:1], None, ALU.add))
            assert ch.n == FIRST
            dve.sem_inc(built, RING)
            for it in passes(dve, PASSES):
                ch = Chain(dve, chain, it * OPS + FIRST)
                for q in range(RING):
                    g = it * RING + q
                    b = q % 2
                    dve.wait_ge(mixed, g + 1)
                    one_hot(dve, k, onehot[b], g)
                    dve.wait_ge(srow_landed[q], (it + 1) * 16)
                    for s in range(GROUP):
                        st = g * GROUP + s
                        dve.tensor_scalar(same[b][:, s, :], srow[q][:, s, :], k.src[:, bass.ds(st, 1)],
                                          k.weight[:, bass.ds(st, 1)], ALU.is_equal, ALU.mult)
                        ch.tick(dve.scalar_tensor_tensor(
                            out=dump[b][:, s, :], in0=srow[q][:, s, :], scalar=k.src[:, bass.ds(st, 1)],
                            in1=earlier[:], op0=ALU.is_equal, op1=ALU.mult, accum_out=before[b][:, s:s + 1]))
                    ch.wait()
                    dve.sem_inc(built, 1)
                    ch.then(dve.scalar_tensor_tensor(out=shift[b][:], in0=before[b][:], scalar=0.5,
                                                     in1=away[:, bass.ds(g * GROUP, GROUP)],
                                                     op0=ALU.is_gt, op1=ALU.mult))
                    dve.wait_ge(passed, g * GROUP + GROUP)
                    ch.tick(dve.tensor_tensor(target[q][:], shift[b][:], k.src[:, bass.ds(g * GROUP, GROUP)],
                                                ALU.add))
                    ch.wait()
                    dve.sem_inc(target_ready, 1)
                assert ch.n == OPS

        @block.tensor
        def _(pe):
            pe.sem_inc(mixed, 2)
            pe.sem_inc(spread, 2)

            def mix_group(it, q):
                g = it * RING + q
                b = q % 2
                pe.wait_ge(built, g + 1 + RING)
                pe.wait_ge(mix_ready, g + 1)
                for s in range(GROUP):
                    ins = pe.matmul(k.psum[:, b, s * P:(s + 1) * P], onehot[b][:, s, :], same[b][:, s, :],
                                    start=True, stop=True)
                ins.then_inc(mixed, 1)

            def spread_group(it, q, j):
                g = it * RING + q
                b = q % 2
                pe.wait_ge(mix_ready, g + 1 + 2)
                pe.wait_ge(update_ready, g + 1)
                for s in range(GROUP):
                    ins = pe.matmul(k.psum[:, 2 + 2 * b + s // 2, (s % 2) * D:(s % 2 + 1) * D],
                                    mix[b][:, s * P:(s + 1) * P],
                                    k.support[:, bass.ds(j[q * GROUP + s], 1), :].rearrange("p o d -> p (o d)"),
                                    start=True, stop=True)
                ins.then_inc(spread, 1)

            one_ahead(pe, nc, k.step_j, NODE_TILES - 1, mix_group, spread_group)

        @block.scalar
        def _(act):
            act.sem_inc(mix_ready, 2)
            act.sem_inc(update_ready, 2)

            def copy_mix(it, q):
                g = it * RING + q
                b = q % 2
                act.wait_ge(mixed, g + 1 + 2)
                act.wait_ge(spread, g + 1)
                act.copy(mix[b][:], k.psum[:, b, :]).then_inc(mix_ready, 1)

            def copy_update(it, q, _):
                g = it * RING + q
                b = q % 2
                act.wait_ge(spread, g + 1 + 2)
                act.wait_ge(passed, g * GROUP + GROUP)
                act.copy(flat(update[q][:]), flat(k.psum[:, 2 + 2 * b:4 + 2 * b, :])).then_inc(update_ready, 1)

            one_ahead(act, nc, None, None, copy_mix, copy_update)

        @block.gpsimd
        def _(pool):
            pool.sem_inc(passed, (RING - 1) * GROUP)
            for it in passes(pool, PASSES):
                for q in range(RING):
                    g = it * RING + q
                    b = q % 2
                    pool.wait_ge(update_ready, g + 1 + 2)
                    pool.wait_ge(target_ready, g + 1)
                    for a in range(GROUP):
                        wait_if_any(pool, scattered[a], g * 16)
                        pool.sem_inc(passed, 1)
                        pool.indirect_dma_start(k.gcn[a],
                                                bass.IndirectOffsetOnAxis(ap=target[q][:, a:a + 1], axis=0),
                                                update[q][:, a, :], None, compute_op=ALU.add
                                                ).then_inc(scattered[a], 16)
            for a in range(GROUP):
                pool.wait_ge(scattered[a], 16 * PASSES * RING)


def gcn_nodes(nc, k, bias, gamma, beta, wq, wk, wv, bq, bkv):
    with ExitStack() as ctx:
        def sb(name, shape, dt=F32):
            return ctx.enter_context(nc.sbuf_tensor(name, shape, dt))

        sem = ctx.enter_context(semaphores(nc))

        B = range(PAIRS)
        ws = [sb(f"n3_w{n}", [P, 2, D]) for n in range(3)]
        rows4 = sb("n3_rows", [P, 4, D])
        bkv_row, eps = sb("n3_bkv", [P, 2 * D]), sb("n3_eps", [P, 1])
        sums = [sb(f"n3_sums{b}", [P, GROUP, 2, D]) for b in B]
        xin = [sb(f"n3_x{b}", [P, 2, D]) for b in B]
        y = [sb(f"n3_y{b}", [P, 2, D]) for b in B]
        out = [sb(f"n3_out{b}", [P, 2, D]) for b in B]
        xn = [sb(f"n3_xn{b}", [P, 2, D]) for b in B]
        kv = [sb(f"n3_kv{b}", [P, 2, 2 * D]) for b in B]
        turned_sb = [sb(f"n3_turned{b}", [P, 2, 2 * P]) for b in B]
        stats = [sb(f"n3_stats{b}", [P, 2, 6]) for b in B]
        mean_var = [sb(f"n3_mv{b}", [P, 2, 2]) for b in B]
        std = [sb(f"n3_std{b}", [P, 2]) for b in B]
        consts = sem("n3_consts")
        landed = [sem(f"n3_landed{b}") for b in B]
        stored = [sem(f"n3_stored{b}") for b in B]
        kv_stored = [sem(f"n3_kv_stored{b}") for b in B]
        (halved, taken, var_ready, std_ready, out_ready, xn_ready, turned, copied, projected, kv_ready, chain) = (
            sem(f"n3_{n}") for n in ("halved", "taken", "var_ready", "std_ready", "out_ready", "xn_ready", "turned",
                                     "copied", "projected", "kv_ready", "chain"))
        block = ctx.enter_context(nc.Block())

        @block.sync
        def _(sp):
            for n, w in enumerate((wq, wk, wv)):
                sp.dma_start(ws[n][:], w.rearrange("(h p) n -> p h n", p=P)).then_inc(consts, 16)
            for n, r in enumerate((bias, gamma, beta, bq)):
                sp.dma_start(rows4[:, n, :], r.partition_broadcast(P)).then_inc(consts, 16)
            sp.dma_start(bkv_row[:], bkv.partition_broadcast(P)).then_inc(consts, 16)
            for it in passes(sp, NODE_PASSES):
                for b in B:
                    m = it * PAIRS + b
                    sp.wait_ge(taken, m + 1)
                    for a in range(GROUP):
                        sp.dma_start(sums[b][:, a], pair(k.gcn[a], m)).then_inc(landed[b], 16)
                    sp.dma_start(xin[b][:], pair(k.x2, m)).then_inc(landed[b], 16)

        @block.gpsimd
        def _(pool):
            for it in passes(pool, NODE_PASSES):
                for b in B:
                    pool.wait_ge(landed[b], (it + 1) * (16 * (GROUP + 1)))
                    pool.tensor_tensor(flat(sums[b][:, 2]), flat(sums[b][:, 2]), flat(sums[b][:, 3]),
                                       ALU.add).then_inc(halved, 1)
                for b in B:
                    m = it * PAIRS + b
                    pool.wait_ge(out_ready, m + 1)
                    pool.dma_start(pair(k.x3, m), out[b][:]).then_inc(stored[b], 16)
                for b in B:
                    m = it * PAIRS + b
                    pool.wait_ge(kv_ready, m + 1 + BANKS)
                    pool.dma_start(pair(k.kv, m), kv[b][:]).then_inc(kv_stored[b], 16)
            for b in B:
                pool.wait_ge(stored[b], 16 * NODE_PASSES)
                pool.wait_ge(kv_stored[b], 16 * NODE_PASSES)

        @block.scalar
        def _(act):
            act.sem_inc(copied, BANKS)
            act.wait_ge(consts, 16 * 8)
            for it in passes(act, NODE_PASSES):
                for n in range(2):
                    for b in B:
                        act.wait_ge(var_ready, (it * 2 + n) * PAIRS + b + 1)
                        act.activation(std[b][:], mean_var[b][:, :, 1], ACT.Sqrt, bias=eps[:, 0:1]
                                       ).then_inc(std_ready, 1)
                for b in B:
                    act.wait_ge(turned, it * PAIRS + b + 1)
                    act.copy(flat(turned_sb[b][:]), k.psum[:, b % BANKS, :]).then_inc(copied, 1)

        @block.tensor
        def _(pe):
            pe.wait_ge(consts, 16 * 8)
            for it in passes(pe, NODE_PASSES):
                for b in B:
                    pe.wait_ge(xn_ready, it * PAIRS + b + 1)
                    pe.wait_ge(copied, bank_free(it * PAIRS + b, b))
                    turn_pair(pe, k.psum[:, b % BANKS], xn[b], k.ident[:]).then_inc(turned, 1)
                for b in B:
                    m = it * PAIRS + b
                    pe.wait_ge(copied, m + 1 + BANKS)
                    pe.wait_ge(kv_ready, bank_free(m, b))
                    for t in range(2):
                        for n in range(3):
                            bank, at = (0, t * D) if n == 0 else (1 + t, (n - 1) * D)
                            bank += 2 + 3 * (b % BANKS)
                            for h in range(2):
                                ins = pe.matmul(k.psum[:, bank, at:at + D], turned_sb[b][:, h, t * P:(t + 1) * P],
                                                ws[n][:, h, :], start=(h == 0), stop=(h == 1))
                    ins.then_inc(projected, 1)

        @block.vector
        def _(dve):
            dve.sem_inc(taken, PAIRS)
            dve.sem_inc(kv_ready, BANKS)
            OPS = 18 * PAIRS
            Chain(dve, chain).then(dve.memset(eps[:], LN_EPS))
            dve.wait_ge(consts, 16 * 8)
            for it in passes(dve, NODE_PASSES):
                ch = Chain(dve, chain, it * OPS + 1)
                for b in B:
                    m = it * PAIRS + b
                    dve.wait_ge(landed[b], (it + 1) * (16 * (GROUP + 1)))
                    ch.then(dve.tensor_tensor(flat(y[b][:]), flat(sums[b][:, 0]), flat(sums[b][:, 1]), ALU.add))
                    dve.wait_ge(halved, m + 1)
                    ch.then(dve.tensor_tensor(flat(y[b][:]), flat(y[b][:]), flat(sums[b][:, 2]), ALU.add))
                    ch.then(dve.tensor_tensor(y[b][:], y[b][:], over_tiles(rows4[:, 0, :]), ALU.add))
                    ch.then(dve.tensor_tensor(y[b][:], y[b][:], xin[b][:], ALU.add))
                    dve.sem_inc(taken, 1)
                    norm_stats(dve, ch, y[b], stats[b], mean_var[b], var_ready)
                for b in B:
                    dve.wait_ge(std_ready, it * 2 * PAIRS + b + 1)
                    wait_if_any(dve, stored[b], it * 16)
                    norm_apply(dve, ch, out[b], y[b], mean_var[b], std[b])
                    dve.sem_inc(out_ready, 1)
                    norm_stats(dve, ch, out[b], stats[b], mean_var[b], var_ready)
                for b in B:
                    dve.wait_ge(std_ready, (it * 2 + 1) * PAIRS + b + 1)
                    norm_apply(dve, ch, xn[b], out[b], mean_var[b], std[b])
                    ch.then(dve.tensor_tensor(xn[b][:], xn[b][:], over_tiles(rows4[:, 1, :]), ALU.mult))
                    ch.then(dve.tensor_tensor(xn[b][:], xn[b][:], over_tiles(rows4[:, 2, :]), ALU.add))
                    dve.sem_inc(xn_ready, 1)
                for b in B:
                    m = it * PAIRS + b
                    dve.wait_ge(projected, m + 1)
                    wait_if_any(dve, kv_stored[b], it * 16)
                    dve.tensor_tensor(k.q[:, bass.ds(2 * m, 2), :],
                                      k.psum[:, 2 + 3 * (b % BANKS), :].rearrange("p (t d) -> p t d", t=2),
                                      over_tiles(rows4[:, 3, :]), ALU.add)
                    dve.tensor_tensor(kv[b][:], k.psum[:, 3 + 3 * (b % BANKS):5 + 3 * (b % BANKS), :],
                                      bkv_row[:].unsqueeze(1).to_broadcast([P, 2, 2 * D]),
                                      ALU.add).then_inc(kv_ready, 1)
                assert ch.n == OPS, ch.n


def att_scores(nc, k, edge_attr, we):
    H = 8
    DH = D // H
    EK = 65
    with ExitStack() as ctx:
        def sb(name, shape, dt=F32):
            return ctx.enter_context(nc.sbuf_tensor(name, shape, dt))

        sem = ctx.enter_context(semaphores(nc))

        we_sb = sb("s3_we", [EK, DH])
        idx = [sb(f"s3_idx{q}", [P, GROUP], I32) for q in range(RING)]
        rows = [sb(f"s3_rows{q}", [P, GROUP, 2 * D]) for q in range(RING)]
        drow = [sb(f"s3_drow{q}", [P, GROUP * P]) for q in range(RING)]
        feat = [sb(f"s3_feat{q}", [EK, GROUP, P]) for q in range(RING)]
        spread = [sb(f"s3_spread{b}", [P, GROUP * P]) for b in range(2)]
        dots = [sb(f"s3_dots{b}", [P, GROUP, D]) for b in range(2)]
        consts = sem("s3_consts")
        gathered = [sem(f"s3_gathered{q}") for q in range(RING)]
        drow_landed = [sem(f"s3_drow_landed{q}") for q in range(RING)]
        feat_landed = [sem(f"s3_feat_landed{q}") for q in range(RING)]
        spilled = [sem(f"s3_spilled{q}") for q in range(RING)]
        ones_ready, idx_ready, passed, spread_ready, looked_up, added, reduced, chain = (
            sem(f"s3_{n}") for n in ("ones_ready", "idx_ready", "passed", "spread_ready", "looked_up", "added",
                                     "reduced", "chain"))
        block = ctx.enter_context(nc.Block())
        dloc_rows = k.rows_dloc.rearrange("(o s) l -> o (s l)", o=1)
        spill_rows = k.spill.rearrange("s p d -> p s d")

        @block.scalar
        def _(act):
            for it in passes(act, PASSES):
                for q in range(RING):
                    g = it * RING + q
                    wait_if_any(act, gathered[q], it * (16 * GROUP))
                    act.copy(idx[q][:], k.src_idx[:, bass.ds(g * GROUP, GROUP)]).then_inc(idx_ready, 1)
                    act.wait_ge(spread_ready, g + 1)
                    act.dma_start(drow[q][:], dloc_rows[:, bass.ds(g * (GROUP * P), GROUP * P)]
                                  .partition_broadcast(P)).then_inc(drow_landed[q], 16)

        @block.gpsimd
        def _(pool):
            for q in range(RING):
                ins = pool.memset(feat[q][EK - 1:EK, :, :], 1.0)
            ins.then_inc(ones_ready, 1)
            for it in passes(pool, PASSES):
                for q in range(RING):
                    g = it * RING + q
                    pool.wait_ge(idx_ready, g + 1)
                    pool.wait_ge(added, g + 1)
                    wait_if_any(pool, spilled[q], it * 16)
                    pool.sem_inc(passed, 1)
                    for s in range(GROUP):
                        pool.indirect_dma_start(rows[q][:, s, :], None, k.kv,
                                                bass.IndirectOffsetOnAxis(ap=idx[q][:, s:s + 1], axis=0)
                                                ).then_inc(gathered[q], 16)

        @block.sync
        def _(sp):
            sp.dma_start(we_sb[:], we).then_inc(consts, 16)

            def load_group(it, q):
                g = it * RING + q
                sp.wait_ge(looked_up, g + 1)
                regs = load_indices(nc, sp, k.step_i, g * GROUP, GROUP, EA_TILES - 1)
                for s in range(GROUP):
                    sp.dma_start(feat[q][0:EK - 1, s, :], edge_attr[:, bass.ds(regs[s] * P, P)]
                                 ).then_inc(feat_landed[q], 16)

            def spill_group(it, q, _):
                g = it * RING + q
                sp.wait_ge(gathered[q], (it + 1) * (16 * GROUP))
                sp.dma_start(spill_rows[:, bass.ds(g * GROUP, GROUP), :], rows[q][:, :, D:2 * D]
                             ).then_inc(spilled[q], 16)

            one_ahead(sp, nc, None, None, load_group, spill_group)
            for q in range(RING):
                sp.wait_ge(spilled[q], 16 * PASSES)

        @block.tensor
        def _(pe):
            pe.sem_inc(looked_up, 2)
            pe.wait_ge(consts, 16)
            pe.wait_ge(ones_ready, 1)
            for it in passes(pe, PASSES):
                j = load_indices(nc, pe, k.step_j, it * (RING * GROUP), RING * GROUP, NODE_TILES - 1)
                for q in range(RING):
                    g = it * RING + q
                    b = q % 2
                    pe.wait_ge(spread_ready, g + 1 + RING)
                    pe.wait_ge(feat_landed[q], (it + 1) * (16 * GROUP))
                    pe.wait_ge(reduced, g + 1)
                    for s in range(GROUP):
                        pe.matmul(k.psum[:, 4 + b, s * DH:(s + 1) * DH], feat[q][:, s, :], we_sb[:],
                                  start=True, stop=True)
                        ins = pe.matmul(k.psum[:, 2 * b + s // 2, (s % 2) * D:(s % 2 + 1) * D],
                                        spread[b][:, s * P:(s + 1) * P],
                                        k.q[:, bass.ds(j[q * GROUP + s], 1), :].rearrange("p o d -> p (o d)"),
                                        start=True, stop=True)
                    ins.then_inc(looked_up, 1)

        @block.vector
        def _(dve):
            dve.sem_inc(spread_ready, RING)
            dve.sem_inc(added, RING)
            dve.sem_inc(reduced, 2)

            def spread_group(it, q):
                g = it * RING + q
                dve.wait_ge(drow_landed[q], (it + 1) * 16)
                dve.wait_ge(looked_up, g + 1)
                dve.tensor_scalar(spread[q % 2][:], drow[q][:], k.lane[:, 0:1], None, ALU.is_equal
                                  ).then_inc(spread_ready, 1)

            def dot_group(it, q, _):
                g = it * RING + q
                b = q % 2
                dve.wait_ge(looked_up, g + 1 + 2)
                dve.wait_ge(gathered[q], (it + 1) * (16 * GROUP))
                for s in range(GROUP):
                    ep = k.psum[:, 4 + b, s * DH:(s + 1) * DH]
                    ins = dve.tensor_tensor(dots[b][:, s, :].rearrange("p (h c) -> p h c", h=H),
                                            rows[q][:, s, 0:D].rearrange("p (h c) -> p h c", h=H),
                                            ep.unsqueeze(1).to_broadcast([P, H, DH]), ALU.add)
                ins.then_inc(added, 1)
                dve.wait_ge(added, g + 1 + RING)
                dve.tensor_tensor(flat(dots[b][:]), flat(dots[b][:]), flat(k.psum[:, 2 * b:2 * b + 2, :]),
                                  ALU.mult).then_inc(chain, 1)
                dve.wait_ge(chain, g + 1)
                dve.tensor_reduce(k.logits[:, bass.ds(g * GROUP, GROUP), 0:H],
                                  dots[b][:].rearrange("p s (h c) -> p s h c", h=H), AX.X, ALU.add
                                  ).then_inc(reduced, 1)

            one_ahead(dve, nc, None, None, spread_group, dot_group)


def att_nodes(nc, k, wo, w1, w2, b1, rows, mixes, out_dram):
    H = 8
    FF = 1024
    NF = FF // P
    with ExitStack() as ctx:
        def sb(name, shape, dt=F32):
            return ctx.enter_context(nc.sbuf_tensor(name, shape, dt))

        sem = ctx.enter_context(semaphores(nc))

        B = range(PAIRS)
        wo_sb, w1_sb, w2_sb = sb("n4_wo", [P, 2, D]), sb("n4_w1", [P, 2, FF]), sb("n4_w2", [P, NF, D])
        b1_col, rows4, mix_col = sb("n4_b1", [P, NF]), sb("n4_rows", [P, 4, D]), sb("n4_mix", [P, 2])
        eps = sb("n4_eps", [P, 1])
        share = sb("n4_share", [P, NT, H])
        xin = [sb(f"n4_x{b}", [P, 2, D]) for b in B]
        y = [sb(f"n4_y{b}", [P, 2, D]) for b in B]
        x4 = [sb(f"n4_x4{b}", [P, 2, D]) for b in B]
        out = [sb(f"n4_out{b}", [P, 2, D]) for b in B]
        turned_sb = [sb(f"n4_turned{b}", [P, 2, 2 * P]) for b in B]
        hidden = [sb(f"n4_hidden{c}", [P, NF, 2 * P]) for c in range(BANKS)]
        stats = [sb(f"n4_stats{b}", [P, 2, 6]) for b in B]
        mean_var = [sb(f"n4_mv{b}", [P, 2, 2]) for b in B]
        std = [sb(f"n4_std{b}", [P, 2]) for b in B]
        consts = sem("n4_consts")
        landed = [sem(f"n4_landed{b}") for b in B]
        stored = [sem(f"n4_stored{b}") for b in B]
        (avg_ready, turned, copied, projected, var_ready, std_ready, xn_ready, half_done, half_ready, ff_done,
         taken, out_ready, chain) = (sem(f"n4_{n}") for n in (
             "avg_ready", "turned", "copied", "projected", "var_ready", "std_ready", "xn_ready", "half_done",
             "half_ready", "ff_done", "taken", "out_ready", "chain"))
        rows_read = sem("n4_rows_read")
        block = ctx.enter_context(nc.Block())
        NCONST = 3 + 1 + 4 + 1

        @block.sync
        def _(sp):
            sp.dma_start(wo_sb[:], wo.rearrange("(h p) n -> p h n", p=P)).then_inc(consts, 16)
            sp.dma_start(w1_sb[:], w1.rearrange("(h p) n -> p h n", p=P)).then_inc(consts, 16)
            sp.dma_start(w2_sb[:], w2.rearrange("(h p) n -> p h n", p=P)).then_inc(consts, 16)
            sp.dma_start(b1_col[:], b1).then_inc(consts, 16)
            for n in range(4):
                sp.dma_start(rows4[:, n, :], rows[n:n + 1, :].partition_broadcast(P)).then_inc(consts, 16)
            sp.dma_start(mix_col[:], mixes.partition_broadcast(P)).then_inc(consts, 16)
            for it in passes(sp, NODE_PASSES):
                for b in B:
                    m = it * PAIRS + b
                    sp.wait_ge(taken, m + 1)
                    sp.dma_start(xin[b][:], pair(k.x3, m)).then_inc(landed[b], 16)

        @block.gpsimd
        def _(pool):
            for it in passes(pool, NODE_PASSES):
                for b in B:
                    m = it * PAIRS + b
                    pool.wait_ge(out_ready, m + 1)
                    pool.dma_start(pair(out_dram, m), out[b][:]).then_inc(stored[b], 16)
            for b in B:
                pool.wait_ge(stored[b], 16 * NODE_PASSES)

        @block.scalar
        def _(act):
            act.sem_inc(copied, BANKS)
            act.wait_ge(consts, 16 * NCONST)
            for it in passes(act, NODE_PASSES):
                def copy_turned(n):
                    for b in B:
                        act.wait_ge(turned, (it * 2 + n) * PAIRS + b + 1)
                        act.copy(flat(turned_sb[b][:]), k.psum[:, b % BANKS, :]).then_inc(copied, 1)

                def root(n):
                    for b in B:
                        act.wait_ge(var_ready, (it * 2 + n) * PAIRS + b + 1)
                        act.activation(std[b][:], mean_var[b][:, :, 1], ACT.Sqrt, bias=eps[:, 0:1]
                                       ).then_inc(std_ready, 1)

                copy_turned(0)
                root(0)
                copy_turned(1)
                for b in B:
                    act.wait_ge(ff_done, bank_free(it * PAIRS + b, b))
                    for half in range(2):
                        act.wait_ge(half_done, (it * PAIRS + b) * 2 + half + 1)
                        for f in range(NF // 2):
                            n = half * (NF // 2) + f
                            ins = act.activation(hidden[b % BANKS][:, n, :],
                                                 k.psum[:, 4 + 2 * half + f // 2, (f % 2) * D:(f % 2 + 1) * D],
                                                 ACT.Gelu, bias=b1_col[:, n:n + 1])
                        ins.then_inc(half_ready, 1)
                root(1)

        @block.tensor
        def _(pe):
            pe.sem_inc(ff_done, BANKS)
            pe.wait_ge(consts, 16 * NCONST)
            for it in passes(pe, NODE_PASSES):
                def half_hidden(b, half):
                    m = it * PAIRS + b
                    wait_if_any(pe, half_ready, m * 2 + half)
                    for f in range(NF // 2):
                        n = half * (NF // 2) + f
                        for h in range(2):
                            ins = pe.matmul(k.psum[:, 4 + 2 * half + f // 2, (f % 2) * D:(f % 2 + 1) * D],
                                            w1_sb[:, h, n * P:(n + 1) * P], turned_sb[b][:, h, :],
                                            start=(h == 0), stop=(h == 1))
                    ins.then_inc(half_done, 1)

                def ff_rows(b):
                    m = it * PAIRS + b
                    pe.wait_ge(half_ready, (m + 1) * 2)
                    pe.wait_ge(rows_read, bank_free((it * 2 + 1) * PAIRS + b, b))
                    for t in range(2):
                        for n in range(NF):
                            ins = pe.matmul(k.psum[:, 2 + b % BANKS, t * D:(t + 1) * D],
                                            hidden[b % BANKS][:, n, t * P:(t + 1) * P],
                                            w2_sb[:, n, :], start=(n == 0), stop=(n == NF - 1))
                    ins.then_inc(ff_done, 1)

                for b in B:
                    pe.wait_ge(avg_ready, it * PAIRS + b + 1)
                    pe.wait_ge(copied, bank_free(it * 2 * PAIRS + b, b))
                    turn_pair(pe, k.psum[:, b % BANKS], y[b], k.ident[:]).then_inc(turned, 1)
                for b in B:
                    pe.wait_ge(copied, it * 2 * PAIRS + b + 1 + BANKS)
                    pe.wait_ge(rows_read, bank_free(it * 2 * PAIRS + b, b))
                    for t in range(2):
                        for h in range(2):
                            ins = pe.matmul(k.psum[:, 2 + b % BANKS, t * D:(t + 1) * D],
                                            turned_sb[b][:, h, t * P:(t + 1) * P],
                                            wo_sb[:, h, :], start=(h == 0), stop=(h == 1))
                    ins.then_inc(projected, 1)
                for b in B:
                    pe.wait_ge(xn_ready, it * PAIRS + b + 1)
                    pe.wait_ge(copied, bank_free((it * 2 + 1) * PAIRS + b, b))
                    turn_pair(pe, k.psum[:, b % BANKS], y[b], k.ident[:]).then_inc(turned, 1)
                for b in B:
                    pe.wait_ge(copied, (it * 2 + 1) * PAIRS + b + 1 + BANKS)
                    for half in range(2):
                        half_hidden(b, half)
                    if b > 0:
                        ff_rows(b - 1)
                ff_rows(PAIRS - 1)

        @block.vector
        def _(dve):
            dve.sem_inc(taken, PAIRS)
            dve.sem_inc(rows_read, BANKS)
            FIRST = 4
            OPS = 19 * PAIRS
            ch = Chain(dve, chain)
            ch.tick(dve.memset(eps[:], LN_EPS))
            ch.then(dve.memset(k.acc[:, NODE_TILES:NT, :], 0.0))
            ch.then(dve.tensor_scalar(share[:], k.acc[:, :, D:D + H], 1e-30, None, ALU.max))
            ch.then(dve.reciprocal(share[:], share[:]))
            dve.wait_ge(consts, 16 * NCONST)
            assert ch.n == FIRST
            for it in passes(dve, NODE_PASSES):
                ch = Chain(dve, chain, it * OPS + FIRST)
                for b in B:
                    m = it * PAIRS + b
                    for t in range(2):
                        w = share[:, bass.ds(2 * m + t, 1), :].rearrange("p o h -> p (o h)")
                        ins = dve.tensor_tensor(
                            y[b][:, t].rearrange("p (h c) -> p h c", h=H),
                            k.acc[:, bass.ds(2 * m + t, 1), 0:D].rearrange("p o (h c) -> p (o h) c", h=H),
                            w.unsqueeze(2).to_broadcast([P, H, D // H]), ALU.mult)
                    ins.then_inc(avg_ready, 1)
                for b in B:
                    m = it * PAIRS + b
                    dve.wait_ge(projected, m + 1)
                    p = k.psum[:, 2 + b % BANKS, :].rearrange("p (t d) -> p t d", t=2)
                    ch.then(dve.tensor_tensor(x4[b][:], p, over_tiles(rows4[:, 0, :]), ALU.add))
                    dve.sem_inc(rows_read, 1)
                    dve.wait_ge(landed[b], (it + 1) * 16)
                    ch.then(dve.scalar_tensor_tensor(out=x4[b][:], in0=x4[b][:], scalar=mix_col[:, 0:1],
                                                     in1=xin[b][:], op0=ALU.mult, op1=ALU.add))
                    norm_stats(dve, ch, x4[b], stats[b], mean_var[b], var_ready)
                for b in B:
                    dve.wait_ge(std_ready, it * 2 * PAIRS + b + 1)
                    norm_apply(dve, ch, y[b], x4[b], mean_var[b], std[b])
                    ch.then(dve.tensor_tensor(y[b][:], y[b][:], over_tiles(rows4[:, 1, :]), ALU.mult))
                    ch.then(dve.tensor_tensor(y[b][:], y[b][:], over_tiles(rows4[:, 2, :]), ALU.add))
                    dve.sem_inc(xn_ready, 1)
                for b in B:
                    m = it * PAIRS + b
                    dve.wait_ge(ff_done, m + 1 + BANKS)
                    p = k.psum[:, 2 + b % BANKS, :].rearrange("p (t d) -> p t d", t=2)
                    ch.then(dve.tensor_tensor(y[b][:], p, over_tiles(rows4[:, 3, :]), ALU.add))
                    dve.sem_inc(rows_read, 1)
                    ch.then(dve.scalar_tensor_tensor(out=y[b][:], in0=y[b][:], scalar=mix_col[:, 1:2],
                                                     in1=x4[b][:], op0=ALU.mult, op1=ALU.add))
                    ch.then(dve.tensor_tensor(y[b][:], y[b][:], xin[b][:], ALU.add))
                    dve.sem_inc(taken, 1)
                    norm_stats(dve, ch, y[b], stats[b], mean_var[b], var_ready)
                for b in B:
                    dve.wait_ge(std_ready, (it * 2 + 1) * PAIRS + b + 1)
                    wait_if_any(dve, stored[b], it * 16)
                    norm_apply(dve, ch, out[b], y[b], mean_var[b], std[b])
                    dve.sem_inc(out_ready, 1)
                assert ch.n == OPS, ch.n


def build(nc, a, out):
    with ExitStack() as ctx:
        def scope(name, shape):
            return nc.sbuf_tensor(name, shape, F32)

        k = allocate(nc, ctx)
        prepare(nc, k, a["src"], a["dst"], a["weight"])
        with scope("att", [P, NT, 8]) as k.att, scope("acc0", [P, NT, D + 12]) as k.acc:
            gat_nodes(nc, k, a["x"], a["l0_w"], a["l0_att_src"], a["l0_att_dst"])
            with scope("aux0", [P, STEPS, 12]) as k.aux:
                with scope("logits0", [P, STEPS, 4]) as k.logits:
                    gat_scores(nc, k)
                    turn_logits(nc, k, 4)
                softmax(nc, k, 4, None, True)
                attend(nc, k, 4, 3)
            gat_finish(nc, k, a["x"], a["l0_bias"], a["l0_slope"])
        with scope("support", [P, NT, D]) as k.support:
            with scope("acc1", [P, NT, D]) as k.acc:
                gin_edges(nc, k, a["edge_attr"])
                gin_nodes(nc, k, a["l1_w1"], a["l1_b1"], a["l1_w2"], a["l1_b2"], a["l1_gamma"], a["l1_beta"], a["l2_w"])
            gcn_edges(nc, k)
        with scope("q", [P, NT, D]) as k.q:
            gcn_nodes(nc, k, a["l2_b"], a["l3_ln1_g"], a["l3_ln1_b"], a["l3_wq"], a["l3_wk"], a["l3_wv"], a["l3_bq"], a["l3_bkv"])
            with scope("logits3", [P, STEPS, 8]) as k.logits:
                att_scores(nc, k, a["edge_feat"], a["l3_we"])
                turn_logits(nc, k, 8)
        with scope("aux3", [P, STEPS, 8]) as k.aux:
            softmax(nc, k, 8, float(D // 8) ** -0.5, False)
            with scope("acc3", [P, NT, D + 8]) as k.acc:
                attend(nc, k, 8, 1)
                att_nodes(nc, k, a["l3_wo"], a["l3_w1"], a["l3_w2"], a["l3_b1"], a["l3_rows"], a["l3_mixes"],
                          out)


def padded(array, rows, value):
    out = np.full((rows, *array.shape[1:]), value, array.dtype)
    out[:array.shape[0]] = array
    return out


def layout(i):
    def index(name, value):
        return padded(i[name], IDX_ROWS * P, value).reshape(IDX_ROWS, P)

    def row(name):
        return i[name].reshape(1, -1)

    def column(name):
        return np.ascontiguousarray(i[name].reshape(-1, P).T)

    return {
        "x": padded(i["x"], NP, 0), "src": index("src", 0), "dst": index("dst", DST_PAD),
        "weight": index("edge_weight", 0), "edge_attr": padded(i["edge_attr_256"], EA_TILES * P, 0),
        "edge_feat": np.ascontiguousarray(padded(i["edge_attr_64"], EA_TILES * P, 0).T),
        "l0_w": i["L0_gnn_W"], "l0_att_src": row("L0_gnn_att_src"), "l0_att_dst": row("L0_gnn_att_dst"),
        "l0_bias": row("L0_gnn_bias"), "l0_slope": row("L0_gnn_prelu_a"),
        "l1_w1": i["L1_gnn_W1"], "l1_b1": column("L1_gnn_b1"), "l1_w2": i["L1_gnn_W2"], "l1_b2": row("L1_gnn_b2"),
        "l1_gamma": row("L1_gnn_gamma"), "l1_beta": row("L1_gnn_beta"),
        "l2_w": i["L2_gnn_W"], "l2_b": row("L2_gnn_b"),
        "l3_ln1_g": row("L3_gnn_ln1_g"), "l3_ln1_b": row("L3_gnn_ln1_b"),
        "l3_wq": i["L3_gnn_Wq"], "l3_wk": i["L3_gnn_Wk"], "l3_wv": i["L3_gnn_Wv"], "l3_bq": row("L3_gnn_bq"),
        "l3_bkv": np.concatenate([row("L3_gnn_bk"), row("L3_gnn_bv")], 1),
        "l3_we": np.concatenate([i["L3_gnn_We"], row("L3_gnn_be")], 0),
        "l3_wo": i["L3_gnn_Wo"], "l3_w1": i["L3_gnn_W1"], "l3_w2": i["L3_gnn_W2"], "l3_b1": column("L3_gnn_b1"),
        "l3_rows": np.concatenate([row(f"L3_gnn_{n}") for n in ("bo", "ln2_g", "ln2_b", "b2")], 0),
        "l3_mixes": np.concatenate([row("L3_gnn_alpha"), row("L3_gnn_beta")], 1),
    }


def kernel(**inputs):
    import concourse.bacc as bacc
    from concourse.bass_utils import run_bass_kernel_spmd

    arrays = layout({name: np.asarray(a) for name, a in inputs.items()})
    nc = bacc.Bacc("TRN2", target_bir_lowering=False, num_devices=1)
    a = {name: nc.dram_tensor(f"in_{name}", v.shape, mybir.dt.from_np(v.dtype),
                                kind="ExternalInput").ap() for name, v in arrays.items()}
    out = nc.dram_tensor("out_x", (NP, D), F32, kind="ExternalOutput").ap()
    build(nc, a, out)
    r = run_bass_kernel_spmd(nc, [{f"in_{name}": v for name, v in arrays.items()}], core_ids=[0])
    return r.results[0]["out_x"][:N]
```

```python
import numpy as np
from contextlib import ExitStack, contextmanager

import concourse.bass as bass
from concourse import mybir

F32 = mybir.dt.float32
I32 = mybir.dt.int32
BF16 = mybir.dt.bfloat16
ALU = mybir.AluOpType
ACT = mybir.ActivationFunctionType
AX = mybir.AxisListType

P = 128
N = 6250
E = 100000
D = 256
NODE_TILES = -(-N // P)
EDGE_TILES = -(-E // P)
NT = 50
NP = NT * P
SPARE_ROW = NODE_TILES * P
GROUP = 4
RING = 4
STEPS = -(-(EDGE_TILES + NODE_TILES - 1) // (GROUP * RING)) * GROUP * RING
PASSES = STEPS // (GROUP * RING)
SEL_TILES = 7
IDX_ROWS = SEL_TILES * P
EA_TILES = STEPS - (NODE_TILES - 1)
DST_PAD = 64 * P
SLOTS = STEPS * P
HALF = STEPS // 2
BIG = 1.0e30
LN_EPS = 1e-5


@contextmanager
def semaphores(nc):
    held = []

    def sem(name):
        held.append(nc.alloc_semaphore(name=name))
        return held[-1]

    yield sem
    nc.all_engine_barrier()
    nc.clear_and_free_semaphores(held)
    nc.all_engine_barrier()


class Chain:

    def __init__(self, eng, sem, base=0):
        self.eng, self.sem, self.base, self.n = eng, sem, base, 0

    def tick(self, ins):
        ins.then_inc(self.sem, 1)
        self.n += 1
        return ins

    def wait(self):
        self.eng.wait_ge(self.sem, self.base + self.n)

    def then(self, ins):
        self.tick(ins)
        self.wait()


def passes(eng, count):
    yield 0
    with eng.Fori(1, count) as it:
        yield it


def wait_if_any(eng, sem, count):
    if not isinstance(count, int) or count > 0:
        eng.wait_ge(sem, count)


def one_ahead(eng, nc, table, top, ahead, now, depth=1):
    def one_pass(it, last):
        steps = None
        if table is not None:
            steps = load_indices(nc, eng, table, it * (RING * GROUP), RING * GROUP, top)
        for q in range(RING):
            if q + depth < RING:
                ahead(it, q + depth)
            elif not last:
                ahead(it + 1, q + depth - RING)
            now(it, q, steps)

    for q in range(depth):
        ahead(0, q)
    one_pass(0, False)
    with eng.Fori(1, PASSES - 1) as it:
        one_pass(it, False)
    one_pass(PASSES - 1, True)


def step_ahead(eng, nc, table, top, ahead, now):
    def one_pass(it, last):
        entries = load_indices(nc, eng, table, it * (RING * GROUP), RING * GROUP, top)
        for q in range(RING):
            for s in range(GROUP):
                now(it, q, s, entries[q * GROUP + s])
                if q + 2 < RING:
                    ahead(it, q + 2, s)
                elif not last:
                    ahead(it + 1, q + 2 - RING, s)

    for q in range(2):
        for s in range(GROUP):
            ahead(0, q, s)
    one_pass(0, False)
    with eng.Fori(1, PASSES - 1) as it:
        one_pass(it, False)
    one_pass(PASSES - 1, True)


def load_indices(nc, eng, row, at, count, top):
    _, values = nc.values_load_multi_w_load_instructions(
        row[0:1, bass.ds(at, count)], engines=[eng.engine], min_val=0, max_val=top,
        skip_runtime_bounds_check_because="step tables are built in range by prepare()")
    return values


class Shared:
    pass


def allocate(nc, ctx):
    k = Shared()

    def sb(name, shape, dt=F32):
        return ctx.enter_context(nc.sbuf_tensor(name, shape, dt))

    def dram(name, shape, dt=F32):
        return nc.dram_tensor(name, shape, dt, kind="Internal").ap()

    k.lane = sb("lane", [P, 1])
    k.iota = sb("iota", [P, P])
    k.ident = sb("ident", [P, P])
    k.src_idx = sb("src_idx", [P, STEPS], I32)
    k.src = sb("src_f", [P, STEPS])
    k.dloc = sb("dloc", [P, STEPS])
    k.keep = sb("keep", [P, STEPS])
    k.weight = sb("weight", [P, STEPS])
    k.step_j = sb("step_j", [1, STEPS], I32)
    k.step_i = sb("step_i", [1, STEPS], I32)
    k.psum = ctx.enter_context(nc.psum_tensor("psum", [P, 8, 512], F32))

    k.ones16 = sb("ones16", [1, P], BF16)
    k.rows_src = dram("rows_src", (STEPS, P))
    k.rows_key = dram("rows_key", (STEPS + 2, P))
    k.rows_mask = dram("rows_mask", (STEPS, P))
    k.rows_dloc = dram("rows_dloc", (STEPS, P), BF16)
    k.rows_weight = dram("rows_weight", (STEPS, P))
    k.hrow = dram("hrow", (NP, 260))
    k.spill = dram("spill", (STEPS, P, D))
    k.scores = dram("scores", (STEPS * 8, P))
    k.alphas = dram("alphas", (3, STEPS * 8, P))
    k.x1 = dram("x1", (NP, D))
    k.x2 = dram("x2", (NP, D))
    k.x3 = dram("x3", (NP, D))
    k.kv = dram("kv", (NP, 2 * D))
    k.gcn = [dram(f"gcn{a}", (NP, D)) for a in range(GROUP)]
    return k


def prepare(nc, k, src, dst, weight):
    with ExitStack() as ctx:
        def sb(name, shape, dt=F32):
            return ctx.enter_context(nc.sbuf_tensor(name, shape, dt))

        sem = ctx.enter_context(semaphores(nc))

        raw = sb("p_raw", [P, 2, SEL_TILES, P], I32)
        tiles = sb("p_tiles", [P, SEL_TILES, 3, P])
        step_i32 = sb("p_step_i32", [P, STEPS], I32)
        lane_i32 = sb("p_lane_i32", [P, 1], I32)
        step = sb("p_step", [P, STEPS])
        ones = sb("p_ones", [P, P])
        bound = sb("p_bound", [P, NODE_TILES])
        below = sb("p_below", [P, SEL_TILES, NODE_TILES])
        last = sb("p_last", [NODE_TILES, 1])
        left = sb("p_left", [NODE_TILES, STEPS])
        jrow = sb("p_jrow", [P, STEPS])
        irow = sb("p_irow", [P, STEPS])
        jcol = sb("p_jcol", [P, SEL_TILES])
        lanes = sb("p_lanes", [P, SEL_TILES])
        select = sb("p_select", [P, SEL_TILES, STEPS])
        rowbuf = sb("p_rowbuf", [P, SEL_TILES, 3, P])
        dlocbuf = sb("p_dlocbuf", [P, SEL_TILES, P])
        dloc16 = sb("p_dloc16", [P, SEL_TILES, P], BF16)
        mask = sb("p_mask", [P, SEL_TILES, P])
        above = sb("p_above", [P, SEL_TILES, P])
        halo = sb("p_halo", [1, 2, P])
        zero = sb("p_zero", [P, NT // 2, D])
        ps = k.psum

        iotas, loaded, dve_done = sem("p_iotas"), sem("p_loaded"), sem("p_dve")
        below_ready, count_ready = sem("p_below_ready"), sem("p_count_ready")
        left_ready, j_ready = sem("p_left_ready"), sem("p_j_ready")
        select_ready, slots_ready = sem("p_select_ready"), sem("p_slots_ready")
        rows_ready, rows_out, stored = sem("p_rows_ready"), sem("p_rows_out"), sem("p_stored")
        mask_ready, zeroed, zero_out = sem("p_mask_ready"), sem("p_zeroed"), sem("p_zero_out")
        block = ctx.enter_context(nc.Block())
        NOPEN = NODE_TILES - 1
        LAST_ROWS = STEPS - (SEL_TILES - 1) * P

        @block.sync
        def _(sp):
            sp.dma_start(raw[:, 0], src.rearrange("(c p) l -> p c l", p=P)).then_inc(loaded, 16)
            sp.dma_start(raw[:, 1], dst.rearrange("(c p) l -> p c l", p=P)).then_inc(loaded, 16)
            sp.dma_start(tiles[:, :, 2, :], weight.rearrange("(c p) l -> p c l", p=P)).then_inc(loaded, 16)
            n = 0
            for c in range(SEL_TILES):
                rows = P if c < SEL_TILES - 1 else LAST_ROWS
                sp.wait_ge(rows_out, c + 1)
                for to, at, rows_of in ((k.rows_src, c * P, rowbuf[0:rows, c, 0, :]),
                                        (k.rows_key, c * P + 1, rowbuf[0:rows, c, 1, :]),
                                        (k.rows_weight, c * P, rowbuf[0:rows, c, 2, :])):
                    sp.dma_start(to[at:at + rows, :], rows_of).then_inc(stored, 16)
                    n += 16
            sp.wait_ge(mask_ready, 1)
            whole = (SEL_TILES - 1) * P
            for to, rows_of in ((k.rows_dloc, dloc16), (k.rows_mask, mask)):
                sp.dma_start(to[0:whole, :].rearrange("(c p) l -> p c l", p=P), rows_of[:, 0:SEL_TILES - 1, :]
                             ).then_inc(stored, 16)
                sp.dma_start(to[whole:STEPS, :], rows_of[0:LAST_ROWS, SEL_TILES - 1, :]).then_inc(stored, 16)
                n += 32
            sp.dma_start(k.rows_key[0:1, :], halo[0:1, 0, :]).then_inc(stored, 16)
            sp.dma_start(k.rows_key[STEPS + 1:STEPS + 2, :], halo[0:1, 1, :]).then_inc(stored, 16)
            sp.wait_ge(stored, n + 32)

        @block.scalar
        def _(act):
            act.wait_ge(zeroed, 1)
            for table in k.gcn:
                for half in table.rearrange("(h t p) d -> h p t d", h=2, p=P):
                    act.dma_start(half, zero[:]).then_inc(zero_out, 16)
            act.wait_ge(zero_out, 16 * 2 * len(k.gcn))

        @block.gpsimd
        def _(pool):
            pool.iota(step_i32[:], pattern=[[1, STEPS]], base=0, channel_multiplier=0).then_inc(iotas, 1)
            pool.iota(lane_i32[:], pattern=[[0, 1]], base=0, channel_multiplier=1).then_inc(iotas, 1)
            pool.memset(zero[:], 0.0).then_inc(zeroed, 1)

        @block.vector
        def _(dve):
            ch = Chain(dve, dve_done)
            ch.tick(dve.memset(ones[:], 1.0))
            ch.tick(dve.memset(k.ones16[:], 1.0))
            ch.tick(dve.memset(dlocbuf[:], 0.0))
            ch.tick(dve.memset(halo[0:1, 0, :], -1.0))
            ch.tick(dve.memset(halo[0:1, 1, :], -2.0))
            ch.tick(dve.memset(k.keep[:, 0:1], 0.0))
            dve.wait_ge(iotas, 2)
            ch.tick(dve.tensor_copy(step[:], step_i32[:]))
            ch.then(dve.tensor_copy(k.lane[:], lane_i32[:]))
            ch.tick(dve.tensor_copy(k.iota[:], step[:, 0:P]))
            ch.tick(dve.tensor_scalar(bound[:], step[:, 0:NODE_TILES], float(P), float(P), ALU.mult, ALU.add))
            for c in range(SEL_TILES):
                ch.tick(dve.tensor_scalar(lanes[:, c:c + 1], k.lane[:], float(P * c), None, ALU.add))
            dve.wait_ge(loaded, 48)
            for a in range(2):
                ch.tick(dve.tensor_copy(tiles[:, :, a, :], raw[:, a]))
            ch.wait()
            ch.tick(dve.tensor_scalar(k.ident[:], k.iota[:], k.lane[:, 0:1], None, ALU.is_equal))
            for c in range(SEL_TILES):
                ins = dve.tensor_scalar(below[:, c, :], bound[:], tiles[:, c, 1, P - 1:P], None, ALU.is_gt)
            ins.then_inc(below_ready, 1)
            dve.wait_ge(count_ready, 1)
            ch.then(dve.tensor_tensor(last[:], ps[0:NODE_TILES, 0, 0:1], k.lane[0:NODE_TILES, :], ALU.add))
            dve.tensor_scalar(left[:], step[0:NODE_TILES, :], last[:, 0:1], None, ALU.is_gt).then_inc(left_ready, 1)
            dve.wait_ge(j_ready, 1)
            ch.tick(dve.tensor_copy(jrow[:, 0:HALF], ps[:, 1, 0:HALF]))
            ch.tick(dve.tensor_copy(jrow[:, HALF:STEPS], ps[:, 2, 0:HALF]))
            ch.tick(dve.tensor_scalar(jcol[:, 0:SEL_TILES - 1], ps[:, 3, 0:SEL_TILES - 1], float(P), None, ALU.mult))
            ch.tick(dve.tensor_scalar(jcol[0:LAST_ROWS, SEL_TILES - 1:SEL_TILES],
                                        ps[0:LAST_ROWS, 3, SEL_TILES - 1:SEL_TILES], float(P), None, ALU.mult))
            ch.wait()
            ch.tick(dve.tensor_copy(k.step_j[:], jrow[0:1, :]))
            ch.tick(dve.tensor_tensor(k.keep[:, 1:STEPS], jrow[:, 1:STEPS], jrow[:, 0:STEPS - 1], ALU.is_equal))
            ch.then(dve.tensor_tensor(irow[:], step[:], jrow[:], ALU.subtract))
            ch.tick(dve.tensor_copy(k.step_i[:], irow[0:1, :]))
            for c in range(SEL_TILES):
                ins = dve.tensor_scalar(select[:, c, :], irow[:], lanes[:, c:c + 1], None, ALU.is_equal)
            ins.then_inc(select_ready, 1)
            dve.wait_ge(slots_ready, 1)
            for h in range(2):
                at = slice(h * HALF, (h + 1) * HALF)
                ch.tick(dve.tensor_copy(k.src_idx[:, at], ps[:, h, 0:HALF]))
                ch.tick(dve.tensor_copy(k.src[:, at], ps[:, h, 0:HALF]))
                ch.tick(dve.scalar_tensor_tensor(out=k.dloc[:, at], in0=jrow[:, at], scalar=-float(P),
                                                   in1=ps[:, 2 + h, 0:HALF], op0=ALU.mult, op1=ALU.add))
                ch.tick(dve.tensor_copy(k.weight[:, at], ps[:, 4 + h, 0:HALF]))
            for c in range(SEL_TILES):
                rows = P if c < SEL_TILES - 1 else LAST_ROWS
                dve.wait_ge(rows_ready, c + 1)
                bank = ps[0:rows, 6 + c % 2, 0:3 * P]
                ch.tick(dve.tensor_copy(rowbuf[0:rows, c, 0:3, :], bank.rearrange("p (a l) -> p a l", a=3)))
                ch.tick(dve.tensor_scalar(dlocbuf[0:rows, c, :], bank[:, P:2 * P], jcol[0:rows, c:c + 1], None,
                                          ALU.subtract))
                ch.wait()
                dve.sem_inc(rows_out, 1)
            ch.tick(dve.tensor_copy(flat(dloc16[:]), flat(dlocbuf[:])))
            ch.tick(dve.tensor_scalar(flat(mask[:]), flat(dlocbuf[:]), 0.0, -BIG, ALU.is_lt, ALU.mult))
            ch.then(dve.tensor_scalar(flat(above[:]), flat(dlocbuf[:]), float(P - 1), -BIG, ALU.is_gt, ALU.mult))
            ch.then(dve.tensor_tensor(flat(mask[:]), flat(mask[:]), flat(above[:]), ALU.add))
            dve.sem_inc(mask_ready, 1)

        @block.tensor
        def _(pe):
            pe.wait_ge(below_ready, 1)
            for c in range(SEL_TILES):
                ins = pe.matmul(ps[0:NODE_TILES, 0, 0:1], below[:, c, :], ones[:, 0:1],
                                start=(c == 0), stop=(c == SEL_TILES - 1))
            ins.then_inc(count_ready, 1)
            pe.wait_ge(left_ready, 1)
            for h in range(2):
                pe.matmul(ps[:, 1 + h, 0:HALF], ones[0:NOPEN, :], left[0:NOPEN, h * HALF:(h + 1) * HALF],
                          start=True, stop=True)
            for c in range(SEL_TILES):
                rows = P if c < SEL_TILES - 1 else LAST_ROWS
                ins = pe.matmul(ps[0:rows, 3, c:c + 1], left[0:NOPEN, c * P:c * P + rows], ones[0:NOPEN, 0:1],
                                start=True, stop=True)
            ins.then_inc(j_ready, 1)
            pe.wait_ge(select_ready, 1)
            for a in range(3):
                for h in range(2):
                    for c in range(SEL_TILES):
                        ins = pe.matmul(ps[:, 2 * a + h, 0:HALF], tiles[:, c, a, :],
                                        select[:, c, h * HALF:(h + 1) * HALF],
                                        start=(c == 0), stop=(c == SEL_TILES - 1))
            ins.then_inc(slots_ready, 1)
            for b in range(SEL_TILES):
                rows = P if b < SEL_TILES - 1 else LAST_ROWS
                if b >= 2:
                    pe.wait_ge(rows_out, b - 1)
                for c in range(SEL_TILES):
                    ins = pe.matmul(ps[0:rows, 6 + b % 2, 0:3 * P], select[:, c, b * P:b * P + rows],
                                    tiles[:, c, :, :].rearrange("p a l -> p (a l)"),
                                    start=(c == 0), stop=(c == SEL_TILES - 1))
                ins.then_inc(rows_ready, 1)


PAIRS = 5
BANKS = 2
NODE_PASSES = NT // (2 * PAIRS)


def bank_free(n, b):
    return n + 1 + (b == 0)


def pair(table, m):
    return table.rearrange("(t p) d -> p t d", p=P)[:, bass.ds(2 * m, 2), :]


def staged(stages):
    def loop(eng):
        def one_pass(it):
            for b in range(PAIRS):
                for lag, run in stages:
                    if b >= lag:
                        if not (isinstance(it, int) and it == NODE_PASSES):
                            run(it, b - lag)
                    elif not (isinstance(it, int) and it == 0):
                        run(it - 1, b - lag + PAIRS)

        one_pass(0)
        one_pass(1)
        with eng.Fori(2, NODE_PASSES) as it:
            one_pass(it)
        one_pass(NODE_PASSES)

    return loop


def transpose_pair(pe, psum_bank, rows, ident, halves=2):
    for t in range(2):
        for h in range(halves):
            at = (t * halves + h) * P
            ins = pe.transpose(psum_bank[:, at:at + P], rows[:, t, h * P:(h + 1) * P], ident)
    return ins


def gat_nodes(nc, k, x, w, att_src, att_dst):
    with ExitStack() as ctx:
        def sb(name, shape, dt=F32):
            return ctx.enter_context(nc.sbuf_tensor(name, shape, dt))

        sem = ctx.enter_context(semaphores(nc))

        WC = D + 8
        wext = sb("n0_wext", [P, 2, WC])
        att = sb("n0_att", [P, 2, D])
        prod = sb("n0_prod", [P, 2, D])
        xin = [sb(f"n0_x{b}", [P, 2, D]) for b in range(PAIRS)]
        xt = [sb(f"n0_xt{b}", [P, 2, 2, P]) for b in range(PAIRS)]
        hout = [sb(f"n0_h{b}", [P, 2, WC]) for b in range(PAIRS)]
        w_landed, w_chain, w_ready = sem("n0_w_landed"), sem("n0_w_chain"), sem("n0_w_ready")
        x_landed = [sem(f"n0_x_landed{b}") for b in range(PAIRS)]
        turned, xt_ready = sem("n0_turned"), sem("n0_xt_ready")
        h_done, h_ready = sem("n0_h_done"), sem("n0_h_ready")
        stored = [sem(f"n0_stored{b}") for b in range(PAIRS)]
        block = ctx.enter_context(nc.Block())
        CREDIT = PAIRS

        @block.sync
        def _(sp):
            sp.dma_start(wext[:, :, 0:D], w.rearrange("(h p) n -> p h n", p=P)).then_inc(w_landed, 16)
            sp.dma_start(att[:, 0, :], att_src.partition_broadcast(P)).then_inc(w_landed, 16)
            sp.dma_start(att[:, 1, :], att_dst.partition_broadcast(P)).then_inc(w_landed, 16)
            for it in passes(sp, NODE_PASSES):
                for b in range(PAIRS):
                    m = it * PAIRS + b
                    sp.wait_ge(turned, m + 1)
                    sp.dma_start(xin[b][:], pair(x, m)).then_inc(x_landed[b], 16)

        @block.gpsimd
        def _(pool):
            for it in passes(pool, NODE_PASSES):
                for b in range(PAIRS):
                    m = it * PAIRS + b
                    pool.wait_ge(h_ready, m + 1 + BANKS)
                    pool.dma_start(pair(k.hrow, m), hout[b][:, :, 0:260]).then_inc(stored[b], 16)
            for b in range(PAIRS):
                pool.wait_ge(stored[b], 16 * NODE_PASSES)

        @block.tensor
        def _(pe):
            pe.sem_inc(turned, CREDIT)
            pe.sem_inc(h_done, CREDIT)
            pe.wait_ge(w_ready, 1)
            for it in passes(pe, NODE_PASSES):
                for b in range(PAIRS):
                    m = it * PAIRS + b
                    pe.wait_ge(x_landed[b], (it + 1) * 16)
                    pe.wait_ge(xt_ready, bank_free(m, b))
                    transpose_pair(pe, k.psum[:, b % BANKS], xin[b], k.ident[:]).then_inc(turned, 1)
                for b in range(PAIRS):
                    m = it * PAIRS + b
                    pe.wait_ge(xt_ready, m + 1 + BANKS)
                    pe.wait_ge(h_ready, bank_free(m, b))
                    for t in range(2):
                        for h in range(2):
                            ins = pe.matmul(k.psum[:, 2 + 2 * (b % BANKS) + t, 0:WC], xt[b][:, t, h, :], wext[:, h, :],
                                            start=(h == 0), stop=(h == 1))
                    ins.then_inc(h_done, 1)

        @block.scalar
        def _(act):
            act.sem_inc(xt_ready, BANKS)
            for it in passes(act, NODE_PASSES):
                for b in range(PAIRS):
                    m = it * PAIRS + b
                    act.wait_ge(turned, m + 1 + CREDIT)
                    act.wait_ge(h_done, m + 1)
                    act.copy(xt[b][:].rearrange("p t h n -> p (t h n)"), k.psum[:, b % BANKS, :]).then_inc(xt_ready, 1)

        @block.vector
        def _(dve):
            dve.sem_inc(h_ready, BANKS)
            ch = Chain(dve, w_chain)
            dve.wait_ge(w_landed, 48)
            for a in range(2):
                for h in range(2):
                    ch.then(dve.tensor_tensor(prod[:, h, :], wext[:, h, 0:D], att[:, a, :], ALU.mult))
                    ch.then(dve.tensor_reduce(wext[:, h, D + 4 * a:D + 4 * a + 4],
                                              prod[:, h, :].rearrange("p (h c) -> p h c", h=4), AX.X, ALU.add))
            dve.sem_inc(w_ready, 1)
            for it in passes(dve, NODE_PASSES):
                for b in range(PAIRS):
                    m = it * PAIRS + b
                    dve.wait_ge(h_done, m + 1 + CREDIT)
                    wait_if_any(dve, stored[b], it * 16)
                    hp = k.psum[:, 2 + 2 * (b % BANKS):4 + 2 * (b % BANKS), :]
                    dve.tensor_copy(k.att[:, bass.ds(2 * m, 2), :], hp[:, :, D:WC])
                    dve.tensor_copy(hout[b][:], hp[:, :, 0:WC]).then_inc(h_ready, 1)


def gat_scores(nc, k):
    H = 4
    with ExitStack() as ctx:
        def sb(name, shape, dt=F32):
            return ctx.enter_context(nc.sbuf_tensor(name, shape, dt))

        sem = ctx.enter_context(semaphores(nc))

        idx = [sb(f"s0_idx{q}", [P, GROUP], I32) for q in range(RING)]
        rows = [sb(f"s0_rows{q}", [P, GROUP, 260]) for q in range(RING)]
        drow = [sb(f"s0_drow{q}", [1, GROUP * P], BF16) for q in range(RING)]
        spread = [sb(f"s0_spread{b}", [P, GROUP * P]) for b in range(2)]
        idx_ready, passed = sem("s0_idx_ready"), sem("s0_passed")
        gathered = [sem(f"s0_gathered{q}") for q in range(RING)]
        drow_landed = [sem(f"s0_drow_landed{q}") for q in range(RING)]
        spilled = [sem(f"s0_spilled{q}") for q in range(RING)]
        spread_ready, looked_up, added = sem("s0_spread_ready"), sem("s0_looked_up"), sem("s0_added")
        handed_out = sem("s0_handed_out")
        block = ctx.enter_context(nc.Block())
        dloc_rows = k.rows_dloc.rearrange("(o s) l -> o (s l)", o=1)
        spill_rows = k.spill.rearrange("s p d -> p s d")

        @block.scalar
        def _(act):
            for it in passes(act, PASSES):
                for q in range(RING):
                    g = it * RING + q
                    wait_if_any(act, gathered[q], it * (16 * GROUP))
                    act.copy(idx[q][:], k.src_idx[:, bass.ds(g * GROUP, GROUP)]).then_inc(idx_ready, 1)
                    act.wait_ge(spread_ready, g + 1)
                    act.dma_start(drow[q][:], dloc_rows[:, bass.ds(g * (GROUP * P), GROUP * P)]
                                  ).then_inc(drow_landed[q], 16)

        @block.gpsimd
        def _(pool):
            for it in passes(pool, PASSES):
                for q in range(RING):
                    g = it * RING + q
                    pool.wait_ge(idx_ready, g + 1)
                    pool.wait_ge(added, g + 1)
                    wait_if_any(pool, spilled[q], it * 16)
                    pool.sem_inc(passed, 1)
                    for s in range(GROUP):
                        pool.indirect_dma_start(rows[q][:, s, :], None, k.hrow,
                                                bass.IndirectOffsetOnAxis(ap=idx[q][:, s:s + 1], axis=0)
                                                ).then_inc(gathered[q], 16)

        @block.sync
        def _(sp):
            for it in passes(sp, PASSES):
                for q in range(RING):
                    g = it * RING + q
                    sp.wait_ge(gathered[q], (it + 1) * (16 * GROUP))
                    sp.dma_start(spill_rows[:, bass.ds(g * GROUP, GROUP), :], rows[q][:, :, 0:D]
                                 ).then_inc(spilled[q], 16)
            for q in range(RING):
                sp.wait_ge(spilled[q], 16 * PASSES)

        @block.vector
        def _(dve):
            dve.sem_inc(spread_ready, RING)
            dve.sem_inc(added, RING)

            def spread_group(it, q):
                g = it * RING + q
                dve.wait_ge(handed_out, g + 1)
                dve.wait_ge(looked_up, g + 1)
                dve.tensor_scalar(spread[q % 2][:], k.psum[:, 6 + q % 2, :], k.lane[:, 0:1], None, ALU.is_equal
                                  ).then_inc(spread_ready, 1)

            def add_group(it, q, _):
                g = it * RING + q
                dve.wait_ge(looked_up, g + 1 + 2)
                dve.wait_ge(gathered[q], (it + 1) * (16 * GROUP))
                dve.tensor_tensor(k.logits[:, bass.ds(g * GROUP, GROUP), 0:H], rows[q][:, :, D:D + H],
                                  k.psum[:, q % 2, 0:GROUP * H].rearrange("p (s h) -> p s h", s=GROUP), ALU.add
                                  ).then_inc(added, 1)

            one_ahead(dve, nc, None, None, spread_group, add_group)

        @block.tensor
        def _(pe):
            pe.sem_inc(looked_up, 2)

            def hand_out(it, q):
                g = it * RING + q
                pe.wait_ge(drow_landed[q], (it + 1) * 16)
                pe.wait_ge(spread_ready, g + 1 + RING - 2)
                pe.matmul(k.psum[:, 6 + q % 2, :], k.ones16[:], drow[q][:], start=True, stop=True
                          ).then_inc(handed_out, 1)

            def look_up(it, q, j):
                g = it * RING + q
                b = q % 2
                pe.wait_ge(spread_ready, g + 1 + RING)
                pe.wait_ge(added, g + 1 + RING - 2)
                for s in range(GROUP):
                    ins = pe.matmul(k.psum[:, b, s * H:(s + 1) * H], spread[b][:, s * P:(s + 1) * P],
                                    k.att[:, bass.ds(j[q * GROUP + s], 1), 4:8]
                                    .rearrange("p o h -> p (o h)"), start=True, stop=True)
                ins.then_inc(looked_up, 1)

            one_ahead(pe, nc, k.step_j, NODE_TILES - 1, hand_out, look_up)


def block_batches(H):
    blocks = STEPS * H // P
    return [(n, min(4, blocks - n)) for n in range(0, blocks, 4)]


def block_rows(table, n, blocks):
    return table[n * P:(n + blocks) * P, :].rearrange("(b r) l -> r b l", r=P)


def turn_logits(nc, k, H):
    BLK = P // H
    batches = block_batches(H)
    with ExitStack() as ctx:
        def sb(name, shape, dt=F32):
            return ctx.enter_context(nc.sbuf_tensor(name, shape, dt))

        sem = ctx.enter_context(semaphores(nc))

        turn = [sb(f"l{H}_turn{q}", [P, 4 * P]) for q in range(RING)]
        turned, turn_ready = sem(f"l{H}_turned"), sem(f"l{H}_turn_ready")
        turn_out = [sem(f"l{H}_turn_out{q}") for q in range(RING)]
        with nc.Block() as block:
            @block.sync
            def _(sp):
                for n, (at, blocks) in enumerate(batches):
                    sp.wait_ge(turn_ready, n + 1)
                    sp.dma_start(block_rows(k.scores, at, blocks),
                                 turn[n % RING][:, 0:blocks * P].rearrange("r (b l) -> r b l", b=blocks)
                                 ).then_inc(turn_out[n % RING], 16)
                for q in range(RING):
                    sp.wait_ge(turn_out[q], 16 * len(batches[q::RING]))

            @block.vector
            def _(dve):
                for n, (_, blocks) in enumerate(batches):
                    dve.wait_ge(turned, n + 1)
                    if n >= RING:
                        dve.wait_ge(turn_out[n % RING], 16 * (n // RING))
                    dve.tensor_copy(turn[n % RING][:, 0:blocks * P], k.psum[:, n % RING, 0:blocks * P]
                                    ).then_inc(turn_ready, 1)

            @block.tensor
            def _(pe):
                for n, (at, blocks) in enumerate(batches):
                    if n >= RING:
                        pe.wait_ge(turn_ready, n + 1 - RING)
                    for b in range(blocks):
                        ins = pe.transpose(k.psum[:, n % RING, b * P:(b + 1) * P],
                                           k.logits[:, (at + b) * BLK:(at + b + 1) * BLK, 0:H]
                                           .rearrange("p s h -> p (s h)"), k.ident[:])
                    ins.then_inc(turned, 1)


def softmax(nc, k, H, scale, leaky):
    CHUNKS = P // H
    CH = STEPS // CHUNKS
    L = CH * P
    BLK = P // H
    OUTS = 3 if leaky else 1
    with ExitStack() as ctx:
        def sb(name, shape, dt=F32):
            return ctx.enter_context(nc.sbuf_tensor(name, shape, dt))

        sem = ctx.enter_context(semaphores(nc))

        logit = sb(f"m{H}_logit", [P, L])
        key = sb(f"m{H}_key", [P, L + 2])
        stop = sb(f"m{H}_stop", [P, L + 1])
        weight = sb(f"m{H}_weight", [P, L]) if scale is not None else None
        best = sb(f"m{H}_best", [P, L])
        ends = sb(f"m{H}_ends", [P, 2])
        row = sb(f"m{H}_row", [1, 2, P])
        cut = sb(f"m{H}_cut", [1, P])
        carried = sb(f"m{H}_carried", [1, P])
        carry = sb(f"m{H}_carry", [P, 1])
        batches = block_batches(H)
        turn = [sb(f"m{H}_turn{q}", [P, 4 * P]) for q in range(RING)]
        landed, key_landed, w_landed, tmp_landed = (sem(f"m{H}_{n}") for n in ("landed", "key", "w", "tmp"))
        chain, ask, got, tmp_free, w_used = (sem(f"m{H}_{n}") for n in ("chain", "ask", "got", "tmp_free", "w_used"))
        masked, flags_ready, best_ready, expo, exp_done = (
            sem(f"m{H}_{n}") for n in ("masked", "flags_ready", "best_ready", "expo", "exp_done"))
        out_done = sem(f"m{H}_out_done")
        score_rows = k.scores[0:STEPS * H, :].rearrange("(c s h) l -> h c s l", c=CHUNKS, h=H)
        alpha_rows = [k.alphas[a, 0:STEPS * H, :].rearrange("(c s h) l -> h c s l", c=CHUNKS, h=H)
                      for a in range(OUTS)]
        split = lambda t: t.rearrange("p (s l) -> p s l", l=P)
        with nc.Block() as block:
            @block.sync
            def _(sp):
                for h in range(H):
                    at = slice(h * CHUNKS, (h + 1) * CHUNKS)
                    sp.dma_start(split(logit[at, :]), score_rows[h]).then_inc(landed, 16)
                for a in range(OUTS):
                    sp.wait_ge(exp_done if a == 0 else best_ready if a == 1 else flags_ready, 1)
                    source = (best, logit, stop)[a]
                    for h in range(H):
                        at = slice(h * CHUNKS, (h + 1) * CHUNKS)
                        sp.dma_start(alpha_rows[a][h], split(source[at, 0:L])).then_inc(out_done, 16)
                sp.wait_ge(out_done, 16 * H * OUTS)

            @block.vector
            def _(dve):
                ch = Chain(dve, chain)
                dve.wait_ge(key_landed, 16 * H)
                ch.then(dve.tensor_tensor(stop[:], key[:, 1:L + 2], key[:, 0:L + 1], ALU.not_equal))
                ch.then(dve.tensor_scalar(key[:, 0:L + 1], stop[:], -BIG, None, ALU.mult))
                dve.wait_ge(landed, 16 * H)
                if leaky:
                    ch.then(dve.scalar_tensor_tensor(out=logit[:], in0=logit[:], scalar=0.2, in1=logit[:],
                                                     op0=ALU.mult, op1=ALU.max))
                if scale is not None:
                    dve.wait_ge(w_landed, 16 * H)
                    ch.then(dve.scalar_tensor_tensor(out=logit[:], in0=logit[:], scalar=scale, in1=weight[:],
                                                     op0=ALU.mult, op1=ALU.mult))
                dve.wait_ge(tmp_landed, 16 * H)
                ch.then(dve.tensor_tensor(logit[:], logit[:], best[:], ALU.add))

                def spread_max(sign, value):
                    fwd = sign > 0
                    view = (lambda t: t[:, 0:L]) if fwd else (lambda t: t[:, L - 1::-1])
                    stops = key[:, 0:L] if fwd else key[:, L:0:-1]
                    ch.tick(dve.tensor_reduce(ends[:, 1:2], key[:, 0:L] if fwd else key[:, 1:L + 1], AX.X, ALU.min))
                    ch.then(dve.tensor_tensor_scan(view(best), stops, view(value), -BIG, ALU.add, ALU.max))
                    ch.tick(dve.tensor_copy(ends[:, 0:1], best[:, L - 1:L] if fwd else best[:, 0:1]))
                    ch.wait()
                    dve.sem_inc(ask, 1)
                    n = 1 if fwd else 3
                    dve.wait_ge(got, n)
                    ch.then(dve.tensor_copy(row[:], k.psum[0:1, 0, 0:2 * P].rearrange("p (a c) -> p a c", a=2)))
                    first = slice(0, P, CHUNKS) if fwd else slice(CHUNKS - 1, P, CHUNKS)
                    ch.then(dve.memset(cut[:], 0.0))
                    ch.then(dve.memset(cut[0:1, first], -BIG))
                    ch.then(dve.memset(carried[:], -BIG))
                    ch.then(dve.tensor_tensor(row[:, 1, :], row[:, 1, :], cut[:], ALU.add))
                    rv = (lambda t: t) if fwd else (lambda t: t[0:1, ::-1])
                    out = row[0:1, 0, :]
                    ch.then(dve.tensor_tensor_scan(rv(cut[0:1, :]), rv(row[0:1, 1, :]), rv(out), -BIG, ALU.add, ALU.max))
                    if fwd:
                        ch.then(dve.tensor_copy(carried[:, 1:P], cut[:, 0:P - 1]))
                    else:
                        ch.then(dve.tensor_copy(carried[:, 0:P - 1], cut[:, 1:P]))
                    ch.then(dve.memset(carried[0:1, first], -BIG))
                    dve.sem_inc(ask, 1)
                    dve.wait_ge(got, n + 1)
                    ch.then(dve.tensor_copy(carry[:], k.psum[:, 1, 0:1]))
                    ch.then(dve.tensor_tensor_scan(view(best), stops, view(value), carry[:, 0:1], ALU.add, ALU.max))

                spread_max(1, logit)
                spread_max(-1, best)
                if leaky:
                    ch.then(dve.tensor_scalar(stop[:, 0:L], key[:, 1:L + 1], 0.0, None, ALU.is_lt))
                    ch.then(dve.tensor_tensor(key[:, 0:L], logit[:], best[:], ALU.subtract))
                    ch.then(dve.tensor_tensor(logit[:], stop[:, 0:L], best[:], ALU.mult))
                    dve.sem_inc(best_ready, 1)
                    dve.sem_inc(flags_ready, 1)
                else:
                    ch.then(dve.tensor_tensor(key[:, 0:L], logit[:], best[:], ALU.subtract))
                dve.sem_inc(expo, 1)

            @block.tensor
            def _(pe):
                for n in (1, 3):
                    pe.wait_ge(ask, n)
                    for a in range(2):
                        ins = pe.transpose(k.psum[0:1, 0, a * P:(a + 1) * P], ends[:, a:a + 1], k.ident[:])
                    ins.then_inc(got, 1)
                    pe.wait_ge(ask, n + 1)
                    pe.transpose(k.psum[:, 1, 0:1], carried[0:1, :], k.ident[0:1, 0:1]).then_inc(got, 1)

            @block.scalar
            def _(act):
                for h in range(H):
                    at = slice(h * CHUNKS, (h + 1) * CHUNKS)
                    act.dma_start(key[at, :], bass.AP(k.rows_key.tensor, P - 1, [[L, CHUNKS], [1, L + 2]])
                                  ).then_inc(key_landed, 16)
                    act.dma_start(split(best[at, :]),
                                  k.rows_mask.rearrange("(c s) l -> c s l", c=CHUNKS)).then_inc(tmp_landed, 16)
                    if scale is not None:
                        act.dma_start(split(weight[at, :]),
                                      k.rows_weight.rearrange("(c s) l -> c s l", c=CHUNKS)).then_inc(w_landed, 16)
                act.wait_ge(expo, 1)
                act.activation(best[:], key[:, 0:L], ACT.Exp).then_inc(exp_done, 1)

        back_in = [sem(f"m{H}_back_in{q}") for q in range(RING)]
        back_turned, back_out = sem(f"m{H}_back_turned"), sem(f"m{H}_back_out")
        units = [(a, at, blocks) for a in range(OUTS) for at, blocks in batches]
        with nc.Block() as block:
            @block.sync
            def _(sp):
                for n, (a, at, blocks) in enumerate(units):
                    if n >= RING:
                        sp.wait_ge(back_turned, n + 1 - RING)
                    sp.dma_start(turn[n % RING][:, 0:blocks * P].rearrange("r (b l) -> r b l", b=blocks),
                                 block_rows(k.alphas[a], at, blocks)).then_inc(back_in[n % RING], 16)

            @block.tensor
            def _(pe):
                for n, (a, at, blocks) in enumerate(units):
                    pe.wait_ge(back_in[n % RING], 16 * (n // RING + 1))
                    if n >= RING:
                        pe.wait_ge(back_out, n + 1 - RING)
                    for b in range(blocks):
                        ins = pe.transpose(k.psum[:, n % RING, b * P:(b + 1) * P],
                                           turn[n % RING][:, b * P:(b + 1) * P], k.ident[:])
                    ins.then_inc(back_turned, 1)

            @block.vector
            def _(dve):
                for n, (a, at, blocks) in enumerate(units):
                    dve.wait_ge(back_turned, n + 1)
                    dve.tensor_copy(k.aux[:, at * BLK:(at + blocks) * BLK, a * H:(a + 1) * H],
                                    k.psum[:, n % RING, 0:blocks * P].rearrange("p (s h) -> p s h", h=H)
                                    ).then_inc(back_out, 1)


def one_hot(dve, k, out, g):
    return dve.tensor_tensor(out[:], k.iota[:].unsqueeze(1).to_broadcast([P, GROUP, P]),
                             k.dloc[:, bass.ds(g * GROUP, GROUP)].unsqueeze(2).to_broadcast([P, GROUP, P]),
                             ALU.is_equal)


def attend(nc, k, H, outs):
    AUX = outs * H
    W = D + AUX
    with ExitStack() as ctx:
        def sb(name, shape, dt=F32):
            return ctx.enter_context(nc.sbuf_tensor(name, shape, dt))

        sem = ctx.enter_context(semaphores(nc))

        rows = [sb(f"t{H}_rows{q}", [P, GROUP, D]) for q in range(RING)]
        msg = [sb(f"t{H}_msg{q}", [P, GROUP, W]) for q in range(RING)]
        apart = [sb(f"t{H}_apart{b}", [P, GROUP, P]) for b in range(2)]
        onehot = [sb(f"t{H}_onehot{q}", [P, GROUP, P]) for q in range(RING)]
        one = sb(f"t{H}_one", [P, 1])
        landed = [sem(f"t{H}_landed{q}") for q in range(RING)]
        weighed, one_weighed = sem(f"t{H}_weighed"), sem(f"t{H}_one_weighed")
        apart_ready, onehot_ready, summed = (
            sem(f"t{H}_{n}") for n in ("apart_ready", "onehot_ready", "summed"))
        added, cleared, half_cleared = (sem(f"t{H}_{n}") for n in ("added", "cleared", "half_cleared"))
        block = ctx.enter_context(nc.Block())
        spill_rows = k.spill.rearrange("s p d -> p s d")
        R = 2 * GROUP
        CREDIT = RING * GROUP
        OWN = 3

        def weigh(eng, q, st, s, first=0, heads=H):
            at = slice(first * (D // H), (first + heads) * (D // H))
            split = lambda t: t.rearrange("p (h c) -> p h c", h=heads)
            a = k.aux[:, bass.ds(st, 1), first:first + heads].rearrange("p o h -> p (o h)")
            return eng.tensor_tensor(split(msg[q][:, s, at]), split(rows[q][:, s, at]),
                                     a.unsqueeze(2).to_broadcast([P, heads, D // H]), ALU.mult)

        @block.sync
        def _(sp):
            for it in passes(sp, PASSES):
                for q in range(RING):
                    g = it * RING + q
                    sp.wait_ge(weighed, g + 1)
                    sp.wait_ge(one_weighed, g + 1)
                    sp.dma_start(rows[q][:], spill_rows[:, bass.ds(g * GROUP, GROUP), :]).then_inc(landed[q], 16)

        @block.gpsimd
        def _(pool):
            pool.sem_inc(weighed, RING)
            half = NT // 2
            pool.memset(k.acc[:, half:NT, :], 0.0).then_inc(half_cleared, 1)
            for it in passes(pool, PASSES):
                for q in range(RING):
                    g = it * RING + q
                    pool.wait_ge(landed[q], (it + 1) * 16)
                    pool.wait_ge(summed, g * GROUP + GROUP)
                    pool.tensor_copy(msg[q][:, :, D:W], k.aux[:, bass.ds(g * GROUP, GROUP), 0:AUX])
                    for s in range(GROUP):
                        if s != OWN:
                            ins = weigh(pool, q, g * GROUP + s, s)
                    ins.then_inc(weighed, 1)

        @block.scalar
        def _(act):
            act.wait_ge(cleared, 2)

            def part_group(it, q):
                g = it * RING + q
                act.wait_ge(onehot_ready, g + 1)
                for s in range(GROUP):
                    ins = act.activation(apart[q % 2][:, s, :], k.iota[:], ACT.Abs,
                                         bias=k.dloc[:, bass.ds(g * GROUP + s, 1)], scale=-1.0)
                ins.then_inc(apart_ready, 1)

            def mark_group(it, q, _):
                g = it * RING + q
                act.wait_ge(summed, g * GROUP + GROUP)
                act.wait_ge(apart_ready, g + 1)
                act.activation(flat(onehot[q][:]), flat(apart[q % 2][:]), ACT.Relu, bias=one[:, 0:1], scale=-1.0
                               ).then_inc(onehot_ready, 1)

            act.sem_inc(onehot_ready, 2)
            one_ahead(act, nc, None, None, part_group, mark_group)

        @block.vector
        def _(dve):
            dve.sem_inc(one_weighed, RING)
            dve.sem_inc(added, R)
            dve.memset(k.acc[:, 0:NT // 2, :], 0.0).then_inc(cleared, 1)
            dve.memset(one[:], 1.0).then_inc(cleared, 1)
            dve.wait_ge(cleared, 2)
            dve.wait_ge(half_cleared, 1)

            def weigh_own(it, q, part):
                g = it * RING + q
                if part == 0:
                    dve.wait_ge(landed[q], (it + 1) * 16)
                    dve.wait_ge(summed, g * GROUP + GROUP)
                ins = weigh(dve, q, g * GROUP + OWN, OWN, part * (H // GROUP), H // GROUP)
                if part == GROUP - 1:
                    ins.then_inc(one_weighed, 1)

            def add_step(it, q, s, j):
                st = (it * RING + q) * GROUP + s
                dve.wait_ge(summed, st + 1 + CREDIT)
                dve.wait_ge(added, st + R)
                at = k.acc[:, bass.ds(j, 1), 0:W].rearrange("p o w -> p (o w)")
                dve.tensor_tensor(at, at, k.psum[:, (q % 2) * GROUP + s, 0:W], ALU.add).then_inc(added, 1)

            step_ahead(dve, nc, k.step_j, NODE_TILES - 1, weigh_own, add_step)

        @block.tensor
        def _(pe):
            pe.sem_inc(summed, CREDIT)
            for it in passes(pe, PASSES):
                for q in range(RING):
                    g = it * RING + q
                    b = q % 2
                    pe.wait_ge(weighed, g + 1 + RING)
                    pe.wait_ge(one_weighed, g + 1 + RING)
                    pe.wait_ge(onehot_ready, g + 1 + 2)
                    pe.wait_ge(added, g * GROUP + GROUP)
                    for s in range(GROUP):
                        pe.matmul(k.psum[:, b * GROUP + s, 0:W], onehot[q][:, s, :], msg[q][:, s, :],
                                  start=True, stop=True).then_inc(summed, 1)


def flat(t):
    return t.rearrange("p t d -> p (t d)")


def over_tiles(row):
    return row.unsqueeze(1).to_broadcast([P, 2, D])


def norm_stats(dve, ch, value, stats, mean_var, var_ready):
    for t in range(2):
        ch.tick(dve.bn_stats(stats[:, t, :], value[:, t, :]))
    ch.wait()
    dve.sem_inc(ch.sem, 1)
    ch.n += 1
    for t in range(2):
        ins = dve.bn_aggr(mean_var[:, t, :], stats[:, t, :])
    ins.then_inc(var_ready, 1)


def norm_apply(dve, ch, out, value, mean_var, std):
    ch.then(dve.reciprocal(std[:], std[:]))
    for t in range(2):
        ch.tick(dve.tensor_scalar(out[:, t, :], value[:, t, :], mean_var[:, t, 0:1], std[:, t:t + 1],
                                    ALU.subtract, ALU.mult))
    ch.wait()


def gat_finish(nc, k, x, bias, slope):
    H = 4
    with ExitStack() as ctx:
        def sb(name, shape, dt=F32):
            return ctx.enter_context(nc.sbuf_tensor(name, shape, dt))

        sem = ctx.enter_context(semaphores(nc))

        own = sb("n1_own", [P, NT, H])
        top = sb("n1_top", [P, NT, H])
        scaled = sb("n1_scaled", [P, NT, H])
        den = sb("n1_den", [P, NT, H])
        bias_row, slope_col, eps = sb("n1_bias", [P, D]), sb("n1_slope", [P, 1]), sb("n1_eps", [P, 1])
        B = range(PAIRS)
        xin = [sb(f"n1_x{b}", [P, 2, D]) for b in B]
        hin = [sb(f"n1_h{b}", [P, 2, D]) for b in B]
        y = [sb(f"n1_y{b}", [P, 2, D]) for b in B]
        neg = [sb(f"n1_neg{b}", [P, 2, D]) for b in B]
        out = [sb(f"n1_out{b}", [P, 2, D]) for b in B]
        stats = [sb(f"n1_stats{b}", [P, 2, 6]) for b in B]
        mean_var = [sb(f"n1_mv{b}", [P, 2, 2]) for b in B]
        std = [sb(f"n1_std{b}", [P, 2]) for b in B]
        consts, diff_ready, exps_ready, coef_ready, chain = (
            sem(f"n1_{n}") for n in ("consts", "diff_ready", "exps_ready", "coef_ready", "chain"))
        loads = [sem(f"n1_loads{b}") for b in B]
        own_ready, var_ready, std_ready, out_ready = (
            sem(f"n1_{n}") for n in ("own_ready", "var_ready", "std_ready", "out_ready"))
        stored = [sem(f"n1_stored{b}") for b in B]
        own_chain, sum_chain, norm_chain = sem("n1_own_chain"), sem("n1_sum_chain"), sem("n1_norm_chain")
        block = ctx.enter_context(nc.Block())
        CREDIT = PAIRS
        heads = lambda t: t.rearrange("p t (h c) -> p t h c", h=H)

        def per_head(table, m):
            return table[:, bass.ds(2 * m, 2), :].unsqueeze(3).to_broadcast([P, 2, H, D // H])

        @block.sync
        def _(sp):
            sp.dma_start(bias_row[:], bias.partition_broadcast(P)).then_inc(consts, 16)
            sp.dma_start(slope_col[:], slope.partition_broadcast(P)).then_inc(consts, 16)
            for it in passes(sp, NODE_PASSES):
                for b in B:
                    m = it * PAIRS + b
                    sp.wait_ge(out_ready, m + 1)
                    sp.dma_start(xin[b][:], pair(x, m)).then_inc(loads[b], 16)
                    sp.dma_start(hin[b][:], pair(k.hrow, m)[:, :, 0:D]).then_inc(loads[b], 16)

        @block.gpsimd
        def _(pool):
            pool.wait_ge(coef_ready, 1)
            pool.wait_ge(consts, 32)

            def weigh_own(it, b):
                m = it * PAIRS + b
                pool.wait_ge(loads[b], (it + 1) * 32)
                for t in range(2):
                    w = own[:, bass.ds(2 * m + t, 1), :].rearrange("p o h -> p (o h)")
                    ins = pool.tensor_tensor(hin[b][:, t].rearrange("p (h c) -> p h c", h=H),
                                             hin[b][:, t].rearrange("p (h c) -> p h c", h=H),
                                             w.unsqueeze(2).to_broadcast([P, H, D // H]), ALU.mult)
                    if t == 0:
                        ins.then_inc(own_chain, 1)
                ins.then_inc(own_chain, 1)
                pool.wait_ge(own_chain, 2 * m + 2)
                pool.tensor_tensor(hin[b][:], hin[b][:], over_tiles(bias_row[:]), ALU.add).then_inc(own_ready, 1)

            def store(it, b):
                m = it * PAIRS + b
                pool.wait_ge(out_ready, m + 1 + CREDIT)
                pool.dma_start(pair(k.x1, m), out[b][:]).then_inc(stored[b], 16)

            staged([(0, weigh_own), (2, store)])(pool)
            for b in B:
                pool.wait_ge(stored[b], 16 * NODE_PASSES)

        @block.scalar
        def _(act):
            act.wait_ge(diff_ready, 1)
            act.activation(scaled[:], scaled[:], ACT.Exp)
            act.activation(own[:], own[:], ACT.Exp).then_inc(exps_ready, 1)
            for it in passes(act, NODE_PASSES):
                for b in B:
                    act.wait_ge(var_ready, it * PAIRS + b + 1)
                    act.activation(std[b][:], mean_var[b][:, :, 1], ACT.Sqrt, bias=eps[:, 0:1]).then_inc(std_ready, 1)

        @block.vector
        def _(dve):
            dve.sem_inc(out_ready, CREDIT)
            ch = Chain(dve, chain)
            ch.tick(dve.memset(eps[:], LN_EPS))
            ch.then(dve.memset(k.acc[:, NODE_TILES:NT, :], 0.0))
            maxima, weights, flag = (k.acc[:, :, D + a * H:D + (a + 1) * H] for a in (1, 0, 2))
            ch.then(dve.tensor_tensor(own[:], k.att[:, :, 0:H], k.att[:, :, H:2 * H], ALU.add))
            ch.then(dve.scalar_tensor_tensor(out=own[:], in0=own[:], scalar=0.2, in1=own[:],
                                             op0=ALU.mult, op1=ALU.max))
            ch.then(dve.tensor_scalar(den[:], flag, -1.0, BIG, ALU.add, ALU.mult))
            ch.then(dve.tensor_tensor(scaled[:], maxima, den[:], ALU.add))
            ch.then(dve.tensor_tensor(top[:], scaled[:], own[:], ALU.max))
            ch.then(dve.tensor_tensor(scaled[:], scaled[:], top[:], ALU.subtract))
            dve.tensor_tensor(own[:], own[:], top[:], ALU.subtract).then_inc(diff_ready, 1)
            dve.wait_ge(exps_ready, 1)
            ch.then(dve.tensor_tensor(den[:], scaled[:], weights, ALU.mult))
            ch.then(dve.tensor_tensor(den[:], den[:], own[:], ALU.add))
            ch.then(dve.tensor_scalar(den[:], den[:], 1e-16, None, ALU.add))
            ch.then(dve.reciprocal(den[:], den[:]))
            ch.tick(dve.tensor_tensor(scaled[:], scaled[:], den[:], ALU.mult))
            ch.then(dve.tensor_tensor(own[:], own[:], den[:], ALU.mult))
            dve.sem_inc(coef_ready, 1)
            dve.wait_ge(consts, 32)

            def combine(it, b):
                m = it * PAIRS + b
                ch = Chain(dve, sum_chain, m * 9)
                for t in range(2):
                    a = scaled[:, bass.ds(2 * m + t, 1), :].rearrange("p o h -> p (o h)")
                    ch.tick(dve.tensor_tensor(
                        y[b][:, t].rearrange("p (h c) -> p h c", h=H),
                        k.acc[:, bass.ds(2 * m + t, 1), 0:D].rearrange("p o (h c) -> p (o h) c", h=H),
                        a.unsqueeze(2).to_broadcast([P, H, D // H]), ALU.mult))
                dve.wait_ge(own_ready, m + 1)
                ch.wait()
                ch.then(dve.tensor_tensor(y[b][:], y[b][:], hin[b][:], ALU.add))
                ch.then(dve.tensor_scalar(neg[b][:], y[b][:], 0.0, None, ALU.min))
                ch.then(dve.scalar_tensor_tensor(out=y[b][:], in0=y[b][:], scalar=0.0, in1=xin[b][:],
                                                 op0=ALU.max, op1=ALU.add))
                ch.then(dve.scalar_tensor_tensor(out=y[b][:], in0=neg[b][:], scalar=slope_col[:, 0:1],
                                                 in1=y[b][:], op0=ALU.mult, op1=ALU.add))
                norm_stats(dve, ch, y[b], stats[b], mean_var[b], var_ready)
                assert ch.n == 9

            def norm(it, b):
                m = it * PAIRS + b
                ch = Chain(dve, norm_chain, m * 3)
                dve.wait_ge(std_ready, m + 1)
                wait_if_any(dve, stored[b], it * 16)
                norm_apply(dve, ch, out[b], y[b], mean_var[b], std[b])
                dve.sem_inc(out_ready, 1)
                assert ch.n == 3

            staged([(0, combine), (1, norm)])(dve)


def gin_edges(nc, k, edge_attr):
    with ExitStack() as ctx:
        def sb(name, shape, dt=F32):
            return ctx.enter_context(nc.sbuf_tensor(name, shape, dt))

        sem = ctx.enter_context(semaphores(nc))

        R = 2 * GROUP
        idx = [sb(f"g_idx{q}", [P, GROUP], I32) for q in range(RING)]
        rows = [sb(f"g_rows{q}", [P, GROUP, D]) for q in range(RING)]
        attr = [sb(f"g_attr{q}", [P, GROUP, D]) for q in range(RING)]
        msg = [sb(f"g_msg{b}", [P, GROUP, D]) for b in range(2)]
        onehot = [sb(f"g_onehot{b}", [P, GROUP, P]) for b in range(2)]
        run = sb("g_run", [P, R, D])
        gathered = [sem(f"g_gathered{q}") for q in range(RING)]
        attr_landed = [sem(f"g_attr_landed{q}") for q in range(RING)]
        idx_landed = [sem(f"g_idx_landed{q}") for q in range(RING)]
        passed, added, msg_ready = (sem(f"g_{n}") for n in ("passed", "added", "msg_ready"))
        onehot_ready, summed, chained, kept = (
            sem(f"g_{n}") for n in ("onehot_ready", "summed", "chained", "kept"))
        block = ctx.enter_context(nc.Block())

        @block.sync
        def _(sp):
            for it in passes(sp, PASSES):
                i = load_indices(nc, sp, k.step_i, it * (RING * GROUP), RING * GROUP, EA_TILES - 1)
                for q in range(RING):
                    g = it * RING + q
                    wait_if_any(sp, gathered[q], it * (16 * GROUP))
                    sp.dma_start(idx[q][:], k.src_idx[:, bass.ds(g * GROUP, GROUP)]).then_inc(idx_landed[q], 16)
                    sp.wait_ge(msg_ready, g + 1)
                    for s in range(GROUP):
                        sp.dma_start(attr[q][:, s, :], edge_attr[bass.ds(i[q * GROUP + s] * P, P), :]
                                     ).then_inc(attr_landed[q], 16)

        @block.gpsimd
        def _(pool):
            for it in passes(pool, PASSES):
                for q in range(RING):
                    pool.wait_ge(idx_landed[q], (it + 1) * 16)
                    pool.wait_ge(added, it * RING + q + 1)
                    pool.sem_inc(passed, 1)
                    for s in range(GROUP):
                        pool.indirect_dma_start(rows[q][:, s, :], None, k.x1,
                                                bass.IndirectOffsetOnAxis(ap=idx[q][:, s:s + 1], axis=0)
                                                ).then_inc(gathered[q], 16)

        @block.scalar
        def _(act):
            act.sem_inc(msg_ready, RING)
            act.sem_inc(kept, R)

            def relu_group(it, q):
                g = it * RING + q
                act.wait_ge(added, g + 1 + RING)
                act.wait_ge(summed, g * GROUP + GROUP)
                act.activation(flat(msg[q % 2][:]), flat(attr[q][:]), ACT.Relu).then_inc(msg_ready, 1)

            def keep_group(it, q, j):
                for s in range(GROUP):
                    st = (it * RING + q) * GROUP + s
                    act.wait_ge(chained, st + 1 + R)
                    act.wait_ge(kept, st + R)
                    act.copy(k.acc[:, bass.ds(j[q * GROUP + s], 1), 0:D].rearrange("p o w -> p (o w)"),
                             run[:, (q % 2) * GROUP + s, :]).then_inc(kept, 1)

            one_ahead(act, nc, k.step_j, NODE_TILES - 1, relu_group, keep_group)

        @block.vector
        def _(dve):
            dve.memset(run[:, R - 1, :], 0.0)
            dve.sem_inc(added, RING)
            dve.sem_inc(chained, R)
            dve.sem_inc(onehot_ready, 2)

            def add_group(it, q):
                g = it * RING + q
                dve.wait_ge(summed, g * GROUP + GROUP)
                one_hot(dve, k, onehot[q % 2], g).then_inc(onehot_ready, 1)
                dve.wait_ge(gathered[q], (it + 1) * (16 * GROUP))
                dve.wait_ge(attr_landed[q], (it + 1) * (16 * GROUP))
                dve.tensor_tensor(flat(attr[q][:]), flat(attr[q][:]), flat(rows[q][:]), ALU.add).then_inc(added, 1)

            def chain_group(it, q, _):
                for s in range(GROUP):
                    st = (it * RING + q) * GROUP + s
                    at = (q % 2) * GROUP + s
                    dve.wait_ge(summed, st + 1 + R)
                    dve.wait_ge(kept, st + 1)
                    dve.wait_ge(chained, st + R)
                    dve.scalar_tensor_tensor(out=run[:, at, :], in0=run[:, (at - 1) % R, :],
                                             scalar=k.keep[:, bass.ds(st, 1)], in1=k.psum[:, at, 0:D],
                                             op0=ALU.mult, op1=ALU.add).then_inc(chained, 1)

            one_ahead(dve, nc, None, None, add_group, chain_group)

        @block.tensor
        def _(pe):
            pe.sem_inc(summed, R)
            for it in passes(pe, PASSES):
                for q in range(RING):
                    g = it * RING + q
                    b = q % 2
                    pe.wait_ge(msg_ready, g + 1 + RING)
                    pe.wait_ge(onehot_ready, g + 1 + 2)
                    for s in range(GROUP):
                        pe.wait_ge(chained, g * GROUP + s + 1)
                        pe.matmul(k.psum[:, b * GROUP + s, 0:D], onehot[b][:, s, :], msg[b][:, s, :],
                                  start=True, stop=True).then_inc(summed, 1)


def turn_pair(pe, bank, rows, ident):
    for h in range(2):
        for t in range(2):
            at = (h * 2 + t) * P
            ins = pe.transpose(bank[:, at:at + P], rows[:, t, h * P:(h + 1) * P], ident)
    return ins


def gin_nodes(nc, k, w1, b1, w2, b2, gamma, beta, w_next):
    with ExitStack() as ctx:
        def sb(name, shape, dt=F32):
            return ctx.enter_context(nc.sbuf_tensor(name, shape, dt))

        sem = ctx.enter_context(semaphores(nc))

        B = range(PAIRS)
        ws = [sb(f"n2_w{n}", [P, 2, D]) for n in range(3)]
        b1_col, rows3 = sb("n2_b1", [P, 2]), sb("n2_rows", [P, 3, D])
        eps = sb("n2_eps", [P, 1])
        xin = [sb(f"n2_x{b}", [P, 2, D]) for b in B]
        z = [sb(f"n2_z{b}", [P, 2, D]) for b in B]
        y = [sb(f"n2_y{b}", [P, 2, D]) for b in B]
        out = [sb(f"n2_out{b}", [P, 2, D]) for b in B]
        turned_sb = [sb(f"n2_turned{b}", [P, 2, 2 * P]) for b in B]
        hidden = [sb(f"n2_hidden{b}", [P, 2, 2 * P]) for b in B]
        stats = [sb(f"n2_stats{b}", [P, 2, 6]) for b in B]
        mean_var = [sb(f"n2_mv{b}", [P, 2, 2]) for b in B]
        std = [sb(f"n2_std{b}", [P, 2]) for b in B]
        consts = sem("n2_consts")
        landed = [sem(f"n2_landed{b}") for b in B]
        stored = [sem(f"n2_stored{b}") for b in B]
        (z_ready, z_turned, z_copied, mixed, hidden_ready, h_done, h_taken, inner_var, inner_std, var_ready,
         std_ready, out_ready, out_turned, out_copied, next_done, support_ready) = (sem(f"n2_{n}") for n in (
             "z_ready", "z_turned", "z_copied", "mixed", "hidden_ready", "h_done", "h_taken", "inner_var",
             "inner_std", "var_ready", "std_ready", "out_ready", "out_turned", "out_copied", "next_done",
             "support_ready"))
        beta_added = sem("n2_beta_added")
        setup, outer_chain, inner_chain, norm_chain = (
            sem(f"n2_{n}") for n in ("setup", "outer_chain", "inner_chain", "norm_chain"))
        block = ctx.enter_context(nc.Block())
        Z_BANK, OUT_BANK, MIX_BANK, H_BANK, NEXT_BANK = 0, 1, 2, 4, 6

        @block.sync
        def _(sp):
            for n, w in enumerate((w1, w2, w_next)):
                sp.dma_start(ws[n][:], w.rearrange("(h p) n -> p h n", p=P)).then_inc(consts, 16)
            sp.dma_start(b1_col[:], b1).then_inc(consts, 16)
            for n, r in enumerate((b2, gamma, beta)):
                sp.dma_start(rows3[:, n, :], r.partition_broadcast(P)).then_inc(consts, 16)
            for it in passes(sp, NODE_PASSES):
                for b in B:
                    m = it * PAIRS + b
                    sp.wait_ge(out_ready, m + 1)
                    sp.dma_start(xin[b][:], pair(k.x1, m)).then_inc(landed[b], 16)

        @block.gpsimd
        def _(pool):
            pool.wait_ge(setup, 2)
            pool.wait_ge(consts, 16 * 7)

            def add_sums(it, b):
                m = it * PAIRS + b
                pool.wait_ge(landed[b], (it + 1) * 16)
                pool.wait_ge(z_turned, m + 1)
                pool.tensor_tensor(z[b][:], xin[b][:], k.acc[:, bass.ds(2 * m, 2), 0:D], ALU.add).then_inc(z_ready, 1)

            def add_beta(it, b):
                pool.wait_ge(inner_var, it * PAIRS + b + 1)
                pool.tensor_tensor(xin[b][:], xin[b][:], over_tiles(rows3[:, 2, :]), ALU.add).then_inc(beta_added, 1)

            def store(it, b):
                m = it * PAIRS + b
                pool.wait_ge(out_ready, m + 1 + PAIRS)
                pool.dma_start(pair(k.x2, m), out[b][:]).then_inc(stored[b], 16)

            staged([(0, add_sums), (4, store), (2, add_beta)])(pool)
            for b in B:
                pool.wait_ge(stored[b], 16 * NODE_PASSES)

        @block.scalar
        def _(act):
            act.sem_inc(z_copied, 1)
            act.sem_inc(out_copied, 1)
            act.sem_inc(hidden_ready, BANKS)
            act.sem_inc(support_ready, BANKS)
            act.wait_ge(consts, 16 * 7)

            def copy_z(it, b):
                act.wait_ge(z_turned, it * PAIRS + b + 1 + PAIRS)
                act.copy(flat(turned_sb[b][:]), k.psum[:, Z_BANK, :]).then_inc(z_copied, 1)

            def hide(it, b):
                act.wait_ge(mixed, it * PAIRS + b + 1)
                for f in range(2):
                    ins = act.activation(hidden[b][:, f, :], k.psum[:, MIX_BANK + b % BANKS, f * 2 * P:(f + 1) * 2 * P],
                                         ACT.Relu, bias=b1_col[:, f:f + 1])
                ins.then_inc(hidden_ready, 1)

            def root_inner(it, b):
                act.wait_ge(inner_var, it * PAIRS + b + 1)
                act.activation(std[b][:], mean_var[b][:, :, 1], ACT.Sqrt, bias=eps[:, 0:1]).then_inc(inner_std, 1)

            def root(it, b):
                act.wait_ge(var_ready, it * PAIRS + b + 1)
                act.activation(std[b][:], mean_var[b][:, :, 1], ACT.Sqrt, bias=eps[:, 0:1]).then_inc(std_ready, 1)

            def copy_out(it, b):
                act.wait_ge(out_turned, it * PAIRS + b + 1)
                act.copy(flat(turned_sb[b][:]), k.psum[:, OUT_BANK, :]).then_inc(out_copied, 1)

            def keep_support(it, b):
                m = it * PAIRS + b
                act.wait_ge(next_done, m + 1)
                act.copy(k.support[:, bass.ds(2 * m, 2), :],
                         k.psum[:, NEXT_BANK + b % BANKS, :].rearrange("p (t d) -> p t d", t=2)
                         ).then_inc(support_ready, 1)

            staged([(5, keep_support), (0, copy_z), (1, hide), (4, copy_out), (3, root), (2, root_inner)])(act)

        @block.tensor
        def _(pe):
            pe.sem_inc(z_turned, PAIRS)
            pe.wait_ge(consts, 16 * 7)

            def rows_by(n, b, left, at):
                for t in range(2):
                    for h in range(2):
                        ins = pe.matmul(k.psum[:, at, t * D:(t + 1) * D], left[b][:, h, t * P:(t + 1) * P],
                                        ws[n][:, h, :], start=(h == 0), stop=(h == 1))
                return ins

            def turn_z(it, b):
                m = it * PAIRS + b
                pe.wait_ge(z_ready, m + 1)
                pe.wait_ge(z_copied, m + 1)
                turn_pair(pe, k.psum[:, Z_BANK], z[b], k.ident[:]).then_inc(z_turned, 1)

            def mix(it, b):
                m = it * PAIRS + b
                pe.wait_ge(z_copied, m + 1 + 1)
                pe.wait_ge(hidden_ready, bank_free(m, b))
                for f in range(2):
                    for h in range(2):
                        ins = pe.matmul(k.psum[:, MIX_BANK + b % BANKS, f * 2 * P:(f + 1) * 2 * P],
                                        ws[0][:, h, f * P:(f + 1) * P], turned_sb[b][:, h, :],
                                        start=(h == 0), stop=(h == 1))
                ins.then_inc(mixed, 1)

            def project(it, b):
                m = it * PAIRS + b
                pe.wait_ge(hidden_ready, m + 1 + BANKS)
                pe.wait_ge(h_taken, bank_free(m, b))
                rows_by(1, b, hidden, H_BANK + b % BANKS).then_inc(h_done, 1)

            def turn_out(it, b):
                m = it * PAIRS + b
                pe.wait_ge(out_ready, m + 1 + PAIRS)
                pe.wait_ge(out_copied, m + 1)
                turn_pair(pe, k.psum[:, OUT_BANK], out[b], k.ident[:]).then_inc(out_turned, 1)

            def support(it, b):
                m = it * PAIRS + b
                pe.wait_ge(out_copied, m + 1 + 1)
                pe.wait_ge(support_ready, bank_free(m, b))
                rows_by(2, b, turned_sb, NEXT_BANK + b % BANKS).then_inc(next_done, 1)

            staged([(5, support), (2, project), (0, turn_z), (1, mix), (4, turn_out)])(pe)

        @block.vector
        def _(dve):
            dve.sem_inc(out_ready, PAIRS)
            dve.sem_inc(h_taken, BANKS)
            dve.memset(k.acc[:, NODE_TILES:NT, :], 0.0).then_inc(setup, 1)
            dve.memset(eps[:], LN_EPS).then_inc(setup, 1)
            dve.wait_ge(setup, 2)
            dve.wait_ge(consts, 16 * 7)

            def residual(it, b):
                m = it * PAIRS + b
                ch = Chain(dve, inner_chain, m * 5)
                dve.wait_ge(landed[b], (it + 1) * 16)
                dve.wait_ge(h_done, m + 1)
                h = k.psum[:, H_BANK + b % BANKS, :].rearrange("p (t d) -> p t d", t=2)
                ch.then(dve.tensor_tensor(y[b][:], h, over_tiles(rows3[:, 0, :]), ALU.add))
                dve.sem_inc(h_taken, 1)
                ch.then(dve.scalar_tensor_tensor(out=y[b][:], in0=y[b][:], scalar=0.0, in1=xin[b][:],
                                                 op0=ALU.max, op1=ALU.add))
                norm_stats(dve, ch, y[b], stats[b], mean_var[b], inner_var)
                assert ch.n == 5

            def inner_norm(it, b):
                m = it * PAIRS + b
                ch = Chain(dve, norm_chain, m * 8)
                dve.wait_ge(inner_std, m + 1)
                norm_apply(dve, ch, y[b], y[b], mean_var[b], std[b])
                ch.then(dve.tensor_tensor(y[b][:], y[b][:], over_tiles(rows3[:, 1, :]), ALU.mult))
                dve.wait_ge(beta_added, m + 1)
                ch.then(dve.tensor_tensor(y[b][:], y[b][:], xin[b][:], ALU.add))
                norm_stats(dve, ch, y[b], stats[b], mean_var[b], var_ready)
                assert ch.n == 8

            def outer_norm(it, b):
                m = it * PAIRS + b
                ch = Chain(dve, outer_chain, m * 3)
                dve.wait_ge(std_ready, m + 1)
                wait_if_any(dve, stored[b], it * 16)
                norm_apply(dve, ch, out[b], y[b], mean_var[b], std[b])
                dve.sem_inc(out_ready, 1)
                assert ch.n == 3

            staged([(4, outer_norm), (3, inner_norm), (2, residual)])(dve)


def gcn_edges(nc, k):
    with ExitStack() as ctx:
        def sb(name, shape, dt=F32):
            return ctx.enter_context(nc.sbuf_tensor(name, shape, dt))

        sem = ctx.enter_context(semaphores(nc))

        away = sb("c_away", [P, STEPS])
        earlier = sb("c_earlier", [P, P])
        srow = [sb(f"c_srow{q}", [P, GROUP, P]) for q in range(RING)]
        onehot = [sb(f"c_onehot{b}", [P, GROUP, P]) for b in range(2)]
        same = [sb(f"c_same{b}", [P, GROUP, P]) for b in range(2)]
        dump = [sb(f"c_dump{b}", [P, GROUP, P]) for b in range(2)]
        before = [sb(f"c_before{b}", [P, GROUP]) for b in range(2)]
        shift = [sb(f"c_shift{b}", [P, GROUP]) for b in range(2)]
        target = [sb(f"c_target{q}", [P, GROUP], I32) for q in range(RING)]
        mix = [sb(f"c_mix{b}", [P, GROUP * P]) for b in range(2)]
        update = [sb(f"c_update{q}", [P, GROUP, D]) for q in range(RING)]
        srow_landed = [sem(f"c_srow_landed{q}") for q in range(RING)]
        scattered = [sem(f"c_scattered{a}") for a in range(GROUP)]
        setup, chain, passed = sem("c_setup"), sem("c_chain"), sem("c_passed")
        built, target_ready, mixed, mix_ready, spread, update_ready = (
            sem(f"c_{n}") for n in ("built", "target_ready", "mixed", "mix_ready", "spread", "update_ready"))
        block = ctx.enter_context(nc.Block())
        src_rows = k.rows_src.rearrange("(o s) l -> o (s l)", o=1)

        @block.sync
        def _(sp):
            for it in passes(sp, PASSES):
                for q in range(RING):
                    g = it * RING + q
                    sp.wait_ge(built, g + 1)
                    sp.dma_start(srow[q][:].rearrange("p s l -> p (s l)"),
                                 src_rows[:, bass.ds(g * (GROUP * P), GROUP * P)].partition_broadcast(P)
                                 ).then_inc(srow_landed[q], 16)

        @block.vector
        def _(dve):
            OPS = RING * 6
            FIRST = 3
            ch = Chain(dve, chain)
            ch.tick(dve.tensor_scalar(away[:], k.src[:], -1.0, float(SPARE_ROW), ALU.mult, ALU.add))
            ch.then(dve.tensor_scalar(earlier[:], k.iota[:], k.lane[:, 0:1], None, ALU.is_lt))
            ch.then(dve.tensor_scalar(away[:], away[:], k.lane[:, 0:1], None, ALU.add))
            assert ch.n == FIRST
            dve.sem_inc(built, RING)
            for it in passes(dve, PASSES):
                ch = Chain(dve, chain, it * OPS + FIRST)
                for q in range(RING):
                    g = it * RING + q
                    b = q % 2
                    dve.wait_ge(mixed, g + 1)
                    one_hot(dve, k, onehot[b], g)
                    dve.wait_ge(srow_landed[q], (it + 1) * 16)
                    for s in range(GROUP):
                        st = g * GROUP + s
                        dve.tensor_scalar(same[b][:, s, :], srow[q][:, s, :], k.src[:, bass.ds(st, 1)],
                                          k.weight[:, bass.ds(st, 1)], ALU.is_equal, ALU.mult)
                        ch.tick(dve.scalar_tensor_tensor(
                            out=dump[b][:, s, :], in0=srow[q][:, s, :], scalar=k.src[:, bass.ds(st, 1)],
                            in1=earlier[:], op0=ALU.is_equal, op1=ALU.mult, accum_out=before[b][:, s:s + 1]))
                    ch.wait()
                    dve.sem_inc(built, 1)
                    ch.then(dve.scalar_tensor_tensor(out=shift[b][:], in0=before[b][:], scalar=0.5,
                                                     in1=away[:, bass.ds(g * GROUP, GROUP)],
                                                     op0=ALU.is_gt, op1=ALU.mult))
                    dve.wait_ge(passed, g * GROUP + GROUP)
                    ch.tick(dve.tensor_tensor(target[q][:], shift[b][:], k.src[:, bass.ds(g * GROUP, GROUP)],
                                                ALU.add))
                    ch.wait()
                    dve.sem_inc(target_ready, 1)
                assert ch.n == OPS

        @block.tensor
        def _(pe):
            pe.sem_inc(mixed, 2)
            pe.sem_inc(spread, 2)

            def mix_group(it, q):
                g = it * RING + q
                b = q % 2
                pe.wait_ge(built, g + 1 + RING)
                pe.wait_ge(mix_ready, g + 1)
                for s in range(GROUP):
                    ins = pe.matmul(k.psum[:, b, s * P:(s + 1) * P], onehot[b][:, s, :], same[b][:, s, :],
                                    start=True, stop=True)
                ins.then_inc(mixed, 1)

            def spread_group(it, q, j):
                g = it * RING + q
                b = q % 2
                pe.wait_ge(mix_ready, g + 1 + 2)
                pe.wait_ge(update_ready, g + 1)
                for s in range(GROUP):
                    ins = pe.matmul(k.psum[:, 2 + 2 * b + s // 2, (s % 2) * D:(s % 2 + 1) * D],
                                    mix[b][:, s * P:(s + 1) * P],
                                    k.support[:, bass.ds(j[q * GROUP + s], 1), :].rearrange("p o d -> p (o d)"),
                                    start=True, stop=True)
                ins.then_inc(spread, 1)

            one_ahead(pe, nc, k.step_j, NODE_TILES - 1, mix_group, spread_group)

        @block.scalar
        def _(act):
            act.sem_inc(mix_ready, 2)
            act.sem_inc(update_ready, 2)

            def copy_mix(it, q):
                g = it * RING + q
                b = q % 2
                act.wait_ge(mixed, g + 1 + 2)
                act.wait_ge(spread, g + 1)
                act.copy(mix[b][:], k.psum[:, b, :]).then_inc(mix_ready, 1)

            def copy_update(it, q, _):
                g = it * RING + q
                b = q % 2
                act.wait_ge(spread, g + 1 + 2)
                act.wait_ge(passed, g * GROUP + GROUP)
                act.copy(flat(update[q][:]), flat(k.psum[:, 2 + 2 * b:4 + 2 * b, :])).then_inc(update_ready, 1)

            one_ahead(act, nc, None, None, copy_mix, copy_update)

        @block.gpsimd
        def _(pool):
            pool.sem_inc(passed, (RING - 1) * GROUP)
            for it in passes(pool, PASSES):
                for q in range(RING):
                    g = it * RING + q
                    b = q % 2
                    pool.wait_ge(update_ready, g + 1 + 2)
                    pool.wait_ge(target_ready, g + 1)
                    for a in range(GROUP):
                        wait_if_any(pool, scattered[a], g * 16)
                        pool.sem_inc(passed, 1)
                        pool.indirect_dma_start(k.gcn[a],
                                                bass.IndirectOffsetOnAxis(ap=target[q][:, a:a + 1], axis=0),
                                                update[q][:, a, :], None, compute_op=ALU.add
                                                ).then_inc(scattered[a], 16)
            for a in range(GROUP):
                pool.wait_ge(scattered[a], 16 * PASSES * RING)


def gcn_nodes(nc, k, bias, gamma, beta, wq, wk, wv, bqkv):
    with ExitStack() as ctx:
        def sb(name, shape, dt=F32):
            return ctx.enter_context(nc.sbuf_tensor(name, shape, dt))

        sem = ctx.enter_context(semaphores(nc))

        B = range(PAIRS)
        ws = [sb(f"n3_w{n}", [P, 2, D]) for n in range(3)]
        bias_row, eps = sb("n3_bias", [P, D]), sb("n3_eps", [P, 1])
        norm_cols = sb("n3_norm_cols", [P, 2, 2])
        b_qkv = sb("n3_b_qkv", [1, 3 * D])
        ones = sb("n3_ones", [3, P], BF16)
        b_by_part = sb("n3_b_by_part", [3, 3 * D], BF16)
        b_lower = sb("n3_b_lower", [1, 2, 3 * D], BF16)
        rest = [sb(f"n3_rest{c}", [P, 2, D]) for c in range(3)]
        sums = [sb(f"n3_sums{b}", [P, GROUP, 2, D]) for b in B]
        xin = [sb(f"n3_x{b}", [P, 2, D]) for b in B]
        y = [sums[b][:, 0] for b in B]
        out = [sb(f"n3_out{b}", [P, 2, D]) for b in B]
        kv = [sb(f"n3_kv{b}", [P, 2, 2 * D]) for b in B]
        xn = [kv[b][:, :, 0:D] for b in B]
        turned_sb = [sb(f"n3_turned{c}", [P, 2, 2 * P]) for c in range(3)]
        stats = [sb(f"n3_stats{b}", [P, 2, 6]) for b in B]
        mean_var = [sb(f"n3_mv{b}", [P, 2, 2]) for b in B]
        std = [sb(f"n3_std{b}", [P, 2]) for b in B]
        consts = sem("n3_consts")
        landed = [sem(f"n3_landed{b}") for b in B]
        stored = [sem(f"n3_stored{b}") for b in B]
        kv_stored = [sem(f"n3_kv_stored{b}") for b in B]
        (halved, taken, var_ready, std_ready, out_ready, next_var, next_std, xn_ready, turned, copied, projected,
         kv_ready) = (sem(f"n3_{n}") for n in (
             "halved", "taken", "var_ready", "std_ready", "out_ready", "next_var", "next_std", "xn_ready", "turned",
             "copied", "projected", "kv_ready"))
        parts_ready, parts_moved = sem("n3_parts_ready"), sem("n3_parts_moved")
        hi_ready, rest_ready, mid_ready, lo_ready, folded, weights_ready = (sem(f"n3_{n}") for n in (
            "hi_ready", "rest_ready", "mid_ready", "lo_ready", "folded", "weights_ready"))
        setup, sum_chain, norm_chain, xn_chain = (
            sem(f"n3_{n}") for n in ("setup", "sum_chain", "norm_chain", "xn_chain"))
        block = ctx.enter_context(nc.Block())
        QKV_BANK = 2

        @block.sync
        def _(sp):
            for n, w in enumerate((wq, wk, wv)):
                sp.dma_start(ws[n][:], w.rearrange("(h p) n -> p h n", p=P)).then_inc(consts, 16)
            sp.dma_start(bias_row[:], bias.partition_broadcast(P)).then_inc(consts, 16)
            sp.dma_start(norm_cols[:, 0, :], gamma).then_inc(consts, 16)
            sp.dma_start(norm_cols[:, 1, :], beta).then_inc(consts, 16)
            sp.dma_start(b_qkv[:], bqkv).then_inc(consts, 16)
            sp.wait_ge(parts_ready, 1)
            for part in range(1, 3):
                sp.dma_start(b_by_part[part:part + 1, :], b_lower[:, part - 1, :]).then_inc(parts_moved, 16)
            for it in passes(sp, NODE_PASSES):
                for b in B:
                    m = it * PAIRS + b
                    sp.wait_ge(taken, m + 1)
                    for a in range(GROUP):
                        sp.dma_start(sums[b][:, a], pair(k.gcn[a], m)).then_inc(landed[b], 16)
                    sp.dma_start(xin[b][:], pair(k.x2, m)).then_inc(landed[b], 16)

        @block.gpsimd
        def _(pool):
            def halve(it, b):
                pool.wait_ge(landed[b], (it + 1) * (16 * (GROUP + 1)))
                pool.tensor_tensor(flat(sums[b][:, 2]), flat(sums[b][:, 2]), flat(sums[b][:, 3]),
                                   ALU.add).then_inc(halved, 1)
                pool.tensor_tensor(xin[b][:], xin[b][:], over_tiles(bias_row[:]), ALU.add).then_inc(halved, 1)

            def store(it, b):
                m = it * PAIRS + b
                pool.wait_ge(out_ready, m + 1)
                pool.dma_start(pair(k.x3, m), out[b][:]).then_inc(stored[b], 16)

            def store_kv(it, b):
                m = it * PAIRS + b
                pool.wait_ge(kv_ready, m + 1 + BANKS)
                pool.dma_start(pair(k.kv, m), kv[b][:]).then_inc(kv_stored[b], 16)

            def lowest_part(it, b):
                m = it * PAIRS + b
                pool.wait_ge(mid_ready, m + 1)
                pool.tensor_tensor(k.q[:, bass.ds(2 * m, 2), 2, :], rest[b % 3][:], k.q[:, bass.ds(2 * m, 2), 1, :],
                                   ALU.subtract).then_inc(lo_ready, 1)

            pool.wait_ge(consts, 16 * 7)
            staged([(5, lowest_part), (0, halve), (4, store_kv), (1, store)])(pool)
            pool.wait_ge(lo_ready, NT // 2 + 2)
            for b in B:
                pool.wait_ge(stored[b], 16 * NODE_PASSES)
                pool.wait_ge(kv_stored[b], 16 * NODE_PASSES)

        @block.scalar
        def _(act):
            act.sem_inc(copied, BANKS)
            act.wait_ge(consts, 16 * 7)

            def root(it, b):
                act.wait_ge(var_ready, it * PAIRS + b + 1)
                act.activation(std[b][:], mean_var[b][:, :, 1], ACT.Sqrt, bias=eps[:, 0:1]).then_inc(std_ready, 1)

            def next_root(it, b):
                act.wait_ge(next_var, it * PAIRS + b + 1)
                act.activation(std[b][:], mean_var[b][:, :, 1], ACT.Sqrt, bias=eps[:, 0:1]).then_inc(next_std, 1)

            def copy_turned(it, b):
                act.wait_ge(turned, it * PAIRS + b + 1)
                act.copy(flat(turned_sb[b % 3][:]), k.psum[:, b % BANKS, :]).then_inc(copied, 1)

            def keep_rows(it, b):
                m = it * PAIRS + b
                bank = QKV_BANK + 3 * (b % BANKS)
                act.wait_ge(projected, m + 1)
                act.copy(k.q[:, bass.ds(2 * m, 2), 0, :], k.psum[:, bank, :].rearrange("p (t d) -> p t d", t=2)
                         ).then_inc(hi_ready, 1)
                act.copy(kv[b][:], k.psum[:, bank + 1:bank + 3, :]).then_inc(kv_ready, 1)

            def middle_part(it, b):
                m = it * PAIRS + b
                act.wait_ge(rest_ready, m + 1 + BANKS)
                act.copy(k.q[:, bass.ds(2 * m, 2), 1, :], rest[b % 3][:]).then_inc(mid_ready, 1)

            staged([(5, middle_part), (2, copy_turned), (1, next_root), (0, root), (3, keep_rows)])(act)

        @block.tensor
        def _(pe):
            pe.wait_ge(consts, 16 * 7)
            for n in range(3):
                for h in range(2):
                    ins = pe.matmul(k.psum[0:1, QKV_BANK + n, 0:D], norm_cols[:, 1, h:h + 1], ws[n][:, h, :],
                                    start=(h == 0), stop=(h == 1))
            ins.then_inc(folded, 1)
            pe.wait_ge(weights_ready, 1)
            pe.wait_ge(parts_moved, 32)

            def turn_xn(it, b):
                m = it * PAIRS + b
                pe.wait_ge(xn_ready, m + 1)
                pe.wait_ge(copied, bank_free(m, b))
                turn_pair(pe, k.psum[:, b % BANKS], xn[b], k.ident[:]).then_inc(turned, 1)

            def project(it, b):
                m = it * PAIRS + b
                pe.wait_ge(copied, m + 1 + BANKS)
                pe.wait_ge(kv_ready, bank_free(m, b))
                pe.wait_ge(rest_ready, bank_free(m, b))
                for t in range(2):
                    for n in range(3):
                        bank, at = (0, t * D) if n == 0 else (1 + t, (n - 1) * D)
                        bank += QKV_BANK + 3 * (b % BANKS)
                        pe.matmul(k.psum[:, bank, at:at + D], ones[:], b_by_part[:, n * D:(n + 1) * D],
                                  start=True, stop=False)
                        for h in range(2):
                            ins = pe.matmul(k.psum[:, bank, at:at + D], turned_sb[b % 3][:, h, t * P:(t + 1) * P],
                                            ws[n][:, h, :], start=False, stop=(h == 1))
                ins.then_inc(projected, 1)

            staged([(3, project), (2, turn_xn)])(pe)

        @block.vector
        def _(dve):
            dve.sem_inc(taken, PAIRS)
            dve.sem_inc(kv_ready, BANKS)
            ch = Chain(dve, setup)
            dve.sem_inc(rest_ready, BANKS)
            dve.sem_inc(lo_ready, 2)
            ch.tick(dve.memset(eps[:], LN_EPS))
            ch.tick(dve.memset(ones[:], 1.0))
            dve.wait_ge(consts, 16 * 7)
            dve.wait_ge(folded, 1)
            ch.tick(dve.tensor_tensor(b_qkv[:].rearrange("p (n d) -> p n d", n=3), k.psum[0:1, QKV_BANK:QKV_BANK + 3, 0:D],
                                      b_qkv[:].rearrange("p (n d) -> p n d", n=3), ALU.add))
            ch.wait()
            ch.then(dve.tensor_copy(b_by_part[0:1, :], b_qkv[:]))
            ch.then(dve.tensor_tensor(b_qkv[:], b_qkv[:], b_by_part[0:1, :], ALU.subtract))
            ch.then(dve.tensor_copy(b_lower[:, 0, :], b_qkv[:]))
            ch.then(dve.tensor_tensor(b_lower[:, 1, :], b_qkv[:], b_lower[:, 0, :], ALU.subtract))
            dve.sem_inc(parts_ready, 1)
            for n in range(3):
                for h in range(2):
                    ch.tick(dve.tensor_scalar(ws[n][:, h, :], ws[n][:, h, :], norm_cols[:, 0, h:h + 1], None, ALU.mult))
            ch.wait()
            dve.sem_inc(weights_ready, 1)

            def add_sums(it, b):
                m = it * PAIRS + b
                ch = Chain(dve, sum_chain, m * 6)
                dve.wait_ge(landed[b], (it + 1) * (16 * (GROUP + 1)))
                ch.then(dve.tensor_tensor(flat(y[b]), flat(y[b]), flat(sums[b][:, 1]), ALU.add))
                dve.wait_ge(halved, 2 * m + 2)
                ch.then(dve.tensor_tensor(flat(y[b]), flat(y[b]), flat(sums[b][:, 2]), ALU.add))
                ch.then(dve.tensor_tensor(y[b], y[b], xin[b][:], ALU.add))
                norm_stats(dve, ch, y[b], stats[b], mean_var[b], var_ready)
                assert ch.n == 6

            def outer_norm(it, b):
                m = it * PAIRS + b
                ch = Chain(dve, norm_chain, m * 6)
                dve.wait_ge(std_ready, m + 1)
                wait_if_any(dve, stored[b], it * 16)
                norm_apply(dve, ch, out[b], y[b], mean_var[b], std[b])
                dve.sem_inc(taken, 1)
                dve.sem_inc(out_ready, 1)
                norm_stats(dve, ch, out[b], stats[b], mean_var[b], next_var)
                assert ch.n == 6

            def next_norm(it, b):
                m = it * PAIRS + b
                ch = Chain(dve, xn_chain, m * 3)
                dve.wait_ge(next_std, m + 1)
                wait_if_any(dve, kv_stored[b], it * 16)
                norm_apply(dve, ch, xn[b], out[b], mean_var[b], std[b])
                dve.sem_inc(xn_ready, 1)
                assert ch.n == 3

            def split_rest(it, b):
                m = it * PAIRS + b
                dve.wait_ge(hi_ready, m + 1)
                dve.wait_ge(lo_ready, m + 1)
                dve.tensor_tensor(rest[b % 3][:],
                                  k.psum[:, QKV_BANK + 3 * (b % BANKS), :].rearrange("p (t d) -> p t d", t=2),
                                  k.q[:, bass.ds(2 * m, 2), 0, :], ALU.subtract).then_inc(rest_ready, 1)

            staged([(4, split_rest), (2, next_norm), (1, outer_norm), (0, add_sums)])(dve)


def att_scores(nc, k, edge_attr, we):
    H = 8
    DH = D // H
    EK = 65
    with ExitStack() as ctx:
        def sb(name, shape, dt=F32):
            return ctx.enter_context(nc.sbuf_tensor(name, shape, dt))

        sem = ctx.enter_context(semaphores(nc))

        we_sb = sb("s3_we", [EK, DH])
        idx = [sb(f"s3_idx{q}", [P, GROUP], I32) for q in range(RING)]
        rows = [sb(f"s3_rows{q}", [P, GROUP, 2 * D]) for q in range(RING)]
        drow = [sb(f"s3_drow{q}", [1, GROUP * P], BF16) for q in range(RING)]
        feat = [sb(f"s3_feat{q}", [EK, GROUP, P]) for q in range(RING)]
        spread = [sb(f"s3_spread{b}", [P, GROUP * P], BF16) for b in range(2)]
        dots = [sb(f"s3_dots{b}", [P, GROUP, D]) for b in range(2)]
        consts = sem("s3_consts")
        gathered = [sem(f"s3_gathered{q}") for q in range(RING)]
        drow_landed = [sem(f"s3_drow_landed{q}") for q in range(RING)]
        feat_landed = [sem(f"s3_feat_landed{q}") for q in range(RING)]
        spilled = [sem(f"s3_spilled{q}") for q in range(RING)]
        ones_ready, idx_ready, passed, spread_ready, looked_up, added, reduced, chain, handed_out = (
            sem(f"s3_{n}") for n in ("ones_ready", "idx_ready", "passed", "spread_ready", "looked_up", "added",
                                     "reduced", "chain", "handed_out"))
        block = ctx.enter_context(nc.Block())
        dloc_rows = k.rows_dloc.rearrange("(o s) l -> o (s l)", o=1)
        spill_rows = k.spill.rearrange("s p d -> p s d")

        @block.scalar
        def _(act):
            for it in passes(act, PASSES):
                for q in range(RING):
                    g = it * RING + q
                    wait_if_any(act, gathered[q], it * (16 * GROUP))
                    act.copy(idx[q][:], k.src_idx[:, bass.ds(g * GROUP, GROUP)]).then_inc(idx_ready, 1)
                    act.wait_ge(spread_ready, g + 1)
                    act.dma_start(drow[q][:], dloc_rows[:, bass.ds(g * (GROUP * P), GROUP * P)]
                                  ).then_inc(drow_landed[q], 16)

        @block.gpsimd
        def _(pool):
            for q in range(RING):
                ins = pool.memset(feat[q][EK - 1:EK, :, :], 1.0)
            ins.then_inc(ones_ready, 1)
            for it in passes(pool, PASSES):
                for q in range(RING):
                    g = it * RING + q
                    pool.wait_ge(idx_ready, g + 1)
                    pool.wait_ge(added, g + 1)
                    wait_if_any(pool, spilled[q], it * 16)
                    pool.sem_inc(passed, 1)
                    for s in range(GROUP):
                        pool.indirect_dma_start(rows[q][:, s, :], None, k.kv,
                                                bass.IndirectOffsetOnAxis(ap=idx[q][:, s:s + 1], axis=0)
                                                ).then_inc(gathered[q], 16)

        @block.sync
        def _(sp):
            sp.dma_start(we_sb[:], we).then_inc(consts, 16)

            def load_group(it, q):
                g = it * RING + q
                sp.wait_ge(looked_up, g + 1)
                regs = load_indices(nc, sp, k.step_i, g * GROUP, GROUP, EA_TILES - 1)
                for s in range(GROUP):
                    sp.dma_start(feat[q][0:EK - 1, s, :], edge_attr[:, bass.ds(regs[s] * P, P)]
                                 ).then_inc(feat_landed[q], 16)

            def spill_group(it, q, _):
                g = it * RING + q
                sp.wait_ge(gathered[q], (it + 1) * (16 * GROUP))
                sp.dma_start(spill_rows[:, bass.ds(g * GROUP, GROUP), :], rows[q][:, :, D:2 * D]
                             ).then_inc(spilled[q], 16)

            one_ahead(sp, nc, None, None, load_group, spill_group, 3)
            for q in range(RING):
                sp.wait_ge(spilled[q], 16 * PASSES)

        @block.tensor
        def _(pe):
            pe.sem_inc(looked_up, RING)
            pe.wait_ge(consts, 16)
            pe.wait_ge(ones_ready, 1)

            def hand_out(it, q):
                g = it * RING + q
                pe.wait_ge(drow_landed[q], (it + 1) * 16)
                pe.wait_ge(spread_ready, g + 1 + RING - 2)
                pe.matmul(k.psum[:, 6 + q % 2, :], k.ones16[:], drow[q][:], start=True, stop=True
                          ).then_inc(handed_out, 1)

            def look_up(it, q, j):
                g = it * RING + q
                b = q % 2
                pe.wait_ge(spread_ready, g + 1 + RING)
                pe.wait_ge(feat_landed[q], (it + 1) * (16 * GROUP))
                pe.wait_ge(reduced, g + 1)
                for s in range(GROUP):
                    pe.matmul(k.psum[:, 4 + b, s * DH:(s + 1) * DH], feat[q][:, s, :], we_sb[:],
                              start=True, stop=True)
                    for part in range(3):
                        ins = pe.matmul(k.psum[:, 2 * b + s // 2, (s % 2) * D:(s % 2 + 1) * D],
                                        spread[b][:, s * P:(s + 1) * P],
                                        k.q[:, bass.ds(j[q * GROUP + s], 1), part, :].rearrange("p o d -> p (o d)"),
                                        start=(part == 0), stop=(part == 2))
                ins.then_inc(looked_up, 1)

            one_ahead(pe, nc, k.step_j, NODE_TILES - 1, hand_out, look_up)

        @block.vector
        def _(dve):
            dve.sem_inc(spread_ready, RING)
            dve.sem_inc(added, RING)
            dve.sem_inc(reduced, 2)

            def spread_group(it, q):
                g = it * RING + q
                dve.wait_ge(handed_out, g + 1)
                dve.wait_ge(looked_up, g + 1 + RING - 2)
                dve.tensor_scalar(spread[q % 2][:], k.psum[:, 6 + q % 2, :], k.lane[:, 0:1], None, ALU.is_equal
                                  ).then_inc(spread_ready, 1)

            def dot_group(it, q, _):
                g = it * RING + q
                b = q % 2
                dve.wait_ge(looked_up, g + 1 + RING)
                dve.wait_ge(gathered[q], (it + 1) * (16 * GROUP))
                for s in range(GROUP):
                    ep = k.psum[:, 4 + b, s * DH:(s + 1) * DH]
                    ins = dve.tensor_tensor(dots[b][:, s, :].rearrange("p (h c) -> p h c", h=H),
                                            rows[q][:, s, 0:D].rearrange("p (h c) -> p h c", h=H),
                                            ep.unsqueeze(1).to_broadcast([P, H, DH]), ALU.add)
                ins.then_inc(added, 1)
                dve.wait_ge(added, g + 1 + RING)
                dve.tensor_tensor(flat(dots[b][:]), flat(dots[b][:]), flat(k.psum[:, 2 * b:2 * b + 2, :]),
                                  ALU.mult).then_inc(chain, 1)
                dve.wait_ge(chain, g + 1)
                dve.tensor_reduce(k.logits[:, bass.ds(g * GROUP, GROUP), 0:H],
                                  dots[b][:].rearrange("p s (h c) -> p s h c", h=H), AX.X, ALU.add
                                  ).then_inc(reduced, 1)

            one_ahead(dve, nc, None, None, spread_group, dot_group)


def att_nodes(nc, k, wo, w1, w2, b1, rows, mixes, out_dram):
    H = 8
    FF = 1024
    NF = FF // P
    with ExitStack() as ctx:
        def sb(name, shape, dt=F32):
            return ctx.enter_context(nc.sbuf_tensor(name, shape, dt))

        sem = ctx.enter_context(semaphores(nc))

        B = range(PAIRS)
        wo_sb, w1_sb, w2_sb = sb("n4_wo", [P, 2, D]), sb("n4_w1", [P, 2, FF]), sb("n4_w2", [P, NF, D])
        b1_col, rows4, mix_col = sb("n4_b1", [P, NF]), sb("n4_rows", [P, 4, D]), sb("n4_mix", [P, 2])
        eps = sb("n4_eps", [P, 1])
        share = sb("n4_share", [P, NT, H])
        xin = [sb(f"n4_x{b}", [P, 2, D]) for b in B]
        y = [sb(f"n4_y{b}", [P, 2, D]) for b in B]
        avg = [sb(f"n4_avg{c}", [P, 2, D]) for c in range(3)]
        x4 = [sb(f"n4_x4{b}", [P, 2, D]) for b in B]
        out = [sb(f"n4_out{b}", [P, 2, D]) for b in B]
        turned_sb = [sb(f"n4_turned{b}", [P, 2, 2 * P]) for b in B]
        hidden = [sb(f"n4_hidden{c}", [P, NF, 2 * P]) for c in range(3)]
        stats = [sb(f"n4_stats{b}", [P, 2, 6]) for b in B]
        mean_var = [sb(f"n4_mv{b}", [P, 2, 2]) for b in B]
        std = [sb(f"n4_std{b}", [P, 2]) for b in B]
        consts = sem("n4_consts")
        landed = [sem(f"n4_landed{b}") for b in B]
        stored = [sem(f"n4_stored{b}") for b in B]
        (avg_ready, avg_turned, avg_copied, projected, projection_read, attn_var, attn_std, xn_ready, xn_turned,
         xn_copied, half_done, half_ready, ff_done, ff_read, taken, var_ready, std_ready, out_ready) = (
             sem(f"n4_{n}") for n in (
                 "avg_ready", "avg_turned", "avg_copied", "projected", "projection_read", "attn_var", "attn_std",
                 "xn_ready", "xn_turned", "xn_copied", "half_done", "half_ready", "ff_done", "ff_read", "taken",
                 "var_ready", "std_ready", "out_ready"))
        share_ready = sem("n4_share_ready")
        setup, attn_chain, xn_chain, ff_chain, out_chain = (
            sem(f"n4_{n}") for n in ("setup", "attn_chain", "xn_chain", "ff_chain", "out_chain"))
        block = ctx.enter_context(nc.Block())
        NCONST = 3 + 1 + 4 + 1
        AVG_BANK, XN_BANK, PROJ_BANK, FF_BANK, HIDDEN_BANK = 0, 1, 2, 3, 4

        @block.sync
        def _(sp):
            sp.dma_start(wo_sb[:], wo.rearrange("(h p) n -> p h n", p=P)).then_inc(consts, 16)
            sp.dma_start(w1_sb[:], w1.rearrange("(h p) n -> p h n", p=P)).then_inc(consts, 16)
            sp.dma_start(w2_sb[:], w2.rearrange("(h p) n -> p h n", p=P)).then_inc(consts, 16)
            sp.dma_start(b1_col[:], b1).then_inc(consts, 16)
            for n in range(4):
                sp.dma_start(rows4[:, n, :], rows[n:n + 1, :].partition_broadcast(P)).then_inc(consts, 16)
            sp.dma_start(mix_col[:], mixes.partition_broadcast(P)).then_inc(consts, 16)
            for it in passes(sp, NODE_PASSES):
                for b in B:
                    m = it * PAIRS + b
                    sp.wait_ge(taken, m + 1)
                    sp.dma_start(xin[b][:], pair(k.x3, m)).then_inc(landed[b], 16)

        @block.gpsimd
        def _(pool):
            pool.wait_ge(share_ready, 1)

            def average(it, b):
                m = it * PAIRS + b
                pool.wait_ge(avg_turned, m + 1)
                for t in range(2):
                    w = share[:, bass.ds(2 * m + t, 1), :].rearrange("p o h -> p (o h)")
                    ins = pool.tensor_tensor(
                        avg[b % 3][:, t].rearrange("p (h c) -> p h c", h=H),
                        k.acc[:, bass.ds(2 * m + t, 1), 0:D].rearrange("p o (h c) -> p (o h) c", h=H),
                        w.unsqueeze(2).to_broadcast([P, H, D // H]), ALU.mult)
                ins.then_inc(avg_ready, 1)

            def store(it, b):
                m = it * PAIRS + b
                pool.wait_ge(out_ready, m + 1)
                pool.dma_start(pair(out_dram, m), out[b][:]).then_inc(stored[b], 16)

            staged([(0, average), (5, store)])(pool)
            for b in B:
                pool.wait_ge(stored[b], 16 * NODE_PASSES)

        @block.scalar
        def _(act):
            act.sem_inc(avg_copied, 1)
            act.sem_inc(xn_copied, 1)
            act.wait_ge(consts, 16 * NCONST)

            def copy_avg(it, b):
                act.wait_ge(avg_turned, it * PAIRS + b + 1 + 2)
                act.copy(flat(turned_sb[b][:]), k.psum[:, AVG_BANK, :]).then_inc(avg_copied, 1)

            def attn_root(it, b):
                act.wait_ge(attn_var, it * PAIRS + b + 1)
                act.activation(std[b][:], mean_var[b][:, :, 1], ACT.Sqrt, bias=eps[:, 0:1]).then_inc(attn_std, 1)

            def copy_xn(it, b):
                act.wait_ge(xn_turned, it * PAIRS + b + 1)
                act.copy(flat(turned_sb[b][:]), k.psum[:, XN_BANK, :]).then_inc(xn_copied, 1)

            def hide(it, b):
                for half in range(2):
                    act.wait_ge(half_done, (it * PAIRS + b) * 2 + half + 1)
                    for f in range(NF // 2):
                        n = half * (NF // 2) + f
                        ins = act.activation(hidden[b % 3][:, n, :],
                                             k.psum[:, HIDDEN_BANK + 2 * half + f // 2, (f % 2) * D:(f % 2 + 1) * D],
                                             ACT.Gelu, bias=b1_col[:, n:n + 1])
                    ins.then_inc(half_ready, 1)

            def root(it, b):
                act.wait_ge(var_ready, it * PAIRS + b + 1)
                act.activation(std[b][:], mean_var[b][:, :, 1], ACT.Sqrt, bias=eps[:, 0:1]).then_inc(std_ready, 1)

            staged([(3, hide), (0, copy_avg), (2, copy_xn), (5, root), (1, attn_root)])(act)

        @block.tensor
        def _(pe):
            pe.sem_inc(avg_turned, 2)
            pe.wait_ge(consts, 16 * NCONST)

            def half_hidden(it, b, half):
                m = it * PAIRS + b
                wait_if_any(pe, half_ready, m * 2)
                for f in range(NF // 2):
                    n = half * (NF // 2) + f
                    for h in range(2):
                        ins = pe.matmul(k.psum[:, HIDDEN_BANK + 2 * half + f // 2, (f % 2) * D:(f % 2 + 1) * D],
                                        w1_sb[:, h, n * P:(n + 1) * P], turned_sb[b][:, h, :],
                                        start=(h == 0), stop=(h == 1))
                ins.then_inc(half_done, 1)

            def mix(it, b):
                pe.wait_ge(xn_copied, it * PAIRS + b + 1 + 1)
                half_hidden(it, b, 0)
                half_hidden(it, b, 1)

            def ff_rows(it, b):
                m = it * PAIRS + b
                pe.wait_ge(half_ready, (m + 1) * 2)
                pe.wait_ge(ff_read, m + 1)
                for t in range(2):
                    for n in range(NF):
                        ins = pe.matmul(k.psum[:, FF_BANK, t * D:(t + 1) * D], hidden[b % 3][:, n, t * P:(t + 1) * P],
                                        w2_sb[:, n, :], start=(n == 0), stop=(n == NF - 1))
                ins.then_inc(ff_done, 1)

            def turn_avg(it, b):
                m = it * PAIRS + b
                pe.wait_ge(avg_ready, m + 1)
                pe.wait_ge(avg_copied, m + 1)
                turn_pair(pe, k.psum[:, AVG_BANK], avg[b % 3], k.ident[:]).then_inc(avg_turned, 1)

            def project(it, b):
                m = it * PAIRS + b
                pe.wait_ge(avg_copied, m + 1 + 1)
                pe.wait_ge(projection_read, m + 1)
                for t in range(2):
                    for h in range(2):
                        ins = pe.matmul(k.psum[:, PROJ_BANK, t * D:(t + 1) * D],
                                        turned_sb[b][:, h, t * P:(t + 1) * P],
                                        wo_sb[:, h, :], start=(h == 0), stop=(h == 1))
                ins.then_inc(projected, 1)

            def turn_xn(it, b):
                m = it * PAIRS + b
                pe.wait_ge(xn_ready, m + 1)
                pe.wait_ge(xn_copied, m + 1)
                turn_pair(pe, k.psum[:, XN_BANK], y[b], k.ident[:]).then_inc(xn_turned, 1)

            staged([(1, project), (0, turn_avg), (3, mix), (2, turn_xn), (4, ff_rows)])(pe)

        @block.vector
        def _(dve):
            dve.sem_inc(taken, PAIRS)
            dve.sem_inc(projection_read, 1)
            dve.sem_inc(ff_read, 1)
            ch = Chain(dve, setup)
            ch.tick(dve.memset(eps[:], LN_EPS))
            ch.then(dve.memset(k.acc[:, NODE_TILES:NT, :], 0.0))
            ch.then(dve.tensor_scalar(share[:], k.acc[:, :, D:D + H], 1e-30, None, ALU.max))
            ch.then(dve.reciprocal(share[:], share[:]))
            dve.sem_inc(share_ready, 1)
            dve.wait_ge(consts, 16 * NCONST)

            def residual(it, b):
                m = it * PAIRS + b
                ch = Chain(dve, attn_chain, m * 5)
                dve.wait_ge(projected, m + 1)
                p = k.psum[:, PROJ_BANK, :].rearrange("p (t d) -> p t d", t=2)
                ch.then(dve.tensor_tensor(x4[b][:], p, over_tiles(rows4[:, 0, :]), ALU.add))
                dve.sem_inc(projection_read, 1)
                dve.wait_ge(landed[b], (it + 1) * 16)
                ch.then(dve.scalar_tensor_tensor(out=x4[b][:], in0=x4[b][:], scalar=mix_col[:, 0:1],
                                                 in1=xin[b][:], op0=ALU.mult, op1=ALU.add))
                norm_stats(dve, ch, x4[b], stats[b], mean_var[b], attn_var)
                assert ch.n == 5

            def inner_norm(it, b):
                m = it * PAIRS + b
                ch = Chain(dve, xn_chain, m * 5)
                dve.wait_ge(attn_std, m + 1)
                norm_apply(dve, ch, y[b], x4[b], mean_var[b], std[b])
                ch.then(dve.tensor_tensor(y[b][:], y[b][:], over_tiles(rows4[:, 1, :]), ALU.mult))
                ch.then(dve.tensor_tensor(y[b][:], y[b][:], over_tiles(rows4[:, 2, :]), ALU.add))
                dve.sem_inc(xn_ready, 1)
                assert ch.n == 5

            def add_ff(it, b):
                m = it * PAIRS + b
                ch = Chain(dve, ff_chain, m * 6)
                dve.wait_ge(ff_done, m + 1)
                p = k.psum[:, FF_BANK, :].rearrange("p (t d) -> p t d", t=2)
                ch.then(dve.tensor_tensor(y[b][:], p, over_tiles(rows4[:, 3, :]), ALU.add))
                dve.sem_inc(ff_read, 1)
                ch.then(dve.scalar_tensor_tensor(out=y[b][:], in0=y[b][:], scalar=mix_col[:, 1:2],
                                                 in1=x4[b][:], op0=ALU.mult, op1=ALU.add))
                ch.then(dve.tensor_tensor(y[b][:], y[b][:], xin[b][:], ALU.add))
                dve.sem_inc(taken, 1)
                norm_stats(dve, ch, y[b], stats[b], mean_var[b], var_ready)
                assert ch.n == 6

            def outer_norm(it, b):
                m = it * PAIRS + b
                ch = Chain(dve, out_chain, m * 3)
                dve.wait_ge(std_ready, m + 1)
                wait_if_any(dve, stored[b], it * 16)
                norm_apply(dve, ch, out[b], y[b], mean_var[b], std[b])
                dve.sem_inc(out_ready, 1)
                assert ch.n == 3

            staged([(1, residual), (2, inner_norm), (5, outer_norm), (4, add_ff)])(dve)


def build(nc, a, out):
    with ExitStack() as ctx:
        def scope(name, shape, dt=F32):
            return nc.sbuf_tensor(name, shape, dt)

        k = allocate(nc, ctx)
        prepare(nc, k, a["src"], a["dst"], a["weight"])
        with scope("att", [P, NT, 8]) as k.att, scope("acc0", [P, NT, D + 12]) as k.acc:
            gat_nodes(nc, k, a["x"], a["l0_w"], a["l0_att_src"], a["l0_att_dst"])
            with scope("aux0", [P, STEPS, 12]) as k.aux:
                with scope("logits0", [P, STEPS, 4]) as k.logits:
                    gat_scores(nc, k)
                    turn_logits(nc, k, 4)
                softmax(nc, k, 4, None, True)
                attend(nc, k, 4, 3)
            gat_finish(nc, k, a["x"], a["l0_bias"], a["l0_slope"])
        with scope("support", [P, NT, D]) as k.support:
            with scope("acc1", [P, NT, D]) as k.acc:
                gin_edges(nc, k, a["edge_attr"])
                gin_nodes(nc, k, a["l1_w1"], a["l1_b1"], a["l1_w2"], a["l1_b2"], a["l1_gamma"], a["l1_beta"], a["l2_w"])
            gcn_edges(nc, k)
        with scope("q", [P, NT, 3, D], BF16) as k.q:
            gcn_nodes(nc, k, a["l2_b"], a["l3_ln1_g"], a["l3_ln1_b"], a["l3_wq"], a["l3_wk"], a["l3_wv"],
                      a["l3_bqkv"])
            with scope("logits3", [P, STEPS, 8]) as k.logits:
                att_scores(nc, k, a["edge_feat"], a["l3_we"])
                turn_logits(nc, k, 8)
        with scope("aux3", [P, STEPS, 8]) as k.aux:
            softmax(nc, k, 8, float(D // 8) ** -0.5, False)
            with scope("acc3", [P, NT, D + 8]) as k.acc:
                attend(nc, k, 8, 1)
                att_nodes(nc, k, a["l3_wo"], a["l3_w1"], a["l3_w2"], a["l3_b1"], a["l3_rows"], a["l3_mixes"],
                          out)


def padded(array, rows, value):
    out = np.full((rows, *array.shape[1:]), value, array.dtype)
    out[:array.shape[0]] = array
    return out


def layout(i):
    def index(name, value):
        return padded(i[name], IDX_ROWS * P, value).reshape(IDX_ROWS, P)

    def row(name):
        return i[name].reshape(1, -1)

    def column(name):
        return np.ascontiguousarray(i[name].reshape(-1, P).T)

    return {
        "x": padded(i["x"], NP, 0), "src": index("src", 0), "dst": index("dst", DST_PAD),
        "weight": index("edge_weight", 0), "edge_attr": padded(i["edge_attr_256"], EA_TILES * P, 0),
        "edge_feat": np.ascontiguousarray(padded(i["edge_attr_64"], EA_TILES * P, 0).T),
        "l0_w": i["L0_gnn_W"], "l0_att_src": row("L0_gnn_att_src"), "l0_att_dst": row("L0_gnn_att_dst"),
        "l0_bias": row("L0_gnn_bias"), "l0_slope": row("L0_gnn_prelu_a"),
        "l1_w1": i["L1_gnn_W1"], "l1_b1": column("L1_gnn_b1"), "l1_w2": i["L1_gnn_W2"], "l1_b2": row("L1_gnn_b2"),
        "l1_gamma": row("L1_gnn_gamma"), "l1_beta": row("L1_gnn_beta"),
        "l2_w": i["L2_gnn_W"], "l2_b": row("L2_gnn_b"),
        "l3_ln1_g": column("L3_gnn_ln1_g"), "l3_ln1_b": column("L3_gnn_ln1_b"),
        "l3_wq": i["L3_gnn_Wq"], "l3_wk": i["L3_gnn_Wk"], "l3_wv": i["L3_gnn_Wv"], 
        "l3_bqkv": np.concatenate([row("L3_gnn_bq"), row("L3_gnn_bk"), row("L3_gnn_bv")], 1),
        "l3_we": np.concatenate([i["L3_gnn_We"], row("L3_gnn_be")], 0),
        "l3_wo": i["L3_gnn_Wo"], "l3_w1": i["L3_gnn_W1"], "l3_w2": i["L3_gnn_W2"], "l3_b1": column("L3_gnn_b1"),
        "l3_rows": np.concatenate([row(f"L3_gnn_{n}") for n in ("bo", "ln2_g", "ln2_b", "b2")], 0),
        "l3_mixes": np.concatenate([row("L3_gnn_alpha"), row("L3_gnn_beta")], 1),
    }


def kernel(**inputs):
    import concourse.bacc as bacc
    from concourse.bass_utils import run_bass_kernel_spmd

    arrays = layout({name: np.asarray(a) for name, a in inputs.items()})
    nc = bacc.Bacc("TRN2", target_bir_lowering=False, num_devices=1)
    a = {name: nc.dram_tensor(f"in_{name}", v.shape, mybir.dt.from_np(v.dtype),
                                kind="ExternalInput").ap() for name, v in arrays.items()}
    out = nc.dram_tensor("out_x", (NP, D), F32, kind="ExternalOutput").ap()
    build(nc, a, out)
    r = run_bass_kernel_spmd(nc, [{f"in_{name}": v for name, v in arrays.items()}], core_ids=[0])
    return r.results[0]["out_x"][:N]
```
